# Optimizing a Trainium2 kernel written in Bass

```python
import numpy as np
import jax
import jax.numpy as jnp

def _softmax(x, axis=-1):
    return jax.nn.softmax(x, axis=axis)

def _gelu(x):
    return jax.nn.gelu(x, approximate=True)

def _silu(x):
    return jax.nn.silu(x)

def _sigmoid(x):
    return jax.nn.sigmoid(x)

def _layernorm(x, axis=-1, eps=1e-05):
    m = jnp.mean(x, axis=axis, keepdims=True)
    v = jnp.var(x, axis=axis, keepdims=True)
    return (x - m) / jnp.sqrt(v + eps)

def _scatter_add(tgt, idx, src, axis=0):
    return tgt.at[idx].add(src)

def _segment_sum(src, seg, n):
    return jax.ops.segment_sum(src, seg, n)
kernel_name = 'mk_xattn_seq_d4_seqx_r8_7bcfbe'

def setup_inputs(seed: int=0):
    np.random.seed(seed)
    _w = jnp.asarray

    def _rec_inputs():
        import jax
        import jax.numpy as jnp
        _rk = jax.random.key(seed)
        x = -0.0002928 + 1 * jax.random.normal(jax.random.fold_in(_rk, 1), (64, 128, 128), jnp.float32)
        _lenS = 128 - jax.random.randint(jax.random.fold_in(_rk, 7), (64,), 0, max(1, 128 // 4) + 1, jnp.int32)
        _lenS2 = 77 - jax.random.randint(jax.random.fold_in(_rk, 8), (64,), 0, max(1, 77 // 4) + 1, jnp.int32)
        _ctx_1024P = jax.random.normal(jax.random.fold_in(_rk, 11), (64, 16, 128), jnp.float32)
        _ctx_1024c = jax.random.dirichlet(jax.random.fold_in(_rk, 511), 0.3 * jnp.ones((16,), jnp.float32), (64, 77))
        _ctx_1024t = jnp.einsum('bsk,bkd->bsd', _ctx_1024c, _ctx_1024P)
        _ctx_1024t = _ctx_1024t * jax.lax.rsqrt(jnp.mean(jnp.square(_ctx_1024t)) + 1e-12) * 0.953939
        ctx_1024 = -1.39393e-06 + 0.999914 * (_ctx_1024t + 0.3 * jax.random.normal(jax.random.fold_in(_rk, 611), (64, 77, 128), jnp.float32))
        fside_Bx16xSxS2_0 = jax.random.uniform(jax.random.fold_in(_rk, 13), (64, 16, 128, 77), jnp.float32, 0.0, 1)
        _validS = jnp.arange(128)[None, :] < _lenS[:, None]
        _validS2 = jnp.arange(77)[None, :] < _lenS2[:, None]
        _causal = jnp.tril(jnp.ones((128, 128), dtype=bool))
        mask_Bx16xSxS2_bk0 = jnp.logical_not(jnp.broadcast_to(_validS2[:, None, None, :], (64, 16, 128, 77)))
        mask_Bx1x1xS2_if1 = jnp.where(jnp.ones((64, 1, 1, 77), dtype=bool), 1, 0).astype(jnp.int32)
        return (x, ctx_1024, fside_Bx16xSxS2_0, mask_Bx16xSxS2_bk0, mask_Bx1x1xS2_if1)
    x, ctx_1024, fside_Bx16xSxS2_0, mask_Bx16xSxS2_bk0, mask_Bx1x1xS2_if1 = _rec_inputs()

    def _L0_xattn_setup():
        import jax, jax.numpy as jnp
        import numpy as np
        B, S, D_MODEL, H, D_FF = (2, 256, 128, 16, 512)
        D_HEAD = D_MODEL // H
        LN_EPS = 1e-05

        def _xavier(key, shape):
            fan_out, fan_in = shape
            std = (2.0 / (fan_in + fan_out)) ** 0.5
            return jax.random.normal(key, shape, dtype=jnp.float32) * std

        def _layer_norm(x, g, b):
            mu = jnp.mean(x, axis=-1, keepdims=True)
            var = jnp.mean((x - mu) ** 2, axis=-1, keepdims=True)
            return (x - mu) * jax.lax.rsqrt(var + LN_EPS) * g + b
        key = jax.random.key(seed)
        ks = jax.random.split(key, 8)
        return {'q': jax.random.normal(ks[0], (B, S, D_MODEL), dtype=jnp.float32), 'k': jax.random.normal(ks[1], (B, S, D_MODEL), dtype=jnp.float32), 'Wq': _xavier(ks[2], (D_MODEL, D_MODEL)), 'bq': jnp.zeros((D_MODEL,), jnp.float32), 'Wk': _xavier(ks[3], (D_MODEL, D_MODEL)), 'bk': jnp.zeros((D_MODEL,), jnp.float32), 'Wv': _xavier(ks[4], (D_MODEL, D_MODEL)), 'bv': jnp.zeros((D_MODEL,), jnp.float32), 'W1': _xavier(ks[5], (D_FF, D_MODEL)), 'b1': jnp.zeros((D_FF,), jnp.float32), 'W2': _xavier(ks[6], (D_MODEL, D_FF)), 'b2': jnp.zeros((D_MODEL,), jnp.float32), 'ln_g': jnp.ones((D_MODEL,), jnp.float32), 'ln_b': jnp.zeros((D_MODEL,), jnp.float32), 'use_causal_mask': 1}
    _L0_xattn_all = _L0_xattn_setup()
    _L0_xattn_in = {k: v for k, v in _L0_xattn_all.items() if k in ('Wq', 'bq', 'Wk', 'bk', 'Wv', 'bv', 'W1', 'b1', 'W2', 'b2', 'ln_g', 'ln_b')}
    del _L0_xattn_all

    def _L1_xattn_setup():
        import jax, jax.numpy as jnp
        import numpy as np
        D_MODEL = 128
        N_HEADS = 16
        D_HEAD = D_MODEL // N_HEADS
        LN_EPS = 1e-05

        def _xavier(key, shape):
            lim = float(np.sqrt(6.0 / (shape[0] + shape[1])))
            return jax.random.uniform(key, shape, jnp.float32, -lim, lim)
        key = jax.random.key(seed)
        ks = jax.random.split(key, 10)
        B, Nq, Nk = (2, 256, 256)
        queries = jax.random.normal(ks[0], (B, Nq, D_MODEL), jnp.float32)
        keys = jax.random.normal(ks[1], (B, Nk, D_MODEL), jnp.float32)
        values = jax.random.normal(ks[2], (B, Nk, D_MODEL), jnp.float32)
        attention_mask = jax.random.bernoulli(ks[3], 0.1, (B, N_HEADS, Nq, Nk))
        attention_weights = jax.random.uniform(ks[4], (B, N_HEADS, Nq, Nk), jnp.float32)
        Wq = _xavier(ks[5], (D_MODEL, D_MODEL))
        Wk = _xavier(ks[6], (D_MODEL, D_MODEL))
        Wv = _xavier(ks[7], (D_MODEL, D_MODEL))
        Wo = _xavier(ks[8], (D_MODEL, D_MODEL))
        b = jnp.zeros((D_MODEL,), jnp.float32)
        gamma = jnp.ones((D_MODEL,), jnp.float32)
        beta = jnp.zeros((D_MODEL,), jnp.float32)
        return {'queries': queries, 'keys': keys, 'values': values, 'attention_mask': attention_mask, 'attention_weights': attention_weights, 'Wq': Wq, 'bq': b, 'Wk': Wk, 'bk': b, 'Wv': Wv, 'bv': b, 'Wo': Wo, 'bo': b, 'gamma': gamma, 'beta': beta}
    _L1_xattn_all = _L1_xattn_setup()
    _L1_xattn_in = {k: v for k, v in _L1_xattn_all.items() if k in ('Wq', 'bq', 'Wk', 'bk', 'Wv', 'bv', 'Wo', 'bo', 'gamma', 'beta')}
    del _L1_xattn_all

    def _L2_xattn_setup():
        import jax, jax.numpy as jnp
        import numpy as np
        EMBED = 128
        HEADS = 16
        HEAD_DIM = EMBED // HEADS
        FF = 4 * EMBED
        EPS = 1e-05

        def layernorm(x, g, b):
            mu = jnp.mean(x, axis=-1, keepdims=True)
            var = jnp.mean((x - mu) ** 2, axis=-1, keepdims=True)
            return (x - mu) * jax.lax.rsqrt(var + EPS) * g + b
        key = jax.random.key(seed)
        ks = jax.random.split(key, 16)
        B, S = (2, 256)
        f32 = jnp.float32
        inp = {'value': jax.random.normal(ks[0], (B, S, EMBED), f32), 'key': jax.random.normal(ks[1], (B, S, EMBED), f32), 'query': jax.random.normal(ks[2], (B, S, EMBED), f32), 'mask': jnp.ones((B, 1, 1, S), jnp.int32), 'wv': jax.random.normal(ks[3], (HEAD_DIM, HEAD_DIM), f32) * 0.02, 'wk': jax.random.normal(ks[4], (HEAD_DIM, HEAD_DIM), f32) * 0.02, 'wq': jax.random.normal(ks[5], (HEAD_DIM, HEAD_DIM), f32) * 0.02, 'w_out': jax.random.normal(ks[6], (EMBED, EMBED), f32) * 0.02, 'b_out': jnp.zeros((EMBED,), f32), 'g1': jnp.ones((EMBED,), f32), 'beta1': jnp.zeros((EMBED,), f32), 'w_ff1': jax.random.normal(ks[7], (EMBED, FF), f32) * 0.02, 'b_ff1': jnp.zeros((FF,), f32), 'w_ff2': jax.random.normal(ks[8], (FF, EMBED), f32) * 0.02, 'b_ff2': jnp.zeros((EMBED,), f32), 'g2': jnp.ones((EMBED,), f32), 'beta2': jnp.zeros((EMBED,), f32)}
        return inp
    _L2_xattn_all = _L2_xattn_setup()
    _L2_xattn_in = {k: v for k, v in _L2_xattn_all.items() if k in ('wv', 'wk', 'wq', 'w_out', 'b_out', 'g1', 'beta1', 'w_ff1', 'b_ff1', 'w_ff2', 'b_ff2', 'g2', 'beta2')}
    del _L2_xattn_all

    def _L3_xattn_setup():
        import jax, jax.numpy as jnp
        import numpy as np
        B, N, DIM = (2, 256, 128)
        HEADS, DH = (16, 64)
        SEG = 64
        NPM = 16
        NM = 16
        DFF = int(DIM * 4 * 2 / 3)
        EPS = 1.1920929e-07

        def rms_norm(x, w):
            return x * jax.lax.rsqrt(jnp.mean(x * x, axis=-1, keepdims=True) + EPS) * w
        key = jax.random.key(seed)
        ks = jax.random.split(key, 10)
        p = lambda i, shape: jax.random.normal(ks[i], shape, jnp.float32) * 0.02
        return {'x': jax.random.normal(ks[0], (B, N, DIM), jnp.float32), 'mem_out': jax.random.normal(ks[1], (B, N, DIM), jnp.float32), 'attn_norm_w': jnp.ones((DIM,), jnp.float32), 'to_qkv_w': p(2, (DIM, 3 * HEADS * DH)), 'to_out_w': p(3, (HEADS * DH, DIM)), 'persist_mem': jax.random.normal(ks[4], (HEADS, NPM, DH), jnp.float32), 'mem_pool_norm_w': jnp.ones((DIM,), jnp.float32), 'to_mem_tokens_w': p(5, (DIM, DIM)), 'ff_norm_w': jnp.ones((DIM,), jnp.float32), 'ff_w1': p(6, (DIM, 2 * DFF)), 'ff_b1': jnp.zeros((2 * DFF,), jnp.float32), 'ff_w2': p(7, (DFF, DIM)), 'ff_b2': jnp.zeros((DIM,), jnp.float32)}
    _L3_xattn_all = _L3_xattn_setup()
    _L3_xattn_in = {k: v for k, v in _L3_xattn_all.items() if k in ('attn_norm_w', 'to_qkv_w', 'to_out_w', 'persist_mem', 'mem_pool_norm_w', 'to_mem_tokens_w', 'ff_norm_w', 'ff_w1', 'ff_b1', 'ff_w2', 'ff_b2')}
    del _L3_xattn_all
    return {'x': x, 'ctx_1024': ctx_1024, 'fside_Bx16xSxS2_0': fside_Bx16xSxS2_0, 'mask_Bx16xSxS2_bk0': mask_Bx16xSxS2_bk0, 'mask_Bx1x1xS2_if1': mask_Bx1x1xS2_if1, 'L0_xattn_Wq': _L0_xattn_in['Wq'], 'L0_xattn_bq': _L0_xattn_in['bq'], 'L0_xattn_Wk': _L0_xattn_in['Wk'], 'L0_xattn_bk': _L0_xattn_in['bk'], 'L0_xattn_Wv': _L0_xattn_in['Wv'], 'L0_xattn_bv': _L0_xattn_in['bv'], 'L0_xattn_W1': _L0_xattn_in['W1'], 'L0_xattn_b1': _L0_xattn_in['b1'], 'L0_xattn_W2': _L0_xattn_in['W2'], 'L0_xattn_b2': _L0_xattn_in['b2'], 'L0_xattn_ln_g': _L0_xattn_in['ln_g'], 'L0_xattn_ln_b': _L0_xattn_in['ln_b'], 'L1_xattn_Wq': _L1_xattn_in['Wq'], 'L1_xattn_bq': _L1_xattn_in['bq'], 'L1_xattn_Wk': _L1_xattn_in['Wk'], 'L1_xattn_bk': _L1_xattn_in['bk'], 'L1_xattn_Wv': _L1_xattn_in['Wv'], 'L1_xattn_bv': _L1_xattn_in['bv'], 'L1_xattn_Wo': _L1_xattn_in['Wo'], 'L1_xattn_bo': _L1_xattn_in['bo'], 'L1_xattn_gamma': _L1_xattn_in['gamma'], 'L1_xattn_beta': _L1_xattn_in['beta'], 'L2_xattn_wv': _L2_xattn_in['wv'], 'L2_xattn_wk': _L2_xattn_in['wk'], 'L2_xattn_wq': _L2_xattn_in['wq'], 'L2_xattn_w_out': _L2_xattn_in['w_out'], 'L2_xattn_b_out': _L2_xattn_in['b_out'], 'L2_xattn_g1': _L2_xattn_in['g1'], 'L2_xattn_beta1': _L2_xattn_in['beta1'], 'L2_xattn_w_ff1': _L2_xattn_in['w_ff1'], 'L2_xattn_b_ff1': _L2_xattn_in['b_ff1'], 'L2_xattn_w_ff2': _L2_xattn_in['w_ff2'], 'L2_xattn_b_ff2': _L2_xattn_in['b_ff2'], 'L2_xattn_g2': _L2_xattn_in['g2'], 'L2_xattn_beta2': _L2_xattn_in['beta2'], 'L3_xattn_attn_norm_w': _L3_xattn_in['attn_norm_w'], 'L3_xattn_to_qkv_w': _L3_xattn_in['to_qkv_w'], 'L3_xattn_to_out_w': _L3_xattn_in['to_out_w'], 'L3_xattn_persist_mem': _L3_xattn_in['persist_mem'], 'L3_xattn_mem_pool_norm_w': _L3_xattn_in['mem_pool_norm_w'], 'L3_xattn_to_mem_tokens_w': _L3_xattn_in['to_mem_tokens_w'], 'L3_xattn_ff_norm_w': _L3_xattn_in['ff_norm_w'], 'L3_xattn_ff_w1': _L3_xattn_in['ff_w1'], 'L3_xattn_ff_b1': _L3_xattn_in['ff_b1'], 'L3_xattn_ff_w2': _L3_xattn_in['ff_w2'], 'L3_xattn_ff_b2': _L3_xattn_in['ff_b2']}

def reference(x, ctx_1024, fside_Bx16xSxS2_0, mask_Bx16xSxS2_bk0, mask_Bx1x1xS2_if1, L0_xattn_Wq, L0_xattn_bq, L0_xattn_Wk, L0_xattn_bk, L0_xattn_Wv, L0_xattn_bv, L0_xattn_W1, L0_xattn_b1, L0_xattn_W2, L0_xattn_b2, L0_xattn_ln_g, L0_xattn_ln_b, L1_xattn_Wq, L1_xattn_bq, L1_xattn_Wk, L1_xattn_bk, L1_xattn_Wv, L1_xattn_bv, L1_xattn_Wo, L1_xattn_bo, L1_xattn_gamma, L1_xattn_beta, L2_xattn_wv, L2_xattn_wk, L2_xattn_wq, L2_xattn_w_out, L2_xattn_b_out, L2_xattn_g1, L2_xattn_beta1, L2_xattn_w_ff1, L2_xattn_b_ff1, L2_xattn_w_ff2, L2_xattn_b_ff2, L2_xattn_g2, L2_xattn_beta2, L3_xattn_attn_norm_w, L3_xattn_to_qkv_w, L3_xattn_to_out_w, L3_xattn_persist_mem, L3_xattn_mem_pool_norm_w, L3_xattn_to_mem_tokens_w, L3_xattn_ff_norm_w, L3_xattn_ff_w1, L3_xattn_ff_b1, L3_xattn_ff_w2, L3_xattn_ff_b2):
    import jax
    import jax.numpy as jnp

    def _L0_xattn_ref(q, k, Wq, bq, Wk, bk, Wv, bv, W1, b1, W2, b2, ln_g, ln_b, use_causal_mask):
        import jax, jax.numpy as jnp
        import numpy as np
        B, S, D_MODEL, H, D_FF = (2, 256, 128, 16, 512)
        D_HEAD = D_MODEL // H
        LN_EPS = 1e-05

        def _xavier(key, shape):
            fan_out, fan_in = shape
            std = (2.0 / (fan_in + fan_out)) ** 0.5
            return jax.random.normal(key, shape, dtype=jnp.float32) * std

        def _layer_norm(x, g, b):
            mu = jnp.mean(x, axis=-1, keepdims=True)
            var = jnp.mean((x - mu) ** 2, axis=-1, keepdims=True)
            return (x - mu) * jax.lax.rsqrt(var + LN_EPS) * g + b
        Bq, Sq, _ = q.shape
        Sk = k.shape[1]
        Q = q @ Wq.T + bq
        K = k @ Wk.T + bk
        V = k @ Wv.T + bv
        Q_ = Q.reshape(Bq, Sq, H, D_HEAD).transpose(0, 2, 1, 3)
        K_ = K.reshape(Bq, Sk, H, D_HEAD).transpose(0, 2, 1, 3)
        V_ = V.reshape(Bq, Sk, H, D_HEAD).transpose(0, 2, 1, 3)
        scores = jnp.einsum('bhqd,bhkd->bhqk', Q_, K_) / D_HEAD ** 0.5
        if use_causal_mask:
            causal = jnp.tril(jnp.ones((Sq, Sk), dtype=bool))
            scores = jnp.where(causal, scores, jnp.float32(-1000000000.0))
        sim = jax.nn.softmax(scores, axis=-1)
        att = jnp.einsum('bhqk,bhkd->bhqd', sim, V_)
        att_h = att.transpose(0, 2, 1, 3).reshape(Bq, Sq, D_MODEL)
        att_h = att_h + q
        att_h = _layer_norm(att_h, ln_g, ln_b)
        ff = jax.nn.gelu(att_h @ W1.T + b1, approximate=False) @ W2.T + b2
        return ff + att_h

    def _L1_xattn_ref(queries, keys, values, attention_mask, attention_weights, Wq, bq, Wk, bk, Wv, bv, Wo, bo, gamma, beta):
        import jax, jax.numpy as jnp
        import numpy as np
        D_MODEL = 128
        N_HEADS = 16
        D_HEAD = D_MODEL // N_HEADS
        LN_EPS = 1e-05

        def _xavier(key, shape):
            lim = float(np.sqrt(6.0 / (shape[0] + shape[1])))
            return jax.random.uniform(key, shape, jnp.float32, -lim, lim)
        B, Nq, D = queries.shape
        h, d = (N_HEADS, D_HEAD)
        q = (queries @ Wq.T + bq).reshape(B, Nq, h, d).transpose(0, 2, 1, 3)
        k = (keys @ Wk.T + bk).reshape(B, -1, h, d).transpose(0, 2, 1, 3)
        v = (values @ Wv.T + bv).reshape(B, -1, h, d).transpose(0, 2, 1, 3)
        scores = jnp.einsum('bhqd,bhkd->bhqk', q, k) / jnp.sqrt(jnp.float32(d))
        scores = scores * attention_weights
        scores = jnp.where(attention_mask, -jnp.inf, scores)
        p_attn = jax.nn.softmax(scores, axis=-1)
        out = jnp.einsum('bhqk,bhkd->bhqd', p_attn, v)
        out = out.transpose(0, 2, 1, 3).reshape(B, Nq, D)
        out = out @ Wo.T + bo
        x = queries + out
        mu = jnp.mean(x, axis=-1, keepdims=True)
        var = jnp.mean(jnp.square(x - mu), axis=-1, keepdims=True)
        return (x - mu) * jax.lax.rsqrt(var + LN_EPS) * gamma + beta

    def _L2_xattn_ref(value, key, query, mask, wv, wk, wq, w_out, b_out, g1, beta1, w_ff1, b_ff1, w_ff2, b_ff2, g2, beta2):
        import jax, jax.numpy as jnp
        import numpy as np
        EMBED = 128
        HEADS = 16
        HEAD_DIM = EMBED // HEADS
        FF = 4 * EMBED
        EPS = 1e-05

        def layernorm(x, g, b):
            mu = jnp.mean(x, axis=-1, keepdims=True)
            var = jnp.mean((x - mu) ** 2, axis=-1, keepdims=True)
            return (x - mu) * jax.lax.rsqrt(var + EPS) * g + b
        B, S, E = query.shape
        v = value.reshape(B, -1, HEADS, HEAD_DIM) @ wv
        k = key.reshape(B, -1, HEADS, HEAD_DIM) @ wk
        q = query.reshape(B, -1, HEADS, HEAD_DIM) @ wq
        scores = jnp.einsum('bqhd,bkhd->bhqk', q, k)
        scores = jnp.where(mask == 0, jnp.float32(-1e+20), scores)
        attn = jax.nn.softmax(scores / jnp.sqrt(jnp.float32(EMBED)), axis=-1)
        out = jnp.einsum('bhqk,bkhd->bqhd', attn, v).reshape(B, S, E)
        attention = out @ w_out + b_out
        x = layernorm(attention + query, g1, beta1)
        ff = jax.nn.relu(x @ w_ff1 + b_ff1) @ w_ff2 + b_ff2
        return layernorm(ff + x, g2, beta2)

    def _L3_xattn_ref(x, mem_out, attn_norm_w, to_qkv_w, to_out_w, persist_mem, mem_pool_norm_w, to_mem_tokens_w, ff_norm_w, ff_w1, ff_b1, ff_w2, ff_b2):
        import jax, jax.numpy as jnp
        import numpy as np
        B, N, DIM = (2, 256, 128)
        HEADS, DH = (16, 64)
        SEG = 64
        NPM = 16
        NM = 16
        DFF = int(DIM * 4 * 2 / 3)
        EPS = 1.1920929e-07

        def rms_norm(x, w):
            return x * jax.lax.rsqrt(jnp.mean(x * x, axis=-1, keepdims=True) + EPS) * w
        b, n, _ = x.shape
        split_heads = lambda t: t.reshape(b, -1, HEADS, DH).transpose(0, 2, 1, 3)
        pooled = rms_norm(mem_out.mean(axis=1), mem_pool_norm_w)
        mem_tok = jnp.broadcast_to((pooled @ to_mem_tokens_w)[:, None, :], (b, NM, DIM))
        _, k_c, v_c = jnp.split(mem_tok @ to_qkv_w, 3, axis=-1)
        k_extra, v_extra = (split_heads(k_c), split_heads(v_c))
        xn = rms_norm(x, attn_norm_w)
        q, k, v = jnp.split(xn @ to_qkv_w, 3, axis=-1)
        q, k, v = (split_heads(q), split_heads(k), split_heads(v))
        pos = jnp.arange(n)
        inv = 1.0 / 10000.0 ** (jnp.arange(0, DH, 2, dtype=jnp.float32) / DH)
        ang = jnp.repeat(pos[:, None].astype(jnp.float32) * inv[None, :], 2, axis=-1)
        cos, sin = (jnp.cos(ang), jnp.sin(ang))

        def rope(t):
            z = t.reshape(t.shape[:-1] + (-1, 2))
            rh = jnp.stack([-z[..., 1], z[..., 0]], axis=-1).reshape(t.shape)
            return t * cos + rh * sin
        q, k = (rope(q), rope(k))
        pm = jnp.broadcast_to(persist_mem[None], (b, HEADS, NPM, DH))
        kf = jnp.concatenate([k_extra, pm, k], axis=2)
        vf = jnp.concatenate([v_extra, pm, v], axis=2)
        P = NPM + NM
        ki = jnp.arange(kf.shape[2])[None, :]
        qi = pos[:, None]
        causal = qi >= ki - P
        seg = qi // SEG == (ki - P) // SEG
        mask = causal & seg | (ki < P)
        scores = jnp.einsum('bhid,bhjd->bhij', q, kf) * DH ** (-0.5)
        scores = jnp.where(mask[None, None], scores, -1e+30)
        probs = jax.nn.softmax(scores, axis=-1)
        o = jnp.einsum('bhij,bhjd->bhid', probs, vf)
        attn_out = o.transpose(0, 2, 1, 3).reshape(b, n, HEADS * DH) @ to_out_w
        x = x + attn_out
        h = rms_norm(x, ff_norm_w) @ ff_w1 + ff_b1
        a, g = jnp.split(h, 2, axis=-1)
        x = x + jax.nn.silu(g) * a @ ff_w2 + ff_b2
        return x
    x = _L0_xattn_ref(x, ctx_1024, L0_xattn_Wq, L0_xattn_bq, L0_xattn_Wk, L0_xattn_bk, L0_xattn_Wv, L0_xattn_bv, L0_xattn_W1, L0_xattn_b1, L0_xattn_W2, L0_xattn_b2, L0_xattn_ln_g, L0_xattn_ln_b, 1)
    x = _L1_xattn_ref(x, ctx_1024, ctx_1024, mask_Bx16xSxS2_bk0, fside_Bx16xSxS2_0, L1_xattn_Wq, L1_xattn_bq, L1_xattn_Wk, L1_xattn_bk, L1_xattn_Wv, L1_xattn_bv, L1_xattn_Wo, L1_xattn_bo, L1_xattn_gamma, L1_xattn_beta)
    x = _L2_xattn_ref(ctx_1024, ctx_1024, x, mask_Bx1x1xS2_if1, L2_xattn_wv, L2_xattn_wk, L2_xattn_wq, L2_xattn_w_out, L2_xattn_b_out, L2_xattn_g1, L2_xattn_beta1, L2_xattn_w_ff1, L2_xattn_b_ff1, L2_xattn_w_ff2, L2_xattn_b_ff2, L2_xattn_g2, L2_xattn_beta2)
    x = _L3_xattn_ref(x, ctx_1024, L3_xattn_attn_norm_w, L3_xattn_to_qkv_w, L3_xattn_to_out_w, L3_xattn_persist_mem, L3_xattn_mem_pool_norm_w, L3_xattn_to_mem_tokens_w, L3_xattn_ff_norm_w, L3_xattn_ff_w1, L3_xattn_ff_b1, L3_xattn_ff_w2, L3_xattn_ff_b2)
    return x

_drawn_inputs = setup_inputs


def setup_inputs(seed=0):
    import zlib

    import numpy as np

    out = dict(_drawn_inputs(seed))
    spreads = {'L0_xattn_bq': (0.0, 0.358),
     'L0_xattn_bk': (0.0, 2.0),
     'L0_xattn_bv': (0.0, 0.1),
     'L0_xattn_b1': (0.0, 0.1),
     'L0_xattn_b2': (0.0, 0.1),
     'L0_xattn_ln_g': (1.0, 0.2),
     'L0_xattn_ln_b': (0.0, 0.1),
     'L1_xattn_bq': (0.0, 0.727),
     'L1_xattn_bk': (0.0, 0.8),
     'L1_xattn_bv': (0.0, 0.1),
     'L1_xattn_bo': (0.0, 0.1),
     'L1_xattn_gamma': (1.0, 0.2),
     'L1_xattn_beta': (0.0, 0.1),
     'L2_xattn_b_out': (0.0, 0.1),
     'L2_xattn_g1': (1.0, 0.2),
     'L2_xattn_beta1': (0.0, 0.1),
     'L2_xattn_b_ff1': (0.0, 0.281),
     'L2_xattn_b_ff2': (0.0, 0.1),
     'L2_xattn_g2': (1.0, 0.2),
     'L2_xattn_beta2': (0.0, 0.1),
     'L3_xattn_attn_norm_w': (1.0, 0.6),
     'L3_xattn_mem_pool_norm_w': (1.0, 0.6),
     'L3_xattn_ff_norm_w': (1.0, 0.6),
     'L3_xattn_ff_b1': (0.0, 0.8),
     'L3_xattn_ff_b2': (0.0, 0.297)}
    factors = {'L2_xattn_wv': 7.443,
     'L2_xattn_wk': 34.493,
     'L2_xattn_wq': 33.291,
     'L2_xattn_w_out': 7.955,
     'L3_xattn_to_mem_tokens_w': 6.194,
     'L3_xattn_ff_w1': 5.089,
     'L3_xattn_ff_w2': 5.074}
    for name, (base, spread) in spreads.items():
        noise = np.random.default_rng([zlib.crc32(name.encode()), seed]).standard_normal(out[name].shape)
        drawn = base * np.exp(spread * noise) if base else spread * noise
        out[name] = jnp.asarray(drawn.astype(out[name].dtype))
    for name, factor in factors.items():
        out[name] = (out[name] * factor).astype(out[name].dtype)
    return out
```

```python
from contextlib import ExitStack
from dataclasses import dataclass

import numpy as np

import concourse.bass as bass
from concourse import mybir

F32 = mybir.dt.float32
BF16 = mybir.dt.bfloat16
I32 = mybir.dt.int32
U8 = mybir.dt.uint8
ACT = mybir.ActivationFunctionType
ALU = mybir.AluOpType
AX = mybir.AxisListType

T = 128
D = 128
C = 77
H = 16
DH = D // H
QH = 4
NQ = H // QH
QC = QH * C
VP = 32
FF = 512
NF = FF // 128
GB = 2
DG = 341
NG = 3
KH = 64
HD3 = H * KH
SEG = 64
NM = 16
NPM = 16
PRE = NM + NPM
HC = 4
LN_EPS = 1e-5
RMS_EPS = 1.1920929e-07
MASKED = -3.0e38


@dataclass(frozen=True)
class Batch:

    pair: object
    par: int

    @property
    def exists(self):
        return not isinstance(self.pair, int) or self.pair >= 0

    @property
    def first(self):
        return isinstance(self.pair, int) and (self.pair, self.par) == (0, 0)

    def __add__(self, k):
        p = self.par + k
        return Batch(self.pair + p // 2 if p // 2 else self.pair, p % 2)


class Event:

    def __init__(self, new_semaphore, name, phases, parts=1, transfers=0):
        self.parts, self.transfers = parts, transfers
        self.sems = [new_semaphore(f"{name}_{s}") for s in range(2)] if transfers else [new_semaphore(name)]
        self.before, self.total = {}, 0
        for phase, batches in phases:
            self.before[phase] = self.total
            self.total += batches

    def sem(self, b):
        return self.sems[b.par if self.transfers else 0]

    def count(self, phase, b, part=0):
        before = self.before[phase]
        if self.transfers:
            return (b.pair + (before // 2 + 1)) * (16 * self.transfers)
        return b.pair * (2 * self.parts) + ((b.par + before) * self.parts + part + 1)

    @property
    def total_count(self):
        return self.total // 2 * 16 * self.transfers


def drive(eng, n, step):
    lo, hi = 2, n - 2
    static = lambda t: step(Batch(t // 2, t % 2), lambda k: 0 <= t + k < n)
    for t in range(-1, lo):
        static(t)
    with eng.Fori(lo // 2, hi // 2) as i:
        for par in range(2):
            step(Batch(i, par), lambda k: True)
    for t in range(hi, n + 1):
        static(t)


def at(ap, b, per=1):
    return ap[bass.ds((b.pair * 2 + b.par) * per, per)]


def build_layers(nc, a, out):
    NB = a["x"].shape[0]
    PAIRS = NB // 2
    GROUPS = NB // GB
    with ExitStack() as ctx:
        def sb(name, shape, dt=F32):
            return ctx.enter_context(nc.sbuf_tensor("sb_" + name, shape, dt))

        def slots(name, shape, dt=F32, n=2):
            return [sb(f"{name}{s}", shape, dt) for s in range(n)]

        def sem(name):
            return ctx.enter_context(nc.semaphore(name))

        def scratch(name, shape):
            return nc.dram_tensor("scratch_" + name, shape, F32, kind="Internal").ap()

        bank = [ctx.enter_context(nc.psum_tensor(f"bank{i}", [128, 512], F32)) for i in range(8)]

        order = ["A0", "F0", "A1", "A2", "F2", "A3", "F3"]
        source, target = {}, {}
        held = a["x"]
        for ph in order:
            source[ph] = held
            held = out if ph == order[-1] else scratch("after_" + ph, [NB, T, D])
            target[ph] = held
        vmem_dram = scratch("vmem", [NB, HD3])

        ident = sb("ident", [128, 128])
        identb = sb("identb", [128, 128], BF16)
        causal = sb("causal", [T, QC], BF16)
        tri = sb("tri", [T, HC * SEG], BF16)
        headmask = sb("headmask", [D, H])
        halfmask = sb("halfmask", [D, 2])
        cos = sb("cos", [T, KH])
        sin = sb("sin", [T, KH])
        onesb = sb("onesb", [1, T], BF16)
        minus_half = sb("minus_half", [128, GB])
        ln_eps = sb("ln_eps", [128, GB])
        consts = [(ident, a["c_ident"]), 
                  (headmask, a["c_headmask"]), (halfmask, a["c_halfmask"]), (cos, a["c_cos"]), (sin, a["c_sin"])]

        def weight(name, shape, src):
            w = sb(name, shape)
            consts.append((w, src))
            return w

        def row_everywhere(name):
            n = a[name].shape[0]
            return weight(name, [128, n], a[name].partition_broadcast(128))

        def column(name):
            return weight(name, [128, 1], a[name].rearrange("(p a) -> p a", a=1))

        cross = {}
        for ph, p in (("A0", "L0_xattn_"), ("A1", "L1_xattn_"), ("A2", "L2_xattn_")):
            w = {k: weight(p + k, [D, D], a[p + k]) for k in ("wq", "wk", "wv")}
            if ph != "A2":
                w |= {k: column(p + k) for k in ("bq", "bk")}
                w["bv"] = row_everywhere(p + "bv")
            if ph == "A0":
                w["bo"] = w["bv"]
            else:
                w["wo"] = weight(p + "wo", [D, D], a[p + "wo"])
                w["bo"] = row_everywhere(p + "bo")
            w |= {k: row_everywhere(p + k) for k in ("ln_g", "ln_b")}
            cross[ph] = w
        ffw = {}
        for ph, p in (("F0", "L0_xattn_"), ("F2", "L2_xattn_")):
            ffw[ph] = {
                "w1": weight(p + "ffw1", [D, FF], a[p + "ffw1"]),
                "b1": weight(p + "ffb1", [128, NF], a[p + "ffb1"]),
                "w2": weight(p + "ffw2", [128, NF, D], a[p + "ffw2"]),
                "b2": row_everywhere(p + "ffb2"),
            }
        ffw["F2"] |= {"g": row_everywhere("L2_xattn_g2"), "b": row_everywhere("L2_xattn_beta2")}
        p = "L3_xattn_"
        wqkv = weight("wqkv", [D, 3 * HD3], a[p + "to_qkv_w"])
        wout3 = weight("wout3", [128, H // 2, D], a[p + "to_out_w"].rearrange("(c p) d -> p c d", p=128))
        attn_norm = column(p + "attn_norm_w")
        ff_norm = column(p + "ff_norm_w")
        pool_norm = row_everywhere(p + "mem_pool_norm_w")
        wmem = weight("wmem", [D, D], a[p + "to_mem_tokens_w"])
        w1g = weight("w1g", [D, 2 * NG * 128], a[p + "ffw1"])
        b1g = weight("b1g", [128, 2 * NG], a[p + "ffb1"])
        w2g = weight("w2g", [128, NG, D], a[p + "ffw2"])
        b2g = row_everywhere(p + "ff_b2")

        REGION = C * D
        region = sb("region", [128, REGION])

        class Carve:

            def __init__(self):
                self.used = 0

            def __call__(self, rows, cols):
                view = region[0:rows, self.used:self.used + cols]
                self.used += cols
                assert self.used <= REGION
                return view

            def slots(self, rows, cols):
                return [self(rows, cols) for _ in range(2)]

        ctx_all = region[0:NB, 0:C * D]

        carve = Carve()
        x_s = slots("x", [T, D])
        ctx_s = slots("ctx", [D, C])
        side_s = carve.slots(T, H * C)
        mask_s = slots("mask", [T, H * C], U8)
        keymask_s = slots("keymask", [1, C], I32)
        keybias_s = slots("keybias", [1, C], BF16)
        xT_s = slots("xT", [D, T])
        qT_s = slots("qT", [D, T])
        kT_s = slots("kT", [D, C])
        kblk_s = carve.slots(D, H * C)
        v_s = slots("v", [C, H * VP])
        xb_s = slots("xb", [T, D])
        prod_s = carve.slots(T, QC)
        scored_s = carve.slots(T, QC)
        shifted_s = carve.slots(T, QC)
        p_s = carve.slots(T, QC)
        pT_s = slots("pT", [C, QH * T])
        max_s = slots("max", [T, QH])
        att_s = carve.slots(128, NQ * T)
        rden_s = slots("rden", [T, H])
        o_s = slots("o", [T, D])
        oT_s = slots("oT", [D, T])
        t_s = slots("t", [T, D])
        stats_s = slots("stats", [T, 6])
        mv_s = slots("mv", [T, 2])
        var_s = slots("var", [T, 1])
        rstd_s = slots("rstd", [T, 1])
        z_s = slots("z", [T, D])
        zg_s = slots("zg", [T, D])
        y_s = slots("y", [T, D])

        fx_s = slots("fx", [T, GB, D])
        fxT_s = slots("fxT", [D, GB * T])
        fh_s = slots("fh", [128, NF, GB * T])
        fg_s = fh_s
        fsilu_s = slots("fsilu", [128, NG, GB * T])
        fxb_s = slots("fxb", [T, GB, D])
        ft_s = slots("ft", [T, GB, D])
        fc_s = slots("fc", [T, GB, D])
        fz_s = slots("fz", [T, GB, D])
        fn_s = slots("fn", [T, GB, D])
        fy_s = slots("fy", [T, GB, D])
        fsq_s = slots("fsq", [T, D])
        fstats_s = slots("fstats", [T, GB, 6])
        fmv_s = slots("fmv", [T, GB, 2])
        fvar_s = slots("fvar", [T, GB])
        frstd_s = slots("frstd", [T, GB])

        kmemT = sb("kmemT", [128, H // 2, NB])
        carve = Carve()
        sq_s = slots("sq", [T, D])
        xn_s = slots("xn", [T, D])
        xnT_s = slots("xnT", [D, T])
        ropeC = {k: carve.slots(T, HC * 2 * KH) for k in "qk"}
        ropeS = {k: carve.slots(T, HC * 2 * KH) for k in "qk"}
        turned = {k: carve.slots(T, HC * 2 * KH) for k in "qk"}
        turnedT = {k: carve.slots(128, HC * T) for k in "qk"}
        v3_s = carve.slots(T, HC * 2 * KH)
        kpre_s = slots("kpre", [128, H // 2, 2 * PRE])
        vpre_s = slots("vpre", [128, H // 4, 4, KH])
        l_s = slots("l", [T, 2 * HC * SEG])
        lp_s = slots("lp", [T, 2 * HC * PRE])
        m_loc = slots("m_loc", [T, 2 * HC])
        m_pre = slots("m_pre", [T, 2 * HC])
        m_all = slots("m_all", [T, 2 * HC])
        d_loc = slots("d_loc", [T, 2 * HC])
        d_pre = slots("d_pre", [T, 2 * HC])
        d_all = slots("d_all", [T, 2 * HC])
        r_all = slots("r_all", [T, 2 * HC])
        dense_s = slots("dense", [T, 2 * HC * T])
        pp_s = slots("pp", [T, 2 * HC * PRE])
        denseT_s = slots("denseT", [T, 2 * HC * T])
        causal32, tri32 = denseT_s[0][:, 0:QC], denseT_s[1][:, 0:HC * SEG]
        consts += [(causal32, a["c_causal"]), (tri32, a["c_tri"])]
        ppT_s = slots("ppT", [128, 2 * T])
        att3_s = slots("att3", [128, HC * T])

        loaded = sem("loaded")
        masks_made = sem("masks_made")
        setup = sem("setup_chain")
        mem_pooled = sem("mem_pooled")
        mem_poolT = sem("mem_poolT")
        mem_poolT_kept = sem("mem_poolT_kept")
        mem_tok = sem("mem_tok")
        mem_tok_kept = sem("mem_tok_kept")
        mem_kv = sem("mem_kv")
        mem_kv_kept = sem("mem_kv_kept")
        mem_stored = sem("mem_stored")
        weights_scaled = sem("weights_scaled")
        zeroed = sem("zeroed")
        N_LOADS = len(consts) + 12

        def event(name, phases, parts=1, transfers=0):
            return Event(sem, name, [(ph, NB if ph[0] == "A" else GROUPS) for ph in phases], parts, transfers)

        CROSS = ["A0", "A1", "A2"]
        X_loaded = event("X_loaded", CROSS, transfers=1)
        ctx_loaded = event("ctx_loaded", CROSS, transfers=1)
        side_loaded = event("side_loaded", ["A1"], transfers=1)
        mask_loaded = event("mask_loaded", ["A1"], transfers=1)
        keymask_loaded = event("keymask_loaded", ["A2"], transfers=1)
        keybias_made = event("keybias_made", ["A2"])
        kv_made = event("kv_made", CROSS)
        k_kept = event("k_kept", CROSS)
        v_kept = event("v_kept", CROSS)
        kblk_made = event("kblk_made", CROSS)
        xT_made = event("xT_made", CROSS)
        xT_kept = event("xT_kept", CROSS)
        q_made = event("q_made", CROSS)
        q_kept = event("q_kept", CROSS)
        xb_made = event("xb_made", CROSS)
        s_made = event("s_made", CROSS, parts=NQ)
        s_weighted = event("s_weighted", ["A1"], parts=NQ)
        s_masked = event("s_masked", ["A1"], parts=NQ)
        max_made = event("max_made", CROSS, parts=NQ)
        shifted = event("shifted", CROSS, parts=NQ)
        exp_made = event("exp_made", CROSS, parts=NQ)
        pT_made = event("pT_made", CROSS, parts=NQ)
        pT_kept = event("pT_kept", CROSS, parts=NQ)
        att_made = event("att_made", CROSS, parts=NQ)
        att_kept = event("att_kept", CROSS)
        back_made = event("back_made", CROSS)
        den_inverted = event("den_inverted", CROSS)
        o_made = event("o_made", CROSS)
        oT_made = event("oT_made", ["A1", "A2"])
        oT_kept = event("oT_kept", ["A1", "A2"])
        proj_made = event("proj_made", ["A1", "A2"])
        sum_made = event("sum_made", CROSS)
        stats_made = event("stats_made", CROSS)
        mv_made = event("mv_made", CROSS)
        var_made = event("var_made", CROSS)
        rstd_made = event("rstd_made", CROSS)
        z_made = event("z_made", CROSS)
        zg_made = event("zg_made", CROSS)
        y_made = event("y_made", CROSS)
        y_stored = event("y_stored", CROSS, transfers=1)

        FFS = ["F0", "F2", "F3"]
        fx_loaded = event("fx_loaded", FFS, transfers=1)
        fxT_made = {ph: event("fxT_made_" + ph, [ph]) for ph in FFS}
        fxT_kept = event("fxT_kept", FFS)
        fxb_made = {ph: event("fxb_made_" + ph, [ph]) for ph in FFS}
        PLAIN = ["F0", "F2"]
        hidden_made = event("hidden_made", PLAIN, parts=NF)
        hidden_kept = event("hidden_kept", PLAIN, parts=NF)
        gates_made = event("gates_made", ["F3"], parts=2 * NG)
        silu_kept = event("silu_kept", ["F3"], parts=NG)
        gated_kept = event("gated_kept", ["F3"], parts=NG)
        fo_made = event("fo_made", FFS)
        ft_made = event("ft_made", FFS)
        fstats_made = event("fstats_made", ["F2", "F3"], parts=GB)
        fmv_made = event("fmv_made", ["F2"], parts=GB)
        fcentred = event("fcentred", ["F2"], parts=GB)
        fvar_made = event("fvar_made", ["F2"])
        frstd_made = event("frstd_made", ["F2", "F3"])
        fz_made = {ph: event("fz_made_" + ph, [ph]) for ph in FFS[1:]}
        fzg_made = event("fzg_made", ["F2"])
        fy_made = event("fy_made", ["F2"])
        fy_stored = sem("fy_stored")
        fy_before = {ph: k * GROUPS for k, ph in enumerate(FFS)}

        x3_loaded = event("x3_loaded", ["A3"], transfers=1)
        vpre_loaded = event("vpre_loaded", ["A3"], transfers=4)
        sq_made = event("sq_made", ["A3"])
        rms_made = event("rms_made", ["A3"])
        xn_made = event("xn_made", ["A3"])
        xnT_made = event("xnT_made", ["A3"])
        xnT_kept = event("xnT_kept", ["A3"])
        q3_made = event("q3_made", ["A3"], parts=2)
        k3_made = event("k3_made", ["A3"], parts=2)
        v3_made = event("v3_made", ["A3"], parts=2)
        v3_kept = event("v3_kept", ["A3"], parts=2)
        q3_roped = event("q3_roped", ["A3"], parts=2)
        k3_roped = event("k3_roped", ["A3"], parts=2)
        q3_turned = event("q3_turned", ["A3"], parts=2)
        k3_turned = event("k3_turned", ["A3"], parts=2)
        qT3_made = event("qT3_made", ["A3"], parts=2)
        kT3_made = event("kT3_made", ["A3"], parts=2)
        qT3_kept = event("qT3_kept", ["A3"], parts=2)
        kT3_kept = event("kT3_kept", ["A3"], parts=2)
        kpre_made = event("kpre_made", ["A3"])
        s3_made = event("s3_made", ["A3"], parts=2)
        max3_parts = event("max3_parts", ["A3"], parts=2)
        max3_made = event("max3_made", ["A3"], parts=2)
        shifted3 = event("shifted3", ["A3"], parts=2)
        exp3_made = event("exp3_made", ["A3"], parts=2)
        den3_parts = event("den3_parts", ["A3"], parts=2)
        den3_sum = event("den3_sum", ["A3"], parts=2)
        den3_inv = event("den3_inv", ["A3"], parts=2)
        p3_rows = event("p3_rows", ["A3"], parts=4)
        p3_made = event("p3_made", ["A3"], parts=2)
        pT3_made = event("pT3_made", ["A3"], parts=6)
        pT3_kept = event("pT3_kept", ["A3"], parts=6)
        att3_made = event("att3_made", ["A3"], parts=2)
        att3_kept = event("att3_kept", ["A3"], parts=2)
        proj3_made = event("proj3_made", ["A3"])
        y3_made = event("y3_made", ["A3"])
        y3_stored = event("y3_stored", ["A3"], transfers=1)

        SCALE = {"A0": DH ** -0.5, "A1": DH ** -0.5, "A2": D ** -0.5}
        scores_bank = bank[0:2]
        pT_bank = bank[2:4]
        att_bank = bank[4:6]
        in_bank = bank[6]
        out_bank = bank[7]
        K_COL, V_COL = 128, 256

        def quarter(ap, c):
            return ap[:, c * QC:(c + 1) * QC]

        def by_head(ap):
            return ap.rearrange("p (h k) -> p h k", k=C)

        def spread(col, n):
            return col.unsqueeze(2).to_broadcast([col.shape[0], col.shape[1], n])

        def phase_before(ph):
            return order[order.index(ph) - 1] if ph != order[0] else None

        def two_before(b, c):
            return (b if c >= 2 else b + -1), (c - 2) % NQ

        def cross_sync(sp, ph):
            def load(b):
                if (b + -2).exists:
                    sp.wait_ge(kv_made.sem(b + -2), kv_made.count(ph, b + -2))
                sp.dma_start(ctx_s[b.par][:], at(a["ctxT"], b).rearrange("b d k -> (b d) k")).then_inc(ctx_loaded.sem(b), 16)
                if ph == "A1":
                    if (b + -2).exists:
                        sp.wait_ge(s_weighted.sem(b + -2), s_weighted.count(ph, b + -2, NQ - 1))
                    sp.dma_start(side_s[b.par][:], at(a["side"], b).rearrange("b t n -> (b t) n")).then_inc(side_loaded.sem(b), 16)
                    if (b + -2).exists:
                        sp.wait_ge(s_masked.sem(b + -2), s_masked.count(ph, b + -2, NQ - 1))
                    sp.dma_start(mask_s[b.par][:], at(a["mask"], b).rearrange("b t n -> (b t) n")).then_inc(mask_loaded.sem(b), 16)
                if ph == "A2":
                    if (b + -2).exists:
                        sp.wait_ge(keybias_made.sem(b + -2), keybias_made.count(ph, b + -2))
                    sp.dma_start(keymask_s[b.par][:], at(a["keymask"], b)).then_inc(keymask_loaded.sem(b), 16)
                prev = phase_before(ph)
                if prev in FFS:
                    sp.wait_ge(fy_stored, (b.pair + (fy_before[prev] + 1)) * 16)
                elif prev:
                    sp.wait_ge(y_stored.sem(b), y_stored.count(prev, b))
                if (b + -2).exists:
                    sp.wait_ge(xT_made.sem(b + -2), xT_made.count(ph, b + -2))
                if (b + -2).exists:
                    sp.wait_ge(xb_made.sem(b + -2), xb_made.count(ph, b + -2))
                sp.dma_start(x_s[b.par][:], at(source[ph], b).rearrange("b t d -> (b t) d")).then_inc(X_loaded.sem(b), 16)

            def step(b, has):
                if has(1):
                    load(b + 1)
                if has(-1):
                    if (b + -1).exists:
                        sp.wait_ge(y_made.sem(b + -1), y_made.count(ph, b + -1))
                    sp.dma_start(at(target[ph], b + -1).rearrange("b t d -> (b t) d"), y_s[(b + -1).par][:]).then_inc(y_stored.sem(b + -1), 16)
            drive(sp, NB, step)

        def cross_tensor(pe, ph):
            w = cross[ph]

            def project_context(b):
                if (b + -1).exists:
                    pe.wait_ge(q_kept.sem(b + -1), q_kept.count(ph, b + -1))
                pe.wait_ge(ctx_loaded.sem(b), ctx_loaded.count(ph, b))
                nc.tensor.matmul(in_bank[:, K_COL:K_COL + C], w["wk"][:], ctx_s[b.par][:], start=True, stop=True)
                nc.tensor.matmul(in_bank[0:C, V_COL:V_COL + D], ctx_s[b.par][:], w["wv"][:], start=True, stop=True).then_inc(kv_made.sem(b), 1)

            def transpose_x(b):
                pe.wait_ge(X_loaded.sem(b), X_loaded.count(ph, b))
                pe.wait_ge(k_kept.sem(b), k_kept.count(ph, b))
                pe.wait_ge(v_kept.sem(b), v_kept.count(ph, b))
                nc.tensor.transpose(in_bank[:, 0:T], x_s[b.par][:], ident[:]).then_inc(xT_made.sem(b), 1)

            def project_queries(b):
                pe.wait_ge(xT_kept.sem(b), xT_kept.count(ph, b))
                nc.tensor.matmul(in_bank[:, 0:T], w["wq"][:], xT_s[b.par][:], start=True, stop=True).then_inc(q_made.sem(b), 1)

            def scores(b, c):
                if c == 0:
                    pe.wait_ge(q_kept.sem(b), q_kept.count(ph, b))
                    pe.wait_ge(kblk_made.sem(b), kblk_made.count(ph, b))
                    if ph == "A2":
                        pe.wait_ge(keybias_made.sem(b), keybias_made.count(ph, b))
                done = s_weighted if ph == "A1" else shifted
                old, old_c = two_before(b, c)
                if old.exists:
                    pe.wait_ge(done.sem(old), done.count(ph, old, old_c))
                dst = scores_bank[c % 2][:, 0:QC]
                mm = nc.tensor.matmul(dst, qT_s[b.par][:], quarter(kblk_s[b.par], c), start=True, stop=(ph == "A1"))
                if ph == "A0":
                    mm = nc.tensor.matmul(dst, identb[:], causal[:], start=False, stop=True)
                if ph == "A2":
                    bias = keybias_s[b.par][0:1, :].unsqueeze(1).to_broadcast([1, QH, C])
                    mm = nc.tensor.matmul(dst, onesb[0:1, :], bias, start=False, stop=True)
                mm.then_inc(s_made.sem(b), 1)

            def transpose_p(b, c):
                pe.wait_ge(exp_made.sem(b), exp_made.count(ph, b, c))
                old, old_c = two_before(b, c)
                if old.exists:
                    pe.wait_ge(pT_kept.sem(old), pT_kept.count(ph, old, old_c))
                for h in range(QH):
                    mm = nc.tensor.transpose(pT_bank[c % 2][0:C, h * T:(h + 1) * T], p_s[c % 2][:, h * C:(h + 1) * C], ident[:])
                mm.then_inc(pT_made.sem(b), 1)

            def attend(b, c):
                pe.wait_ge(pT_kept.sem(b), pT_kept.count(ph, b, c))
                if c == 0:
                    pe.wait_ge(v_kept.sem(b), v_kept.count(ph, b))
                    if (b + -2).exists:
                        pe.wait_ge(att_kept.sem(b + -2), att_kept.count(ph, b + -2))
                for h in range(QH):
                    head = c * QH + h
                    mm = nc.tensor.matmul(att_bank[b.par][VP * h:VP * h + VP, c * T:(c + 1) * T],
                                          v_s[b.par][:, head * VP:(head + 1) * VP], pT_s[c % 2][:, h * T:(h + 1) * T],
                                          start=True, stop=True)
                mm.then_inc(att_made.sem(b), 1)

            def back(b):
                pe.wait_ge(att_kept.sem(b), att_kept.count(ph, b))
                done = o_made if ph == "A0" else sum_made
                if (b + -1).exists:
                    pe.wait_ge(done.sem(b + -1), done.count(ph, b + -1))
                for c in range(NQ):
                    mm = nc.tensor.transpose(out_bank[:, c * T:(c + 1) * T], att_s[b.par][:, c * T:(c + 1) * T], ident[:])
                mm.then_inc(back_made.sem(b), 1)

            def transpose_o(b):
                pe.wait_ge(o_made.sem(b), o_made.count(ph, b))
                nc.tensor.transpose(out_bank[:, 0:T], o_s[b.par][:], ident[:]).then_inc(oT_made.sem(b), 1)

            def project_out(b):
                pe.wait_ge(oT_kept.sem(b), oT_kept.count(ph, b))
                nc.tensor.matmul(out_bank[:, 0:D], oT_s[b.par][:], w["wo"][:], start=True, stop=True).then_inc(proj_made.sem(b), 1)

            def step(b, has):
                if has(0):
                    scores(b, 0)
                if has(1):
                    project_context(b + 1)
                if has(-1):
                    attend(b + -1, 3)
                if has(0):
                    scores(b, 1)
                    transpose_p(b, 0)
                if has(-1):
                    back(b + -1)
                if has(0):
                    scores(b, 2)
                    attend(b, 0)
                    transpose_p(b, 1)
                if has(-1) and ph != "A0":
                    transpose_o(b + -1)
                if has(1):
                    transpose_x(b + 1)
                if has(0):
                    scores(b, 3)
                if has(-1) and ph != "A0":
                    project_out(b + -1)
                if has(0):
                    attend(b, 1)
                    transpose_p(b, 2)
                if has(1):
                    project_queries(b + 1)
                if has(0):
                    attend(b, 2)
                    transpose_p(b, 3)
            drive(pe, NB, step)

        def cross_scalar(act, ph):
            w = cross[ph]

            def exps(b, c):
                act.wait_ge(shifted.sem(b), shifted.count(ph, b, c))
                old, old_c = two_before(b, c)
                if old.exists:
                    act.wait_ge(pT_made.sem(old), pT_made.count(ph, old, old_c))
                nc.scalar.activation(p_s[c % 2][:], shifted_s[c % 2][:], ACT.Exp, scale=SCALE[ph]).then_inc(exp_made.sem(b), 1)

            def keep_pT(b, c):
                act.wait_ge(pT_made.sem(b), pT_made.count(ph, b, c))
                old, old_c = two_before(b, c)
                if old.exists:
                    act.wait_ge(att_made.sem(old), att_made.count(ph, old, old_c))
                nc.scalar.activation(pT_s[c % 2][:], pT_bank[c % 2][0:C, :], ACT.Copy).then_inc(pT_kept.sem(b), 1)

            def keep_k(b):
                act.wait_ge(kv_made.sem(b), kv_made.count(ph, b))
                if (b + -2).exists:
                    act.wait_ge(kblk_made.sem(b + -2), kblk_made.count(ph, b + -2))
                src = in_bank[:, K_COL:K_COL + C]
                if ph == "A2":
                    nc.scalar.activation(kT_s[b.par][:], src, ACT.Copy).then_inc(k_kept.sem(b), 1)
                else:
                    nc.scalar.activation(kT_s[b.par][:], src, ACT.Identity, bias=w["bk"][:, 0:1]).then_inc(k_kept.sem(b), 1)

            def keep_xT(b):
                act.wait_ge(xT_made.sem(b), xT_made.count(ph, b))
                if (b + -2).exists:
                    act.wait_ge(q_made.sem(b + -2), q_made.count(ph, b + -2))
                nc.scalar.activation(xT_s[b.par][:], in_bank[:, 0:T], ACT.Copy).then_inc(xT_kept.sem(b), 1)

            def keep_q(b):
                act.wait_ge(q_made.sem(b), q_made.count(ph, b))
                if (b + -2).exists:
                    act.wait_ge(s_made.sem(b + -2), s_made.count(ph, b + -2, NQ - 1))
                if ph == "A2":
                    nc.scalar.activation(qT_s[b.par][:], in_bank[:, 0:T], ACT.Copy).then_inc(q_kept.sem(b), 1)
                else:
                    nc.scalar.activation(qT_s[b.par][:], in_bank[:, 0:T], ACT.Identity, bias=w["bq"][:, 0:1]).then_inc(q_kept.sem(b), 1)

            def keep_att(b):
                act.wait_ge(att_made.sem(b), att_made.count(ph, b, NQ - 1))
                if (b + -2).exists:
                    act.wait_ge(back_made.sem(b + -2), back_made.count(ph, b + -2))
                nc.scalar.activation(att_s[b.par][:], att_bank[b.par][:], ACT.Copy).then_inc(att_kept.sem(b), 1)

            def keep_oT(b):
                act.wait_ge(oT_made.sem(b), oT_made.count(ph, b))
                if (b + -2).exists:
                    act.wait_ge(proj_made.sem(b + -2), proj_made.count(ph, b + -2))
                nc.scalar.activation(oT_s[b.par][:], out_bank[:, 0:T], ACT.Copy).then_inc(oT_kept.sem(b), 1)

            def step(b, has):
                if has(-1):
                    keep_pT(b + -1, 3)
                if has(0):
                    exps(b, 0)
                if has(1):
                    keep_k(b + 1)
                if has(-1):
                    keep_att(b + -1)
                if has(0):
                    exps(b, 1)
                    keep_pT(b, 0)
                    exps(b, 2)
                    keep_pT(b, 1)
                if has(-1) and ph != "A0":
                    keep_oT(b + -1)
                if has(1):
                    keep_xT(b + 1)
                if has(0):
                    exps(b, 3)
                    keep_pT(b, 2)
                if has(1):
                    keep_q(b + 1)
            drive(act, NB, step)

        def cross_vector(dve, ph):
            w = cross[ph]

            def shift(b, c):
                dve.wait_ge(s_made.sem(b), s_made.count(ph, b, c))
                src = scores_bank[c % 2][:, 0:QC]
                if ph == "A1":
                    if c == 0:
                        dve.wait_ge(side_loaded.sem(b), side_loaded.count(ph, b))
                        dve.wait_ge(mask_loaded.sem(b), mask_loaded.count(ph, b))
                    nc.vector.tensor_tensor(prod_s[c % 2][:], src, quarter(side_s[b.par], c), ALU.mult).then_inc(s_weighted.sem(b), 1)
                    dve.wait_ge(s_weighted.sem(b), s_weighted.count(ph, b, c))
                    nc.vector.scalar_tensor_tensor(scored_s[c % 2][:], quarter(mask_s[b.par], c), MASKED, prod_s[c % 2][:],
                                                   ALU.mult, ALU.add).then_inc(s_masked.sem(b), 1)
                    dve.wait_ge(s_masked.sem(b), s_masked.count(ph, b, c))
                    src = scored_s[c % 2][:]
                nc.vector.tensor_reduce(max_s[c % 2][:], by_head(src), AX.X, ALU.max).then_inc(max_made.sem(b), 1)
                dve.wait_ge(max_made.sem(b), max_made.count(ph, b, c))
                old, old_c = two_before(b, c)
                if old.exists:
                    dve.wait_ge(exp_made.sem(old), exp_made.count(ph, old, old_c))
                nc.vector.tensor_tensor(by_head(shifted_s[c % 2][:]), by_head(src), spread(max_s[c % 2][:], C), ALU.subtract)\
                    .then_inc(shifted.sem(b), 1)

            def keep_v(b):
                dve.wait_ge(kv_made.sem(b), kv_made.count(ph, b))
                dve.wait_ge(k_kept.sem(b), k_kept.count(ph, b))
                if (b + -2).exists:
                    dve.wait_ge(att_made.sem(b + -2), att_made.count(ph, b + -2, NQ - 1))
                dst = v_s[b.par][:].rearrange("p (h v) -> p h v", v=VP)[:, :, 0:DH]
                src = in_bank[0:C, V_COL:V_COL + D].rearrange("p (h v) -> p h v", v=DH)
                if ph != "A1":
                    nc.vector.tensor_copy(dst, src).then_inc(v_kept.sem(b), 1)
                else:
                    nc.vector.tensor_tensor(dst, src, w["bv"][0:C, :].rearrange("p (h v) -> p h v", v=DH), ALU.add).then_inc(v_kept.sem(b), 1)

            def key_bias(b):
                dve.wait_ge(keymask_loaded.sem(b), keymask_loaded.count(ph, b))
                if (b + -2).exists:
                    dve.wait_ge(s_made.sem(b + -2), s_made.count(ph, b + -2, NQ - 1))
                nc.vector.tensor_scalar(keybias_s[b.par][:], keymask_s[b.par][:], 0, -1.0e20, ALU.is_equal, ALU.mult)\
                    .then_inc(keybias_made.sem(b), 1)

            def normalise(b):
                dve.wait_ge(back_made.sem(b), back_made.count(ph, b))
                raw = out_bank[:].rearrange("p (h v) -> p h v", v=VP)
                nc.vector.reciprocal(rden_s[b.par][:].unsqueeze(2), raw[:, :, DH:DH + 1]).then_inc(den_inverted.sem(b), 1)
                dve.wait_ge(den_inverted.sem(b), den_inverted.count(ph, b))
                if ph == "A0":
                    if (b + -2).exists:
                        dve.wait_ge(sum_made.sem(b + -2), sum_made.count(ph, b + -2))
                else:
                    if (b + -2).exists:
                        dve.wait_ge(oT_made.sem(b + -2), oT_made.count(ph, b + -2))
                nc.vector.tensor_tensor(o_s[b.par][:].rearrange("p (h v) -> p h v", v=DH), raw[:, :, 0:DH],
                                        spread(rden_s[b.par][:], DH), ALU.mult).then_inc(o_made.sem(b), 1)

            def sums(b):
                if (b + -2).exists:
                    dve.wait_ge(z_made.sem(b + -2), z_made.count(ph, b + -2))
                dve.wait_ge(xb_made.sem(b), xb_made.count(ph, b))
                if ph == "A0":
                    dve.wait_ge(o_made.sem(b), o_made.count(ph, b))
                    nc.vector.tensor_tensor(t_s[b.par][:], o_s[b.par][:], xb_s[b.par][:], ALU.add).then_inc(sum_made.sem(b), 1)
                else:
                    dve.wait_ge(proj_made.sem(b), proj_made.count(ph, b))
                    nc.vector.tensor_tensor(t_s[b.par][:], out_bank[:, 0:D], xb_s[b.par][:], ALU.add).then_inc(sum_made.sem(b), 1)
                dve.wait_ge(sum_made.sem(b), sum_made.count(ph, b))
                nc.vector.bn_stats(stats_s[b.par][:], t_s[b.par][:]).then_inc(stats_made.sem(b), 1)
                dve.wait_ge(stats_made.sem(b), stats_made.count(ph, b))

            def aggregate(b):
                nc.vector.bn_aggr(mv_s[b.par][:], stats_s[b.par][:]).then_inc(mv_made.sem(b), 1)

            def centre(b):
                dve.wait_ge(rstd_made.sem(b), rstd_made.count(ph, b))
                if (b + -2).exists:
                    dve.wait_ge(zg_made.sem(b + -2), zg_made.count(ph, b + -2))
                nc.vector.tensor_scalar(z_s[b.par][:], t_s[b.par][:], mv_s[b.par][:, 0:1], rstd_s[b.par][:, 0:1],
                                        ALU.subtract, ALU.mult).then_inc(z_made.sem(b), 1)

            def step(b, has):
                if has(0):
                    shift(b, 0)
                if has(1):
                    keep_v(b + 1)
                    if ph == "A2":
                        key_bias(b + 1)
                if has(0):
                    shift(b, 1)
                if has(-1):
                    normalise(b + -1)
                if has(0):
                    shift(b, 2)
                if has(-1):
                    sums(b + -1)
                if has(0):
                    shift(b, 3)
                if has(-1):
                    aggregate(b + -1)
                    centre(b + -1)
            drive(dve, NB, step)

        def cross_gpsimd(pool, ph):
            w = cross[ph]

            def block_keys(b):
                pool.wait_ge(k_kept.sem(b), k_kept.count(ph, b))
                if (b + -2).exists:
                    pool.wait_ge(s_made.sem(b + -2), s_made.count(ph, b + -2, NQ - 1))
                nc.gpsimd.tensor_tensor(by_head(kblk_s[b.par][:]), kT_s[b.par][:].unsqueeze(1).to_broadcast([D, H, C]),
                                        spread(headmask[:], C), ALU.mult).then_inc(kblk_made.sem(b), 1)

            def residual(b):
                pool.wait_ge(X_loaded.sem(b), X_loaded.count(ph, b))
                if (b + -2).exists:
                    pool.wait_ge(sum_made.sem(b + -2), sum_made.count(ph, b + -2))
                nc.gpsimd.tensor_tensor(xb_s[b.par][:], x_s[b.par][:], w["bo"][:], ALU.add).then_inc(xb_made.sem(b), 1)

            def rstd(b):
                pool.wait_ge(mv_made.sem(b), mv_made.count(ph, b))
                nc.gpsimd.tensor_tensor(var_s[b.par][:], mv_s[b.par][:, 1:2], ln_eps[:, 0:1], ALU.add).then_inc(var_made.sem(b), 1)
                pool.wait_ge(var_made.sem(b), var_made.count(ph, b))
                if (b + -2).exists:
                    pool.wait_ge(z_made.sem(b + -2), z_made.count(ph, b + -2))
                nc.gpsimd.tensor_tensor(rstd_s[b.par][:], var_s[b.par][:], minus_half[:, 0:1], ALU.pow).then_inc(rstd_made.sem(b), 1)

            def affine(b):
                pool.wait_ge(z_made.sem(b), z_made.count(ph, b))
                nc.gpsimd.tensor_tensor(zg_s[b.par][:], z_s[b.par][:], w["ln_g"][:], ALU.mult).then_inc(zg_made.sem(b), 1)
                pool.wait_ge(zg_made.sem(b), zg_made.count(ph, b))
                if (b + -2).exists:
                    pool.wait_ge(y_stored.sem(b + -2), y_stored.count(ph, b + -2))
                nc.gpsimd.tensor_tensor(y_s[b.par][:], zg_s[b.par][:], w["ln_b"][:], ALU.add).then_inc(y_made.sem(b), 1)

            def step(b, has):
                if has(1):
                    block_keys(b + 1)
                    residual(b + 1)
                if has(-1):
                    rstd(b + -1)
                    affine(b + -1)
            drive(pool, NB, step)

        FT = GB * T
        fx_bank = bank[0:2]
        fh_bank = bank[2:6]
        fo_bank = bank[6:8]

        def chunks(ph):
            return 2 * NG if ph == "F3" else NF

        def chunk_before(ph, g, j, n):
            j -= n
            return (g, j) if j >= 0 else (g + -1, j + chunks(ph))

        def chunk_bank(ph, g, j):
            return fh_bank[(chunks(ph) * g.par + j) % 4][:, 0:FT]

        def pair_of(ap, g):
            return at(ap, g, GB).rearrange("b t d -> t b d")

        def ff_sync(sp, ph):
            taken = fz_made[ph] if ph == "F3" else fxT_made[ph]

            def step(g, has):
                if has(1):
                    n = g + 1
                    if (n + -2).exists:
                        sp.wait_ge(taken.sem(n + -2), taken.count(ph, n + -2))
                    if (n + -2).exists:
                        sp.wait_ge(fxb_made[ph].sem(n + -2), fxb_made[ph].count(ph, n + -2))
                    stored = y3_stored if ph == "F3" else y_stored
                    even, odd = (Batch(n.pair * 2 + n.par, k) for k in range(2))
                    sp.wait_ge(stored.sem(even), stored.count(phase_before(ph), even))
                    sp.wait_ge(stored.sem(odd), stored.count(phase_before(ph), odd))
                    sp.dma_start(fx_s[n.par][:], pair_of(source[ph], n)).then_inc(fx_loaded.sem(n), 16)
                if has(-1):
                    p = g + -1
                    done = fy_made if ph == "F2" else ft_made
                    sp.wait_ge(done.sem(p), done.count(ph, p))
                    sp.dma_start(pair_of(target[ph], p), (fy_s if ph == "F2" else ft_s)[p.par][:]).then_inc(fy_stored, 16)
            drive(sp, GROUPS, step)

        def ff_tensor(pe, ph):
            w1, w2 = (w1g, w2g) if ph == "F3" else (ffw[ph]["w1"], ffw[ph]["w2"])
            made = gates_made if ph == "F3" else hidden_made

            def wait_kept(g, j):
                if ph == "F3":
                    done = (silu_kept, gated_kept)[j % 2]
                    pe.wait_ge(done.sem(g), done.count(ph, g, j // 2))
                else:
                    pe.wait_ge(hidden_kept.sem(g), hidden_kept.count(ph, g, j))

            def transpose_x(g):
                if (g + -2).exists:
                    pe.wait_ge(fxT_kept.sem(g + -2), fxT_kept.count(ph, g + -2))
                for k in range(GB):
                    if ph == "F3":
                        pe.wait_ge(fz_made[ph].sem(g), fz_made[ph].count(ph, g))
                        src = fz_s[g.par][:, k, :]
                    else:
                        pe.wait_ge(fx_loaded.sem(g), fx_loaded.count(ph, g))
                        src = fx_s[g.par][:, k, :]
                    mm = nc.tensor.transpose(fx_bank[g.par][:, k * T:(k + 1) * T], src, ident[:])
                mm.then_inc(fxT_made[ph].sem(g), 1)

            def hidden(g):
                pe.wait_ge(fxT_kept.sem(g), fxT_kept.count(ph, g))
                for j in range(chunks(ph)):
                    bg, bj = chunk_before(ph, g, j, 4)
                    if bg.exists:
                        wait_kept(bg, bj)
                    col = ((j // 2 + NG * (1 - j % 2)) if ph == "F3" else j) * 128
                    nc.tensor.matmul(chunk_bank(ph, g, j), w1[:, col:col + 128], fxT_s[g.par][:], start=True, stop=True)\
                        .then_inc(made.sem(g), 1)

            def down(g):
                last = range(1, 2 * NG, 2) if ph == "F3" else range(NF)
                wait_kept(g, last[-1])
                if (g + -2).exists:
                    pe.wait_ge(ft_made.sem(g + -2), ft_made.count(ph, g + -2))
                for k in range(GB):
                    for f in range(len(last)):
                        mm = nc.tensor.matmul(fo_bank[g.par][:, k * D:(k + 1) * D], fh_s[g.par][:, f, k * T:(k + 1) * T],
                                              w2[:, f, :], start=(f == 0), stop=(f == len(last) - 1))
                mm.then_inc(fo_made.sem(g), 1)

            def step(g, has):
                if has(0):
                    hidden(g)
                if has(1):
                    transpose_x(g + 1)
                if has(-1):
                    down(g + -1)
            drive(pe, GROUPS, step)

        def ff_scalar(act, ph):
            made = gates_made if ph == "F3" else hidden_made

            def keep_xT(g):
                act.wait_ge(fxT_made[ph].sem(g), fxT_made[ph].count(ph, g))
                if (g + -2).exists:
                    act.wait_ge(made.sem(g + -2), made.count(ph, g + -2, chunks(ph) - 1))
                nc.scalar.activation(fxT_s[g.par][:], fx_bank[g.par][:, 0:FT], ACT.Copy).then_inc(fxT_kept.sem(g), 1)

            def activate(g):
                for j in range(0, chunks(ph), 2 if ph == "F3" else 1):
                    act.wait_ge(made.sem(g), made.count(ph, g, j))
                    src = chunk_bank(ph, g, j)
                    if ph == "F3":
                        if (g + -2).exists:
                            act.wait_ge(gated_kept.sem(g + -2), gated_kept.count(ph, g + -2, j // 2))
                        nc.scalar.activation(fsilu_s[g.par][:, j // 2, :], src, ACT.Silu, bias=b1g[:, NG + j // 2:NG + j // 2 + 1])\
                            .then_inc(silu_kept.sem(g), 1)
                    else:
                        if (g + -2).exists:
                            act.wait_ge(fo_made.sem(g + -2), fo_made.count(ph, g + -2))
                        nc.scalar.activation(fh_s[g.par][:, j, :], src, ACT.Gelu if ph == "F0" else ACT.Relu,
                                             bias=ffw[ph]["b1"][:, j:j + 1]).then_inc(hidden_kept.sem(g), 1)

            def step(g, has):
                if has(0):
                    activate(g)
                if has(1):
                    keep_xT(g + 1)
            drive(act, GROUPS, step)

        def ff_vector(dve, ph):
            def squares(g):
                dve.wait_ge(fx_loaded.sem(g), fx_loaded.count(ph, g))
                if (g + -2).exists:
                    dve.wait_ge(frstd_made.sem(g + -2), frstd_made.count(ph, g + -2))
                for k in range(GB):
                    nc.vector.tensor_tensor_reduce(fsq_s[k][:], fx_s[g.par][:, k, :], fx_s[g.par][:, k, :], 1.0 / D, RMS_EPS, ALU.mult, ALU.add,
                                                   fvar_s[g.par][:, k:k + 1]).then_inc(fstats_made.sem(g), 1)

            def norm(g):
                dve.wait_ge(frstd_made.sem(g), frstd_made.count(ph, g))
                if (g + -2).exists:
                    dve.wait_ge(fxT_made[ph].sem(g + -2), fxT_made[ph].count(ph, g + -2))
                nc.vector.tensor_tensor(fz_s[g.par][:], fx_s[g.par][:], spread(frstd_s[g.par][:], D), ALU.mult).then_inc(fz_made[ph].sem(g), 1)

            def gate(g):
                for f in range(NG):
                    dve.wait_ge(gates_made.sem(g), gates_made.count(ph, g, 2 * f + 1))
                    dve.wait_ge(silu_kept.sem(g), silu_kept.count(ph, g, f))
                    if (g + -2).exists:
                        dve.wait_ge(fo_made.sem(g + -2), fo_made.count(ph, g + -2))
                    nc.vector.scalar_tensor_tensor(fh_s[g.par][:, f, :], chunk_bank(ph, g, 2 * f + 1), b1g[:, f:f + 1],
                                                   fsilu_s[g.par][:, f, :], ALU.add, ALU.mult).then_inc(gated_kept.sem(g), 1)

            def total(g):
                dve.wait_ge(fo_made.sem(g), fo_made.count(ph, g))
                dve.wait_ge(fxb_made[ph].sem(g), fxb_made[ph].count(ph, g))
                if ph == "F2":
                    if (g + -2).exists:
                        dve.wait_ge(fz_made[ph].sem(g + -2), fz_made[ph].count(ph, g + -2))
                else:
                    if not (ph == "F0" and g.first):
                        dve.wait_ge(fy_stored, (g.pair * 2 + (g.par + fy_before[ph])) * 16)
                nc.vector.tensor_tensor(ft_s[g.par][:], fo_bank[g.par][:, 0:GB * D].rearrange("p (b d) -> p b d", b=GB),
                                        fxb_s[g.par][:], ALU.add).then_inc(ft_made.sem(g), 1)

            def layernorm(g):
                dve.wait_ge(ft_made.sem(g), ft_made.count(ph, g))
                nc.vector.bn_stats(fstats_s[g.par][:, 0, :], ft_s[g.par][:, 0, :]).then_inc(fstats_made.sem(g), 1)
                dve.wait_ge(fstats_made.sem(g), fstats_made.count(ph, g, 0))
                nc.vector.bn_stats(fstats_s[g.par][:, 1, :], ft_s[g.par][:, 1, :]).then_inc(fstats_made.sem(g), 1)
                nc.vector.bn_aggr(fmv_s[g.par][:, 0, :], fstats_s[g.par][:, 0, :]).then_inc(fmv_made.sem(g), 1)
                dve.wait_ge(fmv_made.sem(g), fmv_made.count(ph, g, 0))
                dve.wait_ge(fstats_made.sem(g), fstats_made.count(ph, g, 1))
                if (g + -2).exists:
                    dve.wait_ge(fz_made[ph].sem(g + -2), fz_made[ph].count(ph, g + -2))
                centred(g, 0)
                nc.vector.bn_aggr(fmv_s[g.par][:, 1, :], fstats_s[g.par][:, 1, :]).then_inc(fmv_made.sem(g), 1)
                dve.wait_ge(fmv_made.sem(g), fmv_made.count(ph, g, 1))
                centred(g, 1)
                dve.wait_ge(frstd_made.sem(g), frstd_made.count(ph, g))
                dve.wait_ge(fcentred.sem(g), fcentred.count(ph, g, 1))
                if (g + -2).exists:
                    dve.wait_ge(fzg_made.sem(g + -2), fzg_made.count(ph, g + -2))
                nc.vector.tensor_tensor(fz_s[g.par][:], fc_s[g.par][:], spread(frstd_s[g.par][:], D), ALU.mult).then_inc(fz_made[ph].sem(g), 1)

            def centred(g, k):
                nc.vector.tensor_scalar(fc_s[g.par][:, k, :], ft_s[g.par][:, k, :], fmv_s[g.par][:, k, 0:1], None, ALU.subtract)\
                    .then_inc(fcentred.sem(g), 1)

            def step(g, has):
                if has(1) and ph == "F3":
                    squares(g + 1)
                    norm(g + 1)
                if has(0) and ph == "F3":
                    gate(g)
                if has(-1):
                    total(g + -1)
                    if ph == "F2":
                        layernorm(g + -1)
            drive(dve, GROUPS, step)

        def ff_gpsimd(pool, ph):
            b2 = b2g if ph == "F3" else ffw[ph]["b2"]

            def every(row):
                return row[:].unsqueeze(1).to_broadcast([T, GB, D])

            def residual(g):
                pool.wait_ge(fx_loaded.sem(g), fx_loaded.count(ph, g))
                if (g + -2).exists:
                    pool.wait_ge(ft_made.sem(g + -2), ft_made.count(ph, g + -2))
                nc.gpsimd.tensor_tensor(fxb_s[g.par][:], fx_s[g.par][:], every(b2), ALU.add).then_inc(fxb_made[ph].sem(g), 1)

            def rstd(g):
                done = fstats_made if ph == "F3" else fmv_made
                pool.wait_ge(done.sem(g), done.count(ph, g, GB - 1))
                if ph == "F2":
                    nc.gpsimd.tensor_tensor(fvar_s[g.par][:], fmv_s[g.par][:, :, 1], ln_eps[:], ALU.add).then_inc(fvar_made.sem(g), 1)
                    pool.wait_ge(fvar_made.sem(g), fvar_made.count(ph, g))
                if (g + -2).exists:
                    pool.wait_ge(fz_made[ph].sem(g + -2), fz_made[ph].count(ph, g + -2))
                nc.gpsimd.tensor_tensor(frstd_s[g.par][:], fvar_s[g.par][:], minus_half[:], ALU.pow).then_inc(frstd_made.sem(g), 1)

            def affine(g):
                pool.wait_ge(fz_made[ph].sem(g), fz_made[ph].count(ph, g))
                nc.gpsimd.tensor_tensor(fn_s[g.par][:], fz_s[g.par][:], every(ffw[ph]["g"]), ALU.mult).then_inc(fzg_made.sem(g), 1)
                pool.wait_ge(fzg_made.sem(g), fzg_made.count(ph, g))
                pool.wait_ge(fy_stored, (g.pair * 2 + (g.par + fy_before[ph])) * 16)
                nc.gpsimd.tensor_tensor(fy_s[g.par][:], fn_s[g.par][:], every(ffw[ph]["b"]), ALU.add).then_inc(fy_made.sem(g), 1)

            def step(g, has):
                if has(1):
                    if ph == "F3":
                        rstd(g + 1)
                    residual(g + 1)
                if has(-1) and ph == "F2":
                    rstd(g + -1)
                    affine(g + -1)
            drive(pool, GROUPS, step)

        ph3 = "A3"
        in3 = bank[0:2]
        turn3 = bank[2:4]
        s_even, s_odd = bank[4], bank[5]
        att3 = bank[6:8]
        LOC = HC * SEG
        HALF = 2 * HC * KH

        IN = {k: in3[n % 2] for n, k in enumerate(["q0", "k0", "v0", "q1", "k1", "out", "v1", "xn"])}
        TURN = {k: turn3[n % 2] for n, k in enumerate(["p1a", "p1b", "pp1", "q0", "k0", "q1", "k1", "p0a", "p0b", "pp0"])}

        def self_sync(sp):
            def step(b, has):
                if has(1):
                    n = b + 1
                    sp.wait_ge(fy_stored, (n.pair + (fy_before["F2"] + 1)) * 16)
                    if (n + -2).exists:
                        sp.wait_ge(y3_made.sem(n + -2), y3_made.count(ph3, n + -2))
                    sp.dma_start(x_s[n.par][:], at(source[ph3], n).rearrange("b t d -> (b t) d")).then_inc(x3_loaded.sem(n), 16)
                    if (n + -2).exists:
                        sp.wait_ge(att3_made.sem(n + -2), att3_made.count(ph3, n + -2, 1))
                    mem = at(vmem_dram, n).rearrange("b (g k d) -> (b k) g d", k=4, d=KH)
                    for k in range(4):
                        sp.dma_start(vpre_s[n.par][PRE * k:PRE * k + NM, :, k, :],
                                     mem[k:k + 1].to_broadcast([NM, H // 4, KH])).then_inc(vpre_loaded.sem(n), 16)
                if has(-1):
                    if (b + -1).exists:
                        sp.wait_ge(y3_made.sem(b + -1), y3_made.count(ph3, b + -1))
                    sp.dma_start(at(target[ph3], b + -1).rearrange("b t d -> (b t) d"), y_s[(b + -1).par][:]).then_inc(y3_stored.sem(b + -1), 16)
            drive(sp, NB, step)

        def self_tensor(pe):
            made = {"q": q3_made, "k": k3_made, "v": v3_made}

            def project(b, what, h):
                col = "qkv".index(what) * HD3 + h * HALF
                if (what, h) == ("q", 0):
                    pe.wait_ge(xnT_kept.sem(b), xnT_kept.count(ph3, b))
                if (what, h) == ("q", 0):
                    if (b + -1).exists:
                        pe.wait_ge(v3_kept.sem(b + -1), v3_kept.count(ph3, b + -1, 1))
                elif (what, h) == ("v", 0):
                    pe.wait_ge(q3_roped.sem(b), q3_roped.count(ph3, b, 0))
                elif (what, h) == ("q", 1):
                    pe.wait_ge(k3_roped.sem(b), k3_roped.count(ph3, b, 0))
                elif (what, h) == ("k", 1):
                    pe.wait_ge(v3_kept.sem(b), v3_kept.count(ph3, b, 0))
                elif (what, h) == ("v", 1):
                    pe.wait_ge(k3_roped.sem(b), k3_roped.count(ph3, b, 1))
                nc.tensor.matmul(IN[f"{what}{h}"][:], xnT_s[b.par][:], wqkv[:, col:col + HALF], start=True, stop=True)\
                    .then_inc(made[what].sem(b), 1)

            def turn(b, what, h):
                src_done, dst_done = (q3_turned, qT3_made) if what == "q" else (k3_turned, kT3_made)
                pe.wait_ge(src_done.sem(b), src_done.count(ph3, b, h))
                if (what, h) == ("q", 0):
                    if (b + -1).exists:
                        pe.wait_ge(pT3_kept.sem(b + -1), pT3_kept.count(ph3, b + -1, 4))
                elif (what, h) == ("k", 0):
                    if (b + -1).exists:
                        pe.wait_ge(pT3_kept.sem(b + -1), pT3_kept.count(ph3, b + -1, 5))
                elif what == "q":
                    pe.wait_ge(qT3_kept.sem(b), qT3_kept.count(ph3, b, 0))
                else:
                    pe.wait_ge(kT3_kept.sem(b), kT3_kept.count(ph3, b, 0))
                for c in range(HC):
                    mm = nc.tensor.transpose(TURN[f"{what}{h}"][:, c * T:(c + 1) * T], turned[what][h][:, c * 128:(c + 1) * 128], ident[:])
                mm.then_inc(dst_done.sem(b), 1)

            def scores(b, h):
                pe.wait_ge(qT3_kept.sem(b), qT3_kept.count(ph3, b, h))
                pe.wait_ge(kT3_kept.sem(b), kT3_kept.count(ph3, b, h))
                if h == 0:
                    pe.wait_ge(kpre_made.sem(b), kpre_made.count(ph3, b))
                old = b if h else b + -1
                if old.exists:
                    pe.wait_ge(shifted3.sem(old), shifted3.count(ph3, old, 1 - h))
                qT, kT = turnedT["q"][h], turnedT["k"][h]
                for s_bank in (s_even, s_odd):
                    nc.tensor.matmul(s_bank[:, 0:LOC], identb[:], tri[:], start=True, stop=False, skip_group_check=True)
                for c in range(HC):
                    nc.tensor.matmul(s_even[:, LOC + c * 2 * PRE:LOC + (c + 1) * 2 * PRE], qT[:, c * T:(c + 1) * T],
                                     kpre_s[b.par][:, h * HC + c, :], start=False, stop=False, skip_group_check=True)
                for c in range(HC):
                    for r, s_bank in enumerate((s_even, s_odd)):
                        rows = slice(r * KH, (r + 1) * KH)
                        for g in range(T // SEG):
                            own = slice(c * T + g * SEG, c * T + (g + 1) * SEG)
                            mm = nc.tensor.matmul(s_bank[g * SEG:(g + 1) * SEG, c * SEG:(c + 1) * SEG], qT[rows, own], kT[rows, own],
                                                  start=False, stop=(c == HC - 1), skip_group_check=True)
                mm.then_inc(s3_made.sem(b), 1)

            def transpose_p(b, h):
                pe.wait_ge(p3_made.sem(b), p3_made.count(ph3, b, h))
                for r in range(2):
                    if h:
                        pe.wait_ge(pT3_kept.sem(b), pT3_kept.count(ph3, b, 1 + r))
                    else:
                        done = (qT3_kept, kT3_kept)[r]
                        pe.wait_ge(done.sem(b), done.count(ph3, b, 1))
                    for c in range(HC):
                        n = r * HC + c
                        mm = nc.tensor.transpose(TURN[f"p{h}{'ab'[r]}"][:, c * T:(c + 1) * T], dense_s[h][:, n * T:(n + 1) * T], ident[:])
                    mm.then_inc(pT3_made.sem(b), 1)
                pe.wait_ge(pT3_kept.sem(b), pT3_kept.count(ph3, b, 3 * h))
                for n in range(2):
                    mm = nc.tensor.transpose(TURN[f"pp{h}"][:, n * T:(n + 1) * T], pp_s[h][:, n * 128:(n + 1) * 128], ident[:])
                mm.then_inc(pT3_made.sem(b), 1)

            def attend(b, h):
                pe.wait_ge(pT3_kept.sem(b), pT3_kept.count(ph3, b, 3 * h + 2))
                pe.wait_ge(v3_kept.sem(b), v3_kept.count(ph3, b, h))
                if h == 0:
                    pe.wait_ge(vpre_loaded.sem(b), vpre_loaded.count(ph3, b))
                if (b + -1).exists:
                    pe.wait_ge(att3_kept.sem(b + -1), att3_kept.count(ph3, b + -1, h))
                for c in range(HC):
                    for r in range(2):
                        dst = att3[h][r * KH:(r + 1) * KH, c * T:(c + 1) * T]
                        n = r * HC + c
                        nc.tensor.matmul(dst, v3_s[h][:, (2 * c + r) * KH:(2 * c + r + 1) * KH], denseT_s[h][:, n * T:(n + 1) * T],
                                         start=True, stop=False)
                        mm = nc.tensor.matmul(dst, vpre_s[b.par][:, 2 * h + c // 2, (2 * c + r) % 4, :], ppT_s[h][:, (c // 2) * T:(c // 2 + 1) * T],
                                              start=False, stop=True)
                mm.then_inc(att3_made.sem(b), 1)

            def project_out(b):
                pe.wait_ge(att3_kept.sem(b), att3_kept.count(ph3, b, 1))
                for c in range(H // 2):
                    mm = nc.tensor.matmul(IN["out"][:, 0:D], att3_s[c // HC][:, (c % HC) * T:(c % HC + 1) * T], wout3[:, c, :],
                                          start=(c == 0), stop=(c == H // 2 - 1))
                mm.then_inc(proj3_made.sem(b), 1)

            def transpose_x(b):
                pe.wait_ge(xn_made.sem(b), xn_made.count(ph3, b))
                if (b + -2).exists:
                    pe.wait_ge(y3_made.sem(b + -2), y3_made.count(ph3, b + -2))
                nc.tensor.transpose(IN["xn"][:, 0:T], xn_s[b.par][:], ident[:]).then_inc(xnT_made.sem(b), 1)

            def step(b, has):
                if has(0):
                    project(b, "q", 0)
                    project(b, "k", 0)
                    project(b, "v", 0)
                if has(-1):
                    transpose_p(b + -1, 1)
                if has(0):
                    turn(b, "q", 0)
                    turn(b, "k", 0)
                    project(b, "q", 1)
                    project(b, "k", 1)
                if has(-1):
                    attend(b + -1, 1)
                if has(0):
                    scores(b, 0)
                if has(-1):
                    if has(0):
                        pe.wait_ge(q3_roped.sem(b), q3_roped.count(ph3, b, 1))
                    project_out(b + -1)
                if has(0):
                    project(b, "v", 1)
                    turn(b, "q", 1)
                    turn(b, "k", 1)
                if has(0):
                    scores(b, 1)
                    transpose_p(b, 0)
                    attend(b, 0)
                if has(1):
                    transpose_x(b + 1)
            drive(pe, NB, step)

        def self_scalar(act):
            def keep_v(b, h):
                act.wait_ge(v3_made.sem(b), v3_made.count(ph3, b, h))
                if (b + -1).exists:
                    act.wait_ge(att3_made.sem(b + -1), att3_made.count(ph3, b + -1, h))
                nc.scalar.activation(v3_s[h][:], IN[f"v{h}"][:], ACT.Copy).then_inc(v3_kept.sem(b), 1)

            def keep_turned(b, h):
                for what, done, kept in (("q", qT3_made, qT3_kept), ("k", kT3_made, kT3_kept)):
                    act.wait_ge(done.sem(b), done.count(ph3, b, h))
                    if (b + -1).exists:
                        act.wait_ge(s3_made.sem(b + -1), s3_made.count(ph3, b + -1, h))
                    nc.scalar.activation(turnedT[what][h][:], TURN[f"{what}{h}"][:], ACT.Copy).then_inc(kept.sem(b), 1)

            def keep_p(b, h):
                if (b + -1).exists:
                    act.wait_ge(att3_made.sem(b + -1), att3_made.count(ph3, b + -1, h))
                for r in range(2):
                    act.wait_ge(pT3_made.sem(b), pT3_made.count(ph3, b, 3 * h + r))
                    nc.scalar.activation(denseT_s[h][:, r * HC * T:(r + 1) * HC * T], TURN[f"p{h}{'ab'[r]}"][:], ACT.Copy)\
                        .then_inc(pT3_kept.sem(b), 1)
                act.wait_ge(pT3_made.sem(b), pT3_made.count(ph3, b, 3 * h + 2))
                nc.scalar.activation(ppT_s[h][:], TURN[f"pp{h}"][:, 0:2 * T], ACT.Copy).then_inc(pT3_kept.sem(b), 1)

            def keep_att(b, h):
                act.wait_ge(att3_made.sem(b), att3_made.count(ph3, b, h))
                if (b + -1).exists:
                    act.wait_ge(proj3_made.sem(b + -1), proj3_made.count(ph3, b + -1))
                nc.scalar.activation(att3_s[h][:], att3[h][:], ACT.Copy).then_inc(att3_kept.sem(b), 1)

            def exps(b, h):
                act.wait_ge(shifted3.sem(b), shifted3.count(ph3, b, h))
                nc.scalar.activation(l_s[h][:], l_s[h][:], ACT.Exp, scale=KH ** -0.5)
                nc.scalar.activation(lp_s[h][:], lp_s[h][:], ACT.Exp, scale=KH ** -0.5).then_inc(exp3_made.sem(b), 1)

            def keep_xT(b):
                act.wait_ge(xnT_made.sem(b), xnT_made.count(ph3, b))
                if (b + -2).exists:
                    act.wait_ge(v3_made.sem(b + -2), v3_made.count(ph3, b + -2, 1))
                nc.scalar.activation(xnT_s[b.par][:], IN["xn"][:, 0:T], ACT.Copy).then_inc(xnT_kept.sem(b), 1)

            def step(b, has):
                if has(0):
                    keep_v(b, 0)
                if has(-1):
                    keep_p(b + -1, 1)
                if has(0):
                    keep_turned(b, 0)
                if has(-1):
                    keep_att(b + -1, 1)
                if has(0):
                    exps(b, 0)
                    keep_v(b, 1)
                    keep_turned(b, 1)
                if has(0):
                    keep_p(b, 0)
                    exps(b, 1)
                    keep_att(b, 0)
                if has(1):
                    keep_xT(b + 1)
            drive(act, NB, step)

        def by_half(ap, w):
            return ap.rearrange("p (n k) -> p n k", k=w)

        def swap_order(ap):
            return ap.rearrange("p (c r) -> p r c", r=2)

        def self_vector(dve):
            def rope(b, what, h):
                done, roped = (q3_made, q3_roped) if what == "q" else (k3_made, k3_roped)
                dve.wait_ge(done.sem(b), done.count(ph3, b, h))
                done = q3_turned if what == "q" else k3_turned
                if (b + -1).exists:
                    dve.wait_ge(done.sem(b + -1), done.count(ph3, b + -1, h))
                src = IN[f"{what}{h}"][:]
                nc.vector.tensor_tensor(by_half(ropeC[what][h][:], KH), by_half(src, KH),
                                        cos[:].unsqueeze(1).to_broadcast([T, 2 * HC, KH]), ALU.mult)
                pairs = src.rearrange("p (n f two) -> p n f two", two=2, f=KH // 2)
                swapped = ropeS[what][h][:].rearrange("p (n f two) -> p n f two", two=2, f=KH // 2)
                factor = sin[:].rearrange("p (f two) -> p f two", two=2)
                for k in range(2):
                    ins = nc.vector.tensor_tensor(swapped[:, :, :, k], pairs[:, :, :, 1 - k],
                                                  factor[:, :, k].unsqueeze(1).to_broadcast([T, 2 * HC, KH // 2]), ALU.mult)
                ins.then_inc(roped.sem(b), 1)

            def shift(b, h):
                dve.wait_ge(s3_made.sem(b), s3_made.count(ph3, b, h))
                for r, s_bank in enumerate((s_even, s_odd)):
                    nc.vector.tensor_reduce(m_loc[h][:, r * HC:(r + 1) * HC], by_half(s_bank[:, 0:LOC], SEG), AX.X, ALU.max)
                prefix = s_even[:, LOC:LOC + 2 * HC * PRE]
                nc.vector.tensor_reduce(m_pre[h][:], by_half(prefix, PRE), AX.X, ALU.max).then_inc(max3_parts.sem(b), 1)
                dve.wait_ge(max3_parts.sem(b), max3_parts.count(ph3, b, h))
                nc.vector.tensor_tensor(m_all[h][:].rearrange("p (r c) -> p r c", r=2), m_loc[h][:].rearrange("p (r c) -> p r c", r=2),
                                        swap_order(m_pre[h][:]), ALU.max).then_inc(max3_made.sem(b), 1)
                dve.wait_ge(max3_made.sem(b), max3_made.count(ph3, b, h))
                if (b + -1).exists:
                    dve.wait_ge(p3_made.sem(b + -1), p3_made.count(ph3, b + -1, h))
                for r, s_bank in enumerate((s_even, s_odd)):
                    nc.vector.tensor_tensor(by_half(l_s[h][:, r * LOC:(r + 1) * LOC], SEG), by_half(s_bank[:, 0:LOC], SEG),
                                            spread(m_all[h][:, r * HC:(r + 1) * HC], SEG), ALU.subtract)
                for r in range(2):
                    pre_r = lambda ap: ap.rearrange("p (c r k) -> p r c k", r=2, k=PRE)[:, r]
                    ins = nc.vector.tensor_tensor(pre_r(lp_s[h][:]), pre_r(prefix), spread(m_all[h][:, r * HC:(r + 1) * HC], PRE), ALU.subtract)
                ins.then_inc(shifted3.sem(b), 1)

            def denominators(b, h):
                dve.wait_ge(exp3_made.sem(b), exp3_made.count(ph3, b, h))
                nc.vector.tensor_reduce(d_loc[h][:], by_half(l_s[h][:], SEG), AX.X, ALU.add)
                nc.vector.tensor_reduce(d_pre[h][:], by_half(lp_s[h][:], PRE), AX.X, ALU.add).then_inc(den3_parts.sem(b), 1)
                dve.wait_ge(den3_parts.sem(b), den3_parts.count(ph3, b, h))
                nc.vector.tensor_tensor(d_all[h][:].rearrange("p (r c) -> p r c", r=2), d_loc[h][:].rearrange("p (r c) -> p r c", r=2),
                                        swap_order(d_pre[h][:]), ALU.add).then_inc(den3_sum.sem(b), 1)
                dve.wait_ge(den3_sum.sem(b), den3_sum.count(ph3, b, h))
                if (b + -1).exists:
                    dve.wait_ge(p3_made.sem(b + -1), p3_made.count(ph3, b + -1, h))
                nc.vector.reciprocal(r_all[h][:], d_all[h][:]).then_inc(den3_inv.sem(b), 1)

            def squares(b):
                dve.wait_ge(x3_loaded.sem(b), x3_loaded.count(ph3, b))
                if (b + -2).exists:
                    dve.wait_ge(rms_made.sem(b + -2), rms_made.count(ph3, b + -2))
                nc.vector.tensor_tensor_reduce(sq_s[b.par][:], x_s[b.par][:], x_s[b.par][:], 1.0 / D, RMS_EPS, ALU.mult, ALU.add,
                                               var_s[b.par][:]).then_inc(sq_made.sem(b), 1)

            def norm(b):
                dve.wait_ge(rms_made.sem(b), rms_made.count(ph3, b))
                if (b + -2).exists:
                    dve.wait_ge(xnT_made.sem(b + -2), xnT_made.count(ph3, b + -2))
                nc.vector.tensor_scalar(xn_s[b.par][:], x_s[b.par][:], rstd_s[b.par][:, 0:1], None, ALU.mult).then_inc(xn_made.sem(b), 1)

            def residual(b):
                dve.wait_ge(proj3_made.sem(b), proj3_made.count(ph3, b))
                if (b + -2).exists:
                    dve.wait_ge(y3_stored.sem(b + -2), y3_stored.count(ph3, b + -2))
                nc.vector.tensor_tensor(y_s[b.par][:], IN["out"][:, 0:D], x_s[b.par][:], ALU.add).then_inc(y3_made.sem(b), 1)

            def step(b, has):
                if has(-1):
                    denominators(b + -1, 1)
                if has(0):
                    rope(b, "q", 0)
                    rope(b, "k", 0)
                    rope(b, "q", 1)
                    rope(b, "k", 1)
                    shift(b, 0)
                if has(-1):
                    residual(b + -1)
                if has(0):
                    denominators(b, 0)
                if has(1):
                    squares(b + 1)
                if has(0):
                    shift(b, 1)
                if has(1):
                    norm(b + 1)
            drive(dve, NB, step)

        def self_gpsimd(pool):
            def add_up(b, what, h):
                roped, done, used = (q3_roped, q3_turned, qT3_made) if what == "q" else (k3_roped, k3_turned, kT3_made)
                pool.wait_ge(roped.sem(b), roped.count(ph3, b, h))
                if (b + -1).exists:
                    pool.wait_ge(used.sem(b + -1), used.count(ph3, b + -1, h))
                nc.gpsimd.tensor_tensor(turned[what][h][:], ropeC[what][h][:], ropeS[what][h][:], ALU.add).then_inc(done.sem(b), 1)

            def normalise(b, h):
                pool.wait_ge(den3_inv.sem(b), den3_inv.count(ph3, b, h))
                if (b + -1).exists:
                    pool.wait_ge(pT3_made.sem(b + -1), pT3_made.count(ph3, b + -1, 3 * h + 2))
                for g in range(T // SEG):
                    rows = slice(g * SEG, (g + 1) * SEG)
                    nc.gpsimd.tensor_tensor(by_half(dense_s[h][rows, :], T)[:, :, g * SEG:(g + 1) * SEG], by_half(l_s[h][rows, :], SEG),
                                            spread(r_all[h][rows, :], SEG), ALU.mult).then_inc(p3_rows.sem(b), 1)
                    pool.wait_ge(p3_rows.sem(b), p3_rows.count(ph3, b, 2 * h + g))
                for r in range(2):
                    pre_r = lambda ap: ap.rearrange("p (c r k) -> p r c k", r=2, k=PRE)[:, r]
                    ins = nc.gpsimd.tensor_tensor(pre_r(pp_s[h][:]), pre_r(lp_s[h][:]), spread(r_all[h][:, r * HC:(r + 1) * HC], PRE), ALU.mult)
                ins.then_inc(p3_made.sem(b), 1)

            def rms(b):
                pool.wait_ge(sq_made.sem(b), sq_made.count(ph3, b))
                if (b + -2).exists:
                    pool.wait_ge(xn_made.sem(b + -2), xn_made.count(ph3, b + -2))
                nc.gpsimd.tensor_tensor(rstd_s[b.par][:], var_s[b.par][:], minus_half[:, 0:1], ALU.pow).then_inc(rms_made.sem(b), 1)

            def prefix_keys(b):
                if (b + -2).exists:
                    pool.wait_ge(s3_made.sem(b + -2), s3_made.count(ph3, b + -2, 1))
                mem = kmemT[:, :, bass.ds(b.pair * 2 + b.par, 1)].unsqueeze(2).to_broadcast([128, H // 2, 2, NM])
                own = halfmask[:].unsqueeze(1).unsqueeze(3).to_broadcast([128, H // 2, 2, NM])
                nc.gpsimd.tensor_tensor(kpre_s[b.par][:].rearrange("p c (r k) -> p c r k", r=2)[:, :, :, 0:NM], mem, own, ALU.mult)\
                    .then_inc(kpre_made.sem(b), 1)

            def step(b, has):
                if has(-1):
                    normalise(b + -1, 1)
                if has(0):
                    add_up(b, "q", 0)
                    add_up(b, "k", 0)
                if has(1):
                    prefix_keys(b + 1)
                if has(0):
                    add_up(b, "q", 1)
                    add_up(b, "k", 1)
                    normalise(b, 0)
                if has(1):
                    rms(b + 1)
            drive(pool, NB, step)

        with_self = "A3" in order
        pooled = slots("pooled", [NB, D], n=5)
        pool_var = slots("pool_var", [NB, 1], n=3)
        poolT = sb("poolT", [D, NB])
        memT = sb("memT", [D, NB])
        vmem_sb = sb("vmem", [NB, HD3])
        pool_step = sem("pool_step")
        mem_ctx_loaded = sem("mem_ctx_loaded")

        def memory_vector(dve):
            total, mean, square, normed, scaled = pooled
            dve.wait_ge(mem_ctx_loaded, 16)
            nc.vector.tensor_reduce(total[:], ctx_all[:].rearrange("b (k d) -> b d k", d=D), AX.X, ALU.add).then_inc(pool_step, 1)
            dve.wait_ge(pool_step, 1)
            nc.vector.tensor_scalar(mean[:], total[:], 1.0 / C, None, ALU.mult).then_inc(pool_step, 1)
            dve.wait_ge(pool_step, 2)
            nc.vector.tensor_tensor_reduce(square[:], mean[:], mean[:], 1.0, 0.0, ALU.mult, ALU.add, pool_var[0][:]).then_inc(pool_step, 1)
            dve.wait_ge(pool_step, 5)
            nc.vector.tensor_scalar(normed[:], mean[:], pool_var[2][:, 0:1], None, ALU.mult).then_inc(pool_step, 1)
            dve.wait_ge(pool_step, 6)
            nc.vector.tensor_tensor(scaled[:], normed[:], pool_norm[0:NB, :], ALU.mult).then_inc(pool_step, 1)
            dve.wait_ge(mem_kv, 1)
            nc.vector.tensor_scalar(wqkv[:], wqkv[:], attn_norm[:, 0:1], None, ALU.mult).then_inc(weights_scaled, 1)
            nc.vector.tensor_scalar(w1g[:], w1g[:], ff_norm[:, 0:1], None, ALU.mult).then_inc(weights_scaled, 1)
            dve.wait_ge(weights_scaled, 2)

        def memory_gpsimd(pool):
            pool.wait_ge(pool_step, 3)
            nc.gpsimd.tensor_scalar(pool_var[1][:], pool_var[0][:], 1.0 / D, RMS_EPS, ALU.mult, ALU.add).then_inc(pool_step, 1)
            pool.wait_ge(pool_step, 4)
            nc.gpsimd.tensor_tensor(pool_var[2][:], pool_var[1][:], minus_half[0:NB, 0:1], ALU.pow).then_inc(pool_step, 1)

        def memory_tensor(pe):
            pe.wait_ge(pool_step, 7)
            nc.tensor.transpose(bank[0][:, 0:NB], pooled[4][:], ident[0:NB, 0:NB]).then_inc(mem_poolT, 1)
            pe.wait_ge(mem_poolT_kept, 1)
            nc.tensor.matmul(bank[1][:, 0:NB], wmem[:], poolT[:], start=True, stop=True).then_inc(mem_tok, 1)
            pe.wait_ge(mem_tok_kept, 1)
            for c in range(H // 2):
                nc.tensor.matmul(bank[2][:, c * NB:(c + 1) * NB], wqkv[:, HD3 + c * 128:HD3 + (c + 1) * 128], memT[:], start=True, stop=True)
            for n in range(2):
                mm = nc.tensor.matmul(bank[3 + n][0:NB, :], memT[:], wqkv[:, 2 * HD3 + n * 512:2 * HD3 + (n + 1) * 512], start=True, stop=True)
            mm.then_inc(mem_kv, 1)
            pe.wait_ge(mem_kv_kept, 3)
            pe.wait_ge(weights_scaled, 2)

        def memory_scalar(act):
            act.wait_ge(mem_poolT, 1)
            nc.scalar.activation(poolT[:], bank[0][:, 0:NB], ACT.Copy).then_inc(mem_poolT_kept, 1)
            act.wait_ge(mem_tok, 1)
            nc.scalar.activation(memT[:], bank[1][:, 0:NB], ACT.Copy).then_inc(mem_tok_kept, 1)
            act.wait_ge(mem_kv, 1)
            nc.scalar.activation(kmemT[:].rearrange("p c b -> p (c b)"), bank[2][:, 0:H // 2 * NB], ACT.Copy).then_inc(mem_kv_kept, 1)
            for n in range(2):
                nc.scalar.activation(vmem_sb[:, n * 512:(n + 1) * 512], bank[3 + n][0:NB, :], ACT.Copy).then_inc(mem_kv_kept, 1)

        def memory_sync(sp):
            sp.wait_ge(mem_kv_kept, 3)
            sp.dma_start(vmem_dram, vmem_sb[:]).then_inc(mem_stored, 16)
            sp.wait_ge(mem_stored, 16)

        def phases(eng, by_cross, by_ff, by_self):
            for ph in order:
                if ph in cross:
                    by_cross(eng, ph)
                elif ph[0] == "F":
                    by_ff(eng, ph)
                else:
                    by_self(eng)

        block = ctx.enter_context(nc.Block())

        N_ZERO = 11

        @block.sync
        def _(sp):
            sp.dma_start(ctx_all[:], a["ctx"]).then_inc(mem_ctx_loaded, 16)
            for dst, src in consts:
                sp.dma_start(dst[:], src).then_inc(loaded, 16)
            sp.wait_ge(zeroed, N_ZERO)
            for s in range(2):
                for r in range(2):
                    sp.dma_start(kpre_s[s][r * KH:(r + 1) * KH, :, r * PRE + NM:(r + 1) * PRE], a["persistT"][r]).then_inc(loaded, 16)
                for k in range(4):
                    sp.dma_start(vpre_s[s][PRE * k + NM:PRE * (k + 1), :, k, :], a["persist"][k]).then_inc(loaded, 16)
            memory_sync(sp)
            phases(sp, cross_sync, ff_sync, self_sync)
            for slot in range(2):
                sp.wait_ge(y_stored.sems[slot], y_stored.total_count)
                sp.wait_ge(y3_stored.sems[slot], y3_stored.total_count)
            sp.wait_ge(fy_stored, 16 * GROUPS * len(FFS))

        @block.tensor
        def _(pe):
            pe.wait_ge(loaded, 16 * N_LOADS)
            pe.wait_ge(zeroed, N_ZERO)
            pe.wait_ge(masks_made, 3)
            memory_tensor(pe)
            phases(pe, cross_tensor, ff_tensor, self_tensor)

        @block.scalar
        def _(act):
            act.wait_ge(loaded, 16 * N_LOADS)
            memory_scalar(act)
            phases(act, cross_scalar, ff_scalar, self_scalar)

        @block.vector
        def _(dve):
            for s in range(2):
                nc.vector.memset(v_s[s][:], 0.0).then_inc(setup, 1)
                nc.vector.memset(dense_s[s][:], 0.0).then_inc(zeroed, 1)
                nc.vector.memset(kpre_s[s][:], 0.0).then_inc(zeroed, 1)
                nc.vector.memset(vpre_s[s][:], 0.0).then_inc(zeroed, 1)
            dve.wait_ge(setup, 2)
            for s in range(2):
                nc.vector.memset(v_s[s][:].rearrange("p (h v) -> p h v", v=VP)[:, :, DH:DH + 1], 1.0).then_inc(zeroed, 1)
            nc.vector.memset(onesb[:], 1.0).then_inc(zeroed, 1)
            nc.vector.memset(minus_half[:], -0.5).then_inc(zeroed, 1)
            nc.vector.memset(ln_eps[:], LN_EPS).then_inc(zeroed, 1)
            dve.wait_ge(loaded, 16 * N_LOADS)
            dve.wait_ge(zeroed, N_ZERO)
            nc.vector.tensor_copy(identb[:], ident[:]).then_inc(masks_made, 1)
            nc.vector.tensor_copy(causal[:], causal32).then_inc(masks_made, 1)
            nc.vector.tensor_copy(tri[:], tri32).then_inc(masks_made, 1)
            memory_vector(dve)
            phases(dve, cross_vector, ff_vector, self_vector)

        @block.gpsimd
        def _(pool):
            pool.wait_ge(loaded, 16 * N_LOADS)
            pool.wait_ge(zeroed, N_ZERO)
            memory_gpsimd(pool)
            phases(pool, cross_gpsimd, ff_gpsimd, self_gpsimd)


def lay_out(i):
    f = lambda x: np.ascontiguousarray(np.asarray(x))
    NB = i["x"].shape[0]
    a = {"x": f(i["x"]), "ctx": f(i["ctx_1024"]).reshape(NB, C * D)}
    a["ctxT"] = f(np.transpose(i["ctx_1024"], (0, 2, 1)))
    a["side"] = f(np.transpose(i["fside_Bx16xSxS2_0"], (0, 2, 1, 3))).reshape(NB, T, H * C)
    a["mask"] = f(np.transpose(i["mask_Bx16xSxS2_bk0"], (0, 2, 1, 3))).reshape(NB, T, H * C)
    a["keymask"] = f(i["mask_Bx1x1xS2_if1"]).reshape(NB, C)
    for p in ("L0_xattn_", "L1_xattn_"):
        for k in "qkv":
            a[f"{p}w{k}"] = f(np.transpose(i[f"{p}W{k}"]))
            a[f"{p}b{k}"] = f(i[f"{p}b{k}"])
    p = "L0_xattn_"
    a[p + "ln_g"], a[p + "ln_b"] = f(i[p + "ln_g"]), f(i[p + "ln_b"])
    a[p + "ffw1"] = f(np.transpose(i[p + "W1"]))
    a[p + "ffb1"] = f(np.transpose(np.reshape(i[p + "b1"], (NF, 128))))
    a[p + "ffw2"] = f(np.transpose(np.reshape(np.transpose(i[p + "W2"]), (NF, 128, D)), (1, 0, 2)))
    a[p + "ffb2"] = f(i[p + "b2"])
    p = "L1_xattn_"
    a[p + "wo"], a[p + "bo"] = f(np.transpose(i[p + "Wo"])), f(i[p + "bo"])
    a[p + "ln_g"], a[p + "ln_b"] = f(i[p + "gamma"]), f(i[p + "beta"])
    p = "L2_xattn_"
    for k in "qkv":
        w = np.zeros((D, D), np.float32)
        for h in range(H):
            w[h * DH:(h + 1) * DH, h * DH:(h + 1) * DH] = i[f"{p}w{k}"]
        a[f"{p}w{k}"] = w
    a[p + "wo"], a[p + "bo"] = f(i[p + "w_out"]), f(i[p + "b_out"])
    a[p + "ln_g"], a[p + "ln_b"] = f(i[p + "g1"]), f(i[p + "beta1"])
    a[p + "ffw1"] = f(i[p + "w_ff1"])
    a[p + "ffb1"] = f(np.transpose(np.reshape(i[p + "b_ff1"], (NF, 128))))
    a[p + "ffw2"] = f(np.transpose(np.reshape(i[p + "w_ff2"], (NF, 128, D)), (1, 0, 2)))
    a[p + "ffb2"] = f(i[p + "b_ff2"])
    a[p + "g2"], a[p + "beta2"] = f(i[p + "g2"]), f(i[p + "beta2"])
    p = "L3_xattn_"
    for k in ("attn_norm_w", "to_qkv_w", "to_out_w", "mem_pool_norm_w", "to_mem_tokens_w", "ff_norm_w", "ff_b2"):
        a[p + k] = f(i[p + k])
    w1, b1, w2 = (np.asarray(i[p + k]) for k in ("ff_w1", "ff_b1", "ff_w2"))
    pw1 = np.zeros((D, 2, NG * 128), np.float32)
    pw1[:, 0, :DG], pw1[:, 1, :DG] = w1[:, :DG], w1[:, DG:]
    a[p + "ffw1"] = pw1.reshape(D, 2 * NG * 128)
    pb1 = np.zeros((2, NG * 128), np.float32)
    pb1[0, :DG], pb1[1, :DG] = b1[:DG], b1[DG:]
    a[p + "ffb1"] = f(np.transpose(pb1.reshape(2 * NG, 128)))
    pw2 = np.zeros((NG * 128, D), np.float32)
    pw2[:DG] = w2
    a[p + "ffw2"] = f(np.transpose(pw2.reshape(NG, 128, D), (1, 0, 2)))
    pm = np.asarray(i[p + "persist_mem"])
    a["persistT"] = f(np.transpose(pm.reshape(H // 2, 2, NPM, KH), (1, 3, 0, 2)))
    a["persist"] = f(np.transpose(pm.reshape(H // 4, 4, NPM, KH), (1, 2, 0, 3)))

    a["c_ident"] = np.eye(128, dtype=np.float32)
    later = np.arange(C)[None, :] > np.arange(T)[:, None]
    a["c_causal"] = np.tile(np.where(later, -1.0e9, 0.0), (1, QH)).astype(np.float32)
    later = np.arange(SEG)[None, :] > (np.arange(T) % SEG)[:, None]
    a["c_tri"] = np.tile(np.where(later, -1.0e30, 0.0), (1, HC)).astype(np.float32)
    a["c_headmask"] = (np.arange(D)[:, None] // DH == np.arange(H)[None, :]).astype(np.float32)
    a["c_halfmask"] = (np.arange(128)[:, None] // KH == np.arange(2)[None, :]).astype(np.float32)
    inv = (np.float32(1.0) / np.float32(10000.0) ** (np.arange(0, KH, 2, dtype=np.float32) / np.float32(KH))).astype(np.float32)
    angle = np.repeat(np.arange(T, dtype=np.float32)[:, None] * inv[None, :], 2, axis=-1)
    a["c_cos"] = np.cos(angle).astype(np.float32)
    a["c_sin"] = (np.sin(angle) * np.tile([-1.0, 1.0], KH // 2)[None, :]).astype(np.float32)
    return a


def kernel(**inputs):
    import concourse.bacc as bacc
    from concourse.bass_utils import run_bass_kernel_spmd

    nc = bacc.Bacc("TRN2", target_bir_lowering=False, num_devices=1)
    arrays = {"in_" + k: v for k, v in lay_out(inputs).items()}
    aps = {k[3:]: nc.dram_tensor(k, v.shape, mybir.dt.from_np(v.dtype), kind="ExternalInput").ap() for k, v in arrays.items()}
    out = nc.dram_tensor("out", inputs["x"].shape, F32, kind="ExternalOutput").ap()
    build_layers(nc, aps, out)
    return run_bass_kernel_spmd(nc, [arrays], core_ids=[0]).results[0]["out"]
```

```python
from contextlib import ExitStack
from dataclasses import dataclass

import numpy as np

import concourse.bass as bass
from concourse import mybir

F32 = mybir.dt.float32
BF16 = mybir.dt.bfloat16
I32 = mybir.dt.int32
U8 = mybir.dt.uint8
ACT = mybir.ActivationFunctionType
ALU = mybir.AluOpType
AX = mybir.AxisListType

T = 128
D = 128
C = 77
H = 16
DH = D // H
QH = 4
NQ = H // QH
QC = QH * C
VP = 32
FF = 512
NF = FF // 128
GB = 2
DG = 341
NG = 3
KH = 64
HD3 = H * KH
SEG = 64
NM = 16
NPM = 16
PRE = NM + NPM
HC = 4
LN_EPS = 1e-5
RMS_EPS = 1.1920929e-07
MASKED = -3.0e38


@dataclass(frozen=True)
class Batch:

    pair: object
    par: int

    @property
    def exists(self):
        return not isinstance(self.pair, int) or self.pair >= 0

    @property
    def first(self):
        return isinstance(self.pair, int) and (self.pair, self.par) == (0, 0)

    def __add__(self, k):
        p = self.par + k
        return Batch(self.pair + p // 2 if p // 2 else self.pair, p % 2)


class Event:

    def __init__(self, new_semaphore, name, phases, parts=1, transfers=0):
        self.parts, self.transfers = parts, transfers
        self.sems = [new_semaphore(f"{name}_{s}") for s in range(2)] if transfers else [new_semaphore(name)]
        self.before, self.total = {}, 0
        for phase, batches in phases:
            self.before[phase] = self.total
            self.total += batches

    def sem(self, b):
        return self.sems[b.par if self.transfers else 0]

    def count(self, phase, b, part=0):
        before = self.before[phase]
        if self.transfers:
            return (b.pair + (before // 2 + 1)) * (16 * self.transfers)
        return b.pair * (2 * self.parts) + ((b.par + before) * self.parts + part + 1)

    @property
    def total_count(self):
        return self.total // 2 * 16 * self.transfers


def drive(eng, n, step, reach=1):
    lo, hi = 2 * reach, n - 2
    static = lambda t: step(Batch(t // 2, t % 2), lambda k: 0 <= t + k < n)
    for t in range(-reach, lo):
        static(t)
    with eng.Fori(lo // 2, hi // 2) as i:
        for par in range(2):
            step(Batch(i, par), lambda k: True)
    for t in range(hi, n + reach):
        static(t)


def at(ap, b, per=1):
    return ap[bass.ds((b.pair * 2 + b.par) * per, per)]


def build_layers(nc, a, out):
    NB = a["x"].shape[0]
    PAIRS = NB // 2
    GROUPS = NB // GB
    with ExitStack() as ctx:
        def sb(name, shape, dt=F32):
            return ctx.enter_context(nc.sbuf_tensor("sb_" + name, shape, dt))

        def slots(name, shape, dt=F32, n=2):
            return [sb(f"{name}{s}", shape, dt) for s in range(n)]

        def sem(name):
            return ctx.enter_context(nc.semaphore(name))

        def scratch(name, shape):
            return nc.dram_tensor("scratch_" + name, shape, F32, kind="Internal").ap()

        bank = [ctx.enter_context(nc.psum_tensor(f"bank{i}", [128, 512], F32)) for i in range(8)]

        order = ["A0", "F0", "A1", "A2", "F2", "A3", "F3"]
        source, target = {}, {}
        held = a["x"]
        for ph in order:
            source[ph] = held
            held = out if ph == order[-1] else scratch("after_" + ph, [NB, T, D])
            target[ph] = held
        vmem_dram = scratch("vmem", [NB, HD3])

        ident = sb("ident", [128, 128])
        identb = sb("identb", [128, 128], BF16)
        causal = sb("causal", [T, QC], BF16)
        tri = sb("tri", [T, HC * SEG], BF16)
        headmask = sb("headmask", [D, H])
        halfmask = sb("halfmask", [D, 2])
        cos = sb("cos", [T, KH])
        sin = sb("sin", [T, KH])
        onesb = sb("onesb", [1, T], BF16)
        minus_half = sb("minus_half", [128, GB])
        ln_eps = sb("ln_eps", [128, GB])
        consts = [(ident, a["c_ident"]), 
                  (headmask, a["c_headmask"]), (halfmask, a["c_halfmask"]), (cos, a["c_cos"]), (sin, a["c_sin"])]

        def weight(name, shape, src):
            w = sb(name, shape)
            consts.append((w, src))
            return w

        def row_everywhere(name):
            n = a[name].shape[0]
            return weight(name, [128, n], a[name].partition_broadcast(128))

        def column(name):
            return weight(name, [128, 1], a[name].rearrange("(p a) -> p a", a=1))

        cross = {}
        for ph, p in (("A0", "L0_xattn_"), ("A1", "L1_xattn_"), ("A2", "L2_xattn_")):
            w = {k: weight(p + k, [D, D], a[p + k]) for k in ("wq", "wk", "wv")}
            if ph != "A2":
                w |= {k: column(p + k) for k in ("bq", "bk")}
                w["bv"] = row_everywhere(p + "bv")
            if ph == "A0":
                w["bo"] = w["bv"]
            else:
                w["wo"] = weight(p + "wo", [D, D], a[p + "wo"])
                w["bo"] = row_everywhere(p + "bo")
            w |= {k: row_everywhere(p + k) for k in ("ln_g", "ln_b")}
            cross[ph] = w
        ffw = {}
        for ph, p in (("F0", "L0_xattn_"), ("F2", "L2_xattn_")):
            ffw[ph] = {
                "w1": weight(p + "ffw1", [D, FF], a[p + "ffw1"]),
                "b1": weight(p + "ffb1", [128, NF], a[p + "ffb1"]),
                "w2": weight(p + "ffw2", [128, NF, D], a[p + "ffw2"]),
                "b2": row_everywhere(p + "ffb2"),
            }
        ffw["F2"] |= {"g": row_everywhere("L2_xattn_g2"), "b": row_everywhere("L2_xattn_beta2")}
        p = "L3_xattn_"
        wqkv = weight("wqkv", [D, 3 * HD3], a[p + "to_qkv_w"])
        wout3 = weight("wout3", [128, H // 2, D], a[p + "to_out_w"].rearrange("(c p) d -> p c d", p=128))
        attn_norm = column(p + "attn_norm_w")
        ff_norm = column(p + "ff_norm_w")
        pool_norm = row_everywhere(p + "mem_pool_norm_w")
        wmem = weight("wmem", [D, D], a[p + "to_mem_tokens_w"])
        w1g = weight("w1g", [D, 2 * NG * 128], a[p + "ffw1"])
        b1g = weight("b1g", [128, 2 * NG], a[p + "ffb1"])
        w2g = weight("w2g", [128, NG, D], a[p + "ffw2"])
        b2g = row_everywhere(p + "ff_b2")

        REGION = C * D
        region = sb("region", [128, REGION])

        class Carve:

            def __init__(self):
                self.used = 0

            def __call__(self, rows, cols):
                view = region[0:rows, self.used:self.used + cols]
                self.used += cols
                assert self.used <= REGION
                return view

            def slots(self, rows, cols):
                return [self(rows, cols) for _ in range(2)]

        ctx_all = region[0:NB, 0:C * D]

        carve = Carve()
        x_s = slots("x", [T, D])
        ctx_s = slots("ctx", [D, C])
        side_s = carve.slots(T, H * C)
        mask_s = slots("mask", [T, H * C], U8)
        keymask_s = slots("keymask", [1, C], I32)
        keybias_s = slots("keybias", [1, C], BF16)
        xT_s = slots("xT", [D, T])
        qT_s = slots("qT", [D, T])
        kT_s = slots("kT", [D, C])
        kblk_s = carve.slots(D, H * C)
        v_s = slots("v", [C, H * VP])
        xb_s = slots("xb", [T, D])
        prod_s = carve.slots(T, QC)
        scored_s = carve.slots(T, QC)
        shifted_s = carve.slots(T, QC)
        p_s = carve.slots(T, QC)
        pT_s = slots("pT", [C, QH * T])
        max_s = slots("max", [T, QH])
        att_s = carve.slots(128, NQ * T)
        rden_s = slots("rden", [T, H])
        o_s = slots("o", [T, D])
        oT_s = slots("oT", [D, T])
        t_s = slots("t", [T, D])
        stats_s = slots("stats", [T, 6])
        mv_s = slots("mv", [T, 2])
        var_s = slots("var", [T, 1])
        rstd_s = slots("rstd", [T, 1])
        z_s = slots("z", [T, D])
        zg_s = slots("zg", [T, D])
        y_s = slots("y", [T, D])

        fx_s = slots("fx", [T, GB, D])
        fxT_s = slots("fxT", [D, GB * T])
        fh_s = slots("fh", [128, NF, GB * T])
        fg_s = fh_s
        fsilu_s = slots("fsilu", [128, NG, GB * T])
        fxb_s = slots("fxb", [T, GB, D])
        ft_s = slots("ft", [T, GB, D])
        fc_s = slots("fc", [T, GB, D])
        fz_s = slots("fz", [T, GB, D])
        fn_s = slots("fn", [T, GB, D])
        fy_s = slots("fy", [T, GB, D])
        fsq_s = slots("fsq", [T, D])
        fstats_s = slots("fstats", [T, GB, 6])
        fmv_s = slots("fmv", [T, GB, 2])
        fvar_s = slots("fvar", [T, GB])
        frstd_s = slots("frstd", [T, GB])

        kmemT = sb("kmemT", [128, H // 2, NB])
        carve = Carve()
        sq_s = slots("sq", [T, D])
        xn_s = slots("xn", [T, D])
        xnT_s = slots("xnT", [D, T])
        ropeC = {k: carve.slots(T, HC * 2 * KH) for k in "qk"}
        ropeS = {k: carve.slots(T, HC * 2 * KH) for k in "qk"}
        turned = {k: carve.slots(T, HC * 2 * KH) for k in "qk"}
        turnedT = {k: carve.slots(128, HC * T) for k in "qk"}
        v3_s = carve.slots(T, HC * 2 * KH)
        kpre_s = slots("kpre", [128, H // 2, 2 * PRE])
        vpre_s = slots("vpre", [128, H // 4, 4, KH])
        l_s = slots("l", [T, 2 * HC * SEG])
        lp_s = slots("lp", [T, 2 * HC * PRE])
        m_loc = slots("m_loc", [T, 2 * HC])
        m_pre = slots("m_pre", [T, 2 * HC])
        m_all = slots("m_all", [T, 2 * HC])
        d_loc = slots("d_loc", [T, 2 * HC])
        d_pre = slots("d_pre", [T, 2 * HC])
        d_all = slots("d_all", [T, 2 * HC])
        r_all = slots("r_all", [T, 2 * HC])
        dense_s = slots("dense", [T, 2 * HC * T])
        pp_s = slots("pp", [T, 2 * HC * PRE])
        denseT_s = slots("denseT", [T, 2 * HC * T])
        causal32, tri32 = denseT_s[0][:, 0:QC], denseT_s[1][:, 0:HC * SEG]
        consts += [(causal32, a["c_causal"]), (tri32, a["c_tri"])]
        ppT_s = slots("ppT", [128, 2 * T])
        att3_s = slots("att3", [128, HC * T])

        loaded = sem("loaded")
        masks_made = sem("masks_made")
        setup = sem("setup_chain")
        mem_pooled = sem("mem_pooled")
        mem_poolT = sem("mem_poolT")
        mem_poolT_kept = sem("mem_poolT_kept")
        mem_tok = sem("mem_tok")
        mem_tok_kept = sem("mem_tok_kept")
        mem_kv = sem("mem_kv")
        mem_kv_kept = sem("mem_kv_kept")
        mem_stored = sem("mem_stored")
        weights_scaled = sem("weights_scaled")
        zeroed = sem("zeroed")
        N_LOADS = len(consts) + 12

        def event(name, phases, parts=1, transfers=0):
            return Event(sem, name, [(ph, NB if ph[0] == "A" else GROUPS) for ph in phases], parts, transfers)

        CROSS = ["A0", "A1", "A2"]
        X_loaded = event("X_loaded", CROSS, transfers=1)
        ctx_loaded = event("ctx_loaded", CROSS, transfers=1)
        side_loaded = event("side_loaded", ["A1"], transfers=1)
        mask_loaded = event("mask_loaded", ["A1"], transfers=1)
        keymask_loaded = event("keymask_loaded", ["A2"], transfers=1)
        keybias_made = event("keybias_made", ["A2"])
        kv_made = event("kv_made", CROSS)
        k_kept = event("k_kept", CROSS)
        v_kept = event("v_kept", CROSS)
        kblk_made = event("kblk_made", CROSS, parts=NQ)
        xT_made = event("xT_made", CROSS)
        xT_kept = event("xT_kept", CROSS)
        q_made = event("q_made", CROSS)
        q_kept = event("q_kept", CROSS)
        xb_made = event("xb_made", CROSS)
        s_made = event("s_made", CROSS, parts=NQ)
        s_weighted = event("s_weighted", ["A1"], parts=NQ)
        s_masked = event("s_masked", ["A1"], parts=NQ)
        max_made = event("max_made", CROSS, parts=NQ)
        shifted = event("shifted", CROSS, parts=NQ)
        exp_made = event("exp_made", CROSS, parts=NQ)
        pT_made = event("pT_made", CROSS, parts=NQ)
        pT_kept = event("pT_kept", CROSS, parts=NQ)
        att_made = event("att_made", CROSS, parts=NQ)
        att_kept = event("att_kept", CROSS)
        back_made = event("back_made", CROSS)
        den_inverted = event("den_inverted", CROSS)
        o_made = event("o_made", CROSS)
        oT_made = event("oT_made", ["A1", "A2"])
        oT_kept = event("oT_kept", ["A1", "A2"])
        proj_made = event("proj_made", ["A1", "A2"])
        sum_made = event("sum_made", CROSS)
        stats_made = event("stats_made", CROSS)
        mv_made = event("mv_made", CROSS)
        var_made = event("var_made", CROSS)
        rstd_made = event("rstd_made", CROSS)
        z_made = event("z_made", CROSS)
        zg_made = event("zg_made", CROSS)
        y_made = event("y_made", CROSS)
        y_stored = event("y_stored", CROSS, transfers=1)

        FFS = ["F0", "F2", "F3"]
        fx_loaded = event("fx_loaded", FFS, transfers=1)
        fxT_made = {ph: event("fxT_made_" + ph, [ph]) for ph in FFS}
        fxT_kept = event("fxT_kept", FFS)
        fxb_made = {ph: event("fxb_made_" + ph, [ph]) for ph in FFS}
        PLAIN = ["F0", "F2"]
        hidden_made = event("hidden_made", PLAIN, parts=NF)
        hidden_kept = event("hidden_kept", PLAIN, parts=NF)
        gates_made = event("gates_made", ["F3"], parts=2 * NG)
        silu_kept = event("silu_kept", ["F3"], parts=NG)
        gated_kept = event("gated_kept", ["F3"], parts=NG)
        fo_made = event("fo_made", FFS)
        ft_made = event("ft_made", FFS)
        fstats_made = event("fstats_made", ["F2", "F3"], parts=GB)
        fmv_made = event("fmv_made", ["F2"], parts=GB)
        fcentred = event("fcentred", ["F2"], parts=GB)
        fvar_made = event("fvar_made", ["F2"])
        frstd_made = event("frstd_made", ["F2", "F3"])
        fz_made = {ph: event("fz_made_" + ph, [ph]) for ph in FFS[1:]}
        fzg_made = event("fzg_made", ["F2"])
        fy_made = event("fy_made", ["F2"])
        fy_stored = sem("fy_stored")
        fy_before = {ph: k * GROUPS for k, ph in enumerate(FFS)}

        x3_loaded = event("x3_loaded", ["A3"], transfers=1)
        xr_loaded = event("xr_loaded", ["A3"], transfers=1)
        vpre_loaded = event("vpre_loaded", ["A3"], transfers=4)
        sq_made = event("sq_made", ["A3"])
        rms_made = event("rms_made", ["A3"])
        xn_made = event("xn_made", ["A3"])
        xnT_made = event("xnT_made", ["A3"])
        xnT_kept = event("xnT_kept", ["A3"])
        q3_made = event("q3_made", ["A3"], parts=2)
        k3_made = event("k3_made", ["A3"], parts=2)
        v3_made = event("v3_made", ["A3"], parts=2)
        v3_kept = event("v3_kept", ["A3"], parts=2)
        q3_roped = event("q3_roped", ["A3"], parts=2)
        k3_roped = event("k3_roped", ["A3"], parts=2)
        q3_turned = event("q3_turned", ["A3"], parts=2)
        k3_turned = event("k3_turned", ["A3"], parts=2)
        qT3_made = event("qT3_made", ["A3"], parts=2)
        kT3_made = event("kT3_made", ["A3"], parts=2)
        qT3_kept = event("qT3_kept", ["A3"], parts=2)
        kT3_kept = event("kT3_kept", ["A3"], parts=2)
        kpre_made = event("kpre_made", ["A3"])
        s3_made = event("s3_made", ["A3"], parts=2)
        max3_parts = event("max3_parts", ["A3"], parts=2)
        max3_made = event("max3_made", ["A3"], parts=2)
        shifted3 = event("shifted3", ["A3"], parts=2)
        exp3_made = event("exp3_made", ["A3"], parts=2)
        den3_parts = event("den3_parts", ["A3"], parts=2)
        den3_sum = event("den3_sum", ["A3"], parts=2)
        den3_inv = event("den3_inv", ["A3"], parts=2)
        p3_rows = event("p3_rows", ["A3"], parts=2)
        p3_second = event("p3_second", ["A3"], parts=2)
        p3_made = event("p3_made", ["A3"], parts=2)
        pT3_made = event("pT3_made", ["A3"], parts=6)
        pT3_kept = event("pT3_kept", ["A3"], parts=6)
        att3_made = event("att3_made", ["A3"], parts=2)
        att3_kept = event("att3_kept", ["A3"], parts=2)
        proj3_made = event("proj3_made", ["A3"])
        y3_made = event("y3_made", ["A3"])
        y3_stored = event("y3_stored", ["A3"], transfers=1)

        SCALE = {"A0": DH ** -0.5, "A1": DH ** -0.5, "A2": D ** -0.5}
        scores_bank = bank[0:2]
        pT_bank = bank[2:4]
        att_bank = bank[4]
        kv_bank = bank[5]
        x_bank = bank[6]
        out_bank = bank[7]
        K_COL, V_COL, Q_COL = 0, 128, 128

        def quarter(ap, c):
            return ap[:, c * QC:(c + 1) * QC]

        def by_head(ap):
            return ap.rearrange("p (h k) -> p h k", k=C)

        def spread(col, n):
            return col.unsqueeze(2).to_broadcast([col.shape[0], col.shape[1], n])

        def phase_before(ph):
            return order[order.index(ph) - 1] if ph != order[0] else None

        def two_before(b, c):
            return (b if c >= 2 else b + -1), (c - 2) % NQ

        def cross_sync(sp, ph):
            def load(b):
                if (b + -2).exists:
                    sp.wait_ge(kv_made.sem(b + -2), kv_made.count(ph, b + -2))
                sp.dma_start(ctx_s[b.par][:], at(a["ctxT"], b).rearrange("b d k -> (b d) k")).then_inc(ctx_loaded.sem(b), 16)
                if ph == "A1":
                    if (b + -2).exists:
                        sp.wait_ge(s_weighted.sem(b + -2), s_weighted.count(ph, b + -2, NQ - 1))
                    sp.dma_start(side_s[b.par][:], at(a["side"], b).rearrange("b t n -> (b t) n")).then_inc(side_loaded.sem(b), 16)
                    if (b + -2).exists:
                        sp.wait_ge(s_masked.sem(b + -2), s_masked.count(ph, b + -2, NQ - 1))
                    sp.dma_start(mask_s[b.par][:], at(a["mask"], b).rearrange("b t n -> (b t) n")).then_inc(mask_loaded.sem(b), 16)
                if ph == "A2":
                    if (b + -2).exists:
                        sp.wait_ge(keybias_made.sem(b + -2), keybias_made.count(ph, b + -2))
                    sp.dma_start(keymask_s[b.par][:], at(a["keymask"], b)).then_inc(keymask_loaded.sem(b), 16)
                prev = phase_before(ph)
                if prev in FFS:
                    sp.wait_ge(fy_stored, (b.pair + (fy_before[prev] + 1)) * 16)
                elif prev:
                    sp.wait_ge(y_stored.sem(b), y_stored.count(prev, b))
                if (b + -2).exists:
                    sp.wait_ge(xT_made.sem(b + -2), xT_made.count(ph, b + -2))
                if (b + -2).exists:
                    sp.wait_ge(xb_made.sem(b + -2), xb_made.count(ph, b + -2))
                sp.dma_start(x_s[b.par][:], at(source[ph], b).rearrange("b t d -> (b t) d")).then_inc(X_loaded.sem(b), 16)

            def step(b, has):
                if has(2):
                    load(b + 2)
                if has(-2):
                    sp.wait_ge(y_made.sem(b + -2), y_made.count(ph, b + -2))
                    sp.dma_start(at(target[ph], b + -2).rearrange("b t d -> (b t) d"), y_s[(b + -2).par][:]).then_inc(y_stored.sem(b + -2), 16)
            drive(sp, NB, step, reach=2)

        def cross_tensor(pe, ph):
            w = cross[ph]

            def project_context(b):
                if (b + -1).exists:
                    pe.wait_ge(k_kept.sem(b + -1), k_kept.count(ph, b + -1))
                    pe.wait_ge(v_kept.sem(b + -1), v_kept.count(ph, b + -1))
                pe.wait_ge(ctx_loaded.sem(b), ctx_loaded.count(ph, b))
                nc.tensor.matmul(kv_bank[:, K_COL:K_COL + C], w["wk"][:], ctx_s[b.par][:], start=True, stop=True)
                nc.tensor.matmul(kv_bank[0:C, V_COL:V_COL + D], ctx_s[b.par][:], w["wv"][:], start=True, stop=True).then_inc(kv_made.sem(b), 1)

            def transpose_x(b):
                pe.wait_ge(X_loaded.sem(b), X_loaded.count(ph, b))
                if (b + -1).exists:
                    pe.wait_ge(q_kept.sem(b + -1), q_kept.count(ph, b + -1))
                nc.tensor.transpose(x_bank[:, 0:T], x_s[b.par][:], ident[:]).then_inc(xT_made.sem(b), 1)

            def project_queries(b):
                pe.wait_ge(xT_kept.sem(b), xT_kept.count(ph, b))
                nc.tensor.matmul(x_bank[:, Q_COL:Q_COL + T], w["wq"][:], xT_s[b.par][:], start=True, stop=True).then_inc(q_made.sem(b), 1)

            def scores(b, c):
                pe.wait_ge(kblk_made.sem(b), kblk_made.count(ph, b, c))
                if c == 0:
                    pe.wait_ge(q_kept.sem(b), q_kept.count(ph, b))
                    if ph == "A2":
                        pe.wait_ge(keybias_made.sem(b), keybias_made.count(ph, b))
                done = s_weighted if ph == "A1" else shifted
                old, old_c = two_before(b, c)
                if old.exists:
                    pe.wait_ge(done.sem(old), done.count(ph, old, old_c))
                dst = scores_bank[c % 2][:, 0:QC]
                mm = nc.tensor.matmul(dst, qT_s[b.par][:], quarter(kblk_s[b.par], c), start=True, stop=(ph == "A1"))
                if ph == "A0":
                    mm = nc.tensor.matmul(dst, identb[:], causal[:], start=False, stop=True)
                if ph == "A2":
                    bias = keybias_s[b.par][0:1, :].unsqueeze(1).to_broadcast([1, QH, C])
                    mm = nc.tensor.matmul(dst, onesb[0:1, :], bias, start=False, stop=True)
                mm.then_inc(s_made.sem(b), 1)

            def transpose_p(b, c):
                pe.wait_ge(exp_made.sem(b), exp_made.count(ph, b, c))
                old, old_c = two_before(b, c)
                if old.exists:
                    pe.wait_ge(pT_kept.sem(old), pT_kept.count(ph, old, old_c))
                for h in range(QH):
                    mm = nc.tensor.transpose(pT_bank[c % 2][0:C, h * T:(h + 1) * T], p_s[c % 2][:, h * C:(h + 1) * C], ident[:])
                mm.then_inc(pT_made.sem(b), 1)

            def attend(b, c):
                pe.wait_ge(pT_kept.sem(b), pT_kept.count(ph, b, c))
                if c == 0:
                    pe.wait_ge(v_kept.sem(b), v_kept.count(ph, b))
                    if (b + -1).exists:
                        pe.wait_ge(att_kept.sem(b + -1), att_kept.count(ph, b + -1))
                for h in range(QH):
                    head = c * QH + h
                    mm = nc.tensor.matmul(att_bank[VP * h:VP * h + VP, c * T:(c + 1) * T],
                                          v_s[b.par][:, head * VP:(head + 1) * VP], pT_s[c % 2][:, h * T:(h + 1) * T],
                                          start=True, stop=True)
                mm.then_inc(att_made.sem(b), 1)

            def back(b):
                pe.wait_ge(att_kept.sem(b), att_kept.count(ph, b))
                done = o_made if ph == "A0" else sum_made
                if (b + -1).exists:
                    pe.wait_ge(done.sem(b + -1), done.count(ph, b + -1))
                for c in range(NQ):
                    mm = nc.tensor.transpose(out_bank[:, c * T:(c + 1) * T], att_s[b.par][:, c * T:(c + 1) * T], ident[:])
                mm.then_inc(back_made.sem(b), 1)

            def transpose_o(b):
                pe.wait_ge(o_made.sem(b), o_made.count(ph, b))
                nc.tensor.transpose(out_bank[:, 0:T], o_s[b.par][:], ident[:]).then_inc(oT_made.sem(b), 1)

            def project_out(b):
                pe.wait_ge(oT_kept.sem(b), oT_kept.count(ph, b))
                nc.tensor.matmul(out_bank[:, 0:D], oT_s[b.par][:], w["wo"][:], start=True, stop=True).then_inc(proj_made.sem(b), 1)

            def step(b, has):
                if has(0):
                    scores(b, 2)
                    transpose_p(b, 0)
                if has(-1):
                    attend(b + -1, 3)
                if has(1):
                    project_context(b + 1)
                    transpose_x(b + 1)
                if has(0):
                    scores(b, 3)
                if has(1):
                    project_queries(b + 1)
                if has(0):
                    transpose_p(b, 1)
                    attend(b, 0)
                if has(-1):
                    back(b + -1)
                if has(1):
                    scores(b + 1, 0)
                if has(0):
                    transpose_p(b, 2)
                    attend(b, 1)
                if has(-1) and ph != "A0":
                    transpose_o(b + -1)
                if has(1):
                    scores(b + 1, 1)
                if has(0):
                    transpose_p(b, 3)
                    attend(b, 2)
                if has(-1) and ph != "A0":
                    project_out(b + -1)
            drive(pe, NB, step, reach=2)

        def cross_scalar(act, ph):
            w = cross[ph]

            def exps(b, c):
                act.wait_ge(shifted.sem(b), shifted.count(ph, b, c))
                old, old_c = two_before(b, c)
                if old.exists:
                    act.wait_ge(pT_made.sem(old), pT_made.count(ph, old, old_c))
                nc.scalar.activation(p_s[c % 2][:], shifted_s[c % 2][:], ACT.Exp, scale=SCALE[ph]).then_inc(exp_made.sem(b), 1)

            def keep_pT(b, c):
                act.wait_ge(pT_made.sem(b), pT_made.count(ph, b, c))
                old, old_c = two_before(b, c)
                if old.exists:
                    act.wait_ge(att_made.sem(old), att_made.count(ph, old, old_c))
                nc.scalar.activation(pT_s[c % 2][:], pT_bank[c % 2][0:C, :], ACT.Copy).then_inc(pT_kept.sem(b), 1)

            def keep_k(b):
                act.wait_ge(kv_made.sem(b), kv_made.count(ph, b))
                if (b + -2).exists:
                    act.wait_ge(kblk_made.sem(b + -2), kblk_made.count(ph, b + -2, NQ - 1))
                src = kv_bank[:, K_COL:K_COL + C]
                if ph == "A2":
                    nc.scalar.activation(kT_s[b.par][:], src, ACT.Copy).then_inc(k_kept.sem(b), 1)
                else:
                    nc.scalar.activation(kT_s[b.par][:], src, ACT.Identity, bias=w["bk"][:, 0:1]).then_inc(k_kept.sem(b), 1)

            def keep_xT(b):
                act.wait_ge(xT_made.sem(b), xT_made.count(ph, b))
                if (b + -2).exists:
                    act.wait_ge(q_made.sem(b + -2), q_made.count(ph, b + -2))
                nc.scalar.activation(xT_s[b.par][:], x_bank[:, 0:T], ACT.Copy).then_inc(xT_kept.sem(b), 1)

            def keep_q(b):
                act.wait_ge(q_made.sem(b), q_made.count(ph, b))
                if (b + -2).exists:
                    act.wait_ge(s_made.sem(b + -2), s_made.count(ph, b + -2, NQ - 1))
                if ph == "A2":
                    nc.scalar.activation(qT_s[b.par][:], x_bank[:, Q_COL:Q_COL + T], ACT.Copy).then_inc(q_kept.sem(b), 1)
                else:
                    nc.scalar.activation(qT_s[b.par][:], x_bank[:, Q_COL:Q_COL + T], ACT.Identity, bias=w["bq"][:, 0:1]).then_inc(q_kept.sem(b), 1)

            def keep_att(b):
                act.wait_ge(att_made.sem(b), att_made.count(ph, b, NQ - 1))
                if (b + -2).exists:
                    act.wait_ge(back_made.sem(b + -2), back_made.count(ph, b + -2))
                nc.scalar.activation(att_s[b.par][:], att_bank[:], ACT.Copy).then_inc(att_kept.sem(b), 1)

            def keep_oT(b):
                act.wait_ge(oT_made.sem(b), oT_made.count(ph, b))
                if (b + -2).exists:
                    act.wait_ge(proj_made.sem(b + -2), proj_made.count(ph, b + -2))
                nc.scalar.activation(oT_s[b.par][:], out_bank[:, 0:T], ACT.Copy).then_inc(oT_kept.sem(b), 1)

            def step(b, has):
                if has(0):
                    exps(b, 1)
                    keep_pT(b, 0)
                if has(1):
                    keep_k(b + 1)
                    keep_xT(b + 1)
                if has(-1):
                    keep_att(b + -1)
                if has(1):
                    keep_q(b + 1)
                if has(0):
                    exps(b, 2)
                    keep_pT(b, 1)
                    exps(b, 3)
                    keep_pT(b, 2)
                if has(-1) and ph != "A0":
                    keep_oT(b + -1)
                if has(1):
                    exps(b + 1, 0)
                if has(0):
                    keep_pT(b, 3)
            drive(act, NB, step, reach=2)

        def cross_vector(dve, ph):
            w = cross[ph]

            def shift(b, c):
                dve.wait_ge(s_made.sem(b), s_made.count(ph, b, c))
                src = scores_bank[c % 2][:, 0:QC]
                if ph == "A1":
                    if c == 0:
                        dve.wait_ge(side_loaded.sem(b), side_loaded.count(ph, b))
                        dve.wait_ge(mask_loaded.sem(b), mask_loaded.count(ph, b))
                    nc.vector.tensor_tensor(prod_s[c % 2][:], src, quarter(side_s[b.par], c), ALU.mult).then_inc(s_weighted.sem(b), 1)
                    dve.wait_ge(s_weighted.sem(b), s_weighted.count(ph, b, c))
                    old, old_c = two_before(b, c)
                    if old.exists:
                        dve.wait_ge(shifted.sem(old), shifted.count(ph, old, old_c))
                    nc.vector.scalar_tensor_tensor(scored_s[c % 2][:], quarter(mask_s[b.par], c), MASKED, prod_s[c % 2][:],
                                                   ALU.mult, ALU.add).then_inc(s_masked.sem(b), 1)
                    dve.wait_ge(s_masked.sem(b), s_masked.count(ph, b, c))
                    src = scored_s[c % 2][:]
                nc.vector.tensor_reduce(max_s[c % 2][:], by_head(src), AX.X, ALU.max).then_inc(max_made.sem(b), 1)
                if ph != "A1":
                    dve.wait_ge(max_made.sem(b), max_made.count(ph, b, c))
                    old, old_c = two_before(b, c)
                    if old.exists:
                        dve.wait_ge(exp_made.sem(old), exp_made.count(ph, old, old_c))
                    nc.vector.tensor_tensor(by_head(shifted_s[c % 2][:]), by_head(src), spread(max_s[c % 2][:], C), ALU.subtract)\
                        .then_inc(shifted.sem(b), 1)

            def keep_v(b):
                dve.wait_ge(kv_made.sem(b), kv_made.count(ph, b))
                dve.wait_ge(k_kept.sem(b), k_kept.count(ph, b))
                if (b + -2).exists:
                    dve.wait_ge(att_made.sem(b + -2), att_made.count(ph, b + -2, NQ - 1))
                dst = v_s[b.par][:].rearrange("p (h v) -> p h v", v=VP)[:, :, 0:DH]
                src = kv_bank[0:C, V_COL:V_COL + D].rearrange("p (h v) -> p h v", v=DH)
                if ph != "A1":
                    nc.vector.tensor_copy(dst, src).then_inc(v_kept.sem(b), 1)
                else:
                    nc.vector.tensor_tensor(dst, src, w["bv"][0:C, :].rearrange("p (h v) -> p h v", v=DH), ALU.add).then_inc(v_kept.sem(b), 1)

            def key_bias(b):
                dve.wait_ge(keymask_loaded.sem(b), keymask_loaded.count(ph, b))
                if (b + -2).exists:
                    dve.wait_ge(s_made.sem(b + -2), s_made.count(ph, b + -2, NQ - 1))
                nc.vector.tensor_scalar(keybias_s[b.par][:], keymask_s[b.par][:], 0, -1.0e20, ALU.is_equal, ALU.mult)\
                    .then_inc(keybias_made.sem(b), 1)

            def residual(b):
                dve.wait_ge(X_loaded.sem(b), X_loaded.count(ph, b))
                if (b + -2).exists:
                    dve.wait_ge(sum_made.sem(b + -2), sum_made.count(ph, b + -2))
                nc.vector.tensor_tensor(xb_s[b.par][:], x_s[b.par][:], w["bo"][:], ALU.add).then_inc(xb_made.sem(b), 1)

            def normalise(b):
                dve.wait_ge(back_made.sem(b), back_made.count(ph, b))
                raw = out_bank[:].rearrange("p (h v) -> p h v", v=VP)
                nc.vector.reciprocal(rden_s[b.par][:].unsqueeze(2), raw[:, :, DH:DH + 1]).then_inc(den_inverted.sem(b), 1)
                dve.wait_ge(den_inverted.sem(b), den_inverted.count(ph, b))
                if ph == "A0":
                    if (b + -2).exists:
                        dve.wait_ge(sum_made.sem(b + -2), sum_made.count(ph, b + -2))
                else:
                    if (b + -2).exists:
                        dve.wait_ge(oT_made.sem(b + -2), oT_made.count(ph, b + -2))
                nc.vector.tensor_tensor(o_s[b.par][:].rearrange("p (h v) -> p h v", v=DH), raw[:, :, 0:DH],
                                        spread(rden_s[b.par][:], DH), ALU.mult).then_inc(o_made.sem(b), 1)

            def sums(b):
                if (b + -2).exists:
                    dve.wait_ge(z_made.sem(b + -2), z_made.count(ph, b + -2))
                dve.wait_ge(xb_made.sem(b), xb_made.count(ph, b))
                if ph == "A0":
                    dve.wait_ge(o_made.sem(b), o_made.count(ph, b))
                    nc.vector.tensor_tensor(t_s[b.par][:], o_s[b.par][:], xb_s[b.par][:], ALU.add).then_inc(sum_made.sem(b), 1)
                else:
                    dve.wait_ge(proj_made.sem(b), proj_made.count(ph, b))
                    nc.vector.tensor_tensor(t_s[b.par][:], out_bank[:, 0:D], xb_s[b.par][:], ALU.add).then_inc(sum_made.sem(b), 1)
                dve.wait_ge(sum_made.sem(b), sum_made.count(ph, b))
                nc.vector.bn_stats(stats_s[b.par][:], t_s[b.par][:]).then_inc(stats_made.sem(b), 1)
                dve.wait_ge(stats_made.sem(b), stats_made.count(ph, b))

            def aggregate(b):
                nc.vector.bn_aggr(mv_s[b.par][:], stats_s[b.par][:]).then_inc(mv_made.sem(b), 1)

            def centre(b):
                dve.wait_ge(rstd_made.sem(b), rstd_made.count(ph, b))
                if (b + -2).exists:
                    dve.wait_ge(zg_made.sem(b + -2), zg_made.count(ph, b + -2))
                nc.vector.tensor_scalar(z_s[b.par][:], t_s[b.par][:], mv_s[b.par][:, 0:1], rstd_s[b.par][:, 0:1],
                                        ALU.subtract, ALU.mult).then_inc(z_made.sem(b), 1)

            def step(b, has):
                if has(-2):
                    sums(b + -2)
                if has(0):
                    shift(b, 2)
                if has(-2):
                    aggregate(b + -2)
                if has(1) and ph == "A2":
                    key_bias(b + 1)
                if has(0):
                    shift(b, 3)
                if has(0) and ph == "A1":
                    residual(b)
                if has(1):
                    keep_v(b + 1)
                if has(-1):
                    normalise(b + -1)
                if has(1):
                    shift(b + 1, 0)
                if has(-2):
                    centre(b + -2)
                if has(1):
                    shift(b + 1, 1)
            drive(dve, NB, step, reach=2)

        def cross_gpsimd(pool, ph):
            w = cross[ph]

            def block_keys(b, c):
                pool.wait_ge(k_kept.sem(b), k_kept.count(ph, b))
                if (b + -2).exists:
                    pool.wait_ge(s_made.sem(b + -2), s_made.count(ph, b + -2, c))
                nc.gpsimd.tensor_tensor(by_head(quarter(kblk_s[b.par], c)), kT_s[b.par][:].unsqueeze(1).to_broadcast([D, QH, C]),
                                        spread(headmask[:, c * QH:(c + 1) * QH], C), ALU.mult).then_inc(kblk_made.sem(b), 1)

            def shift(b, c):
                pool.wait_ge(max_made.sem(b), max_made.count(ph, b, c))
                old, old_c = two_before(b, c)
                if old.exists:
                    pool.wait_ge(exp_made.sem(old), exp_made.count(ph, old, old_c))
                nc.gpsimd.tensor_tensor(by_head(shifted_s[c % 2][:]), by_head(scored_s[c % 2][:]), spread(max_s[c % 2][:], C), ALU.subtract)\
                    .then_inc(shifted.sem(b), 1)

            def residual(b):
                pool.wait_ge(X_loaded.sem(b), X_loaded.count(ph, b))
                if (b + -2).exists:
                    pool.wait_ge(sum_made.sem(b + -2), sum_made.count(ph, b + -2))
                nc.gpsimd.tensor_tensor(xb_s[b.par][:], x_s[b.par][:], w["bo"][:], ALU.add).then_inc(xb_made.sem(b), 1)

            def rstd(b):
                pool.wait_ge(mv_made.sem(b), mv_made.count(ph, b))
                nc.gpsimd.tensor_tensor(var_s[b.par][:], mv_s[b.par][:, 1:2], ln_eps[:, 0:1], ALU.add).then_inc(var_made.sem(b), 1)
                pool.wait_ge(var_made.sem(b), var_made.count(ph, b))
                if (b + -2).exists:
                    pool.wait_ge(z_made.sem(b + -2), z_made.count(ph, b + -2))
                nc.gpsimd.tensor_tensor(rstd_s[b.par][:], var_s[b.par][:], minus_half[:, 0:1], ALU.pow).then_inc(rstd_made.sem(b), 1)

            def affine(b):
                pool.wait_ge(z_made.sem(b), z_made.count(ph, b))
                nc.gpsimd.tensor_tensor(zg_s[b.par][:], z_s[b.par][:], w["ln_g"][:], ALU.mult).then_inc(zg_made.sem(b), 1)
                pool.wait_ge(zg_made.sem(b), zg_made.count(ph, b))
                if (b + -2).exists:
                    pool.wait_ge(y_stored.sem(b + -2), y_stored.count(ph, b + -2))
                nc.gpsimd.tensor_tensor(y_s[b.par][:], zg_s[b.par][:], w["ln_b"][:], ALU.add).then_inc(y_made.sem(b), 1)

            def step(b, has):
                weighted = ph == "A1"
                if has(0) and weighted:
                    shift(b, 2)
                if has(1):
                    block_keys(b + 1, 0)
                if has(-2):
                    rstd(b + -2)
                if has(0) and weighted:
                    shift(b, 3)
                if has(1):
                    block_keys(b + 1, 1)
                if has(0) and not weighted:
                    residual(b)
                if has(1) and weighted:
                    shift(b + 1, 0)
                if has(1):
                    block_keys(b + 1, 2)
                if has(1) and weighted:
                    shift(b + 1, 1)
                if has(1):
                    block_keys(b + 1, 3)
                if has(-2):
                    affine(b + -2)
            drive(pool, NB, step, reach=2)

        FT = GB * T
        fx_bank = bank[0:2]
        fh_bank = bank[2:6]
        fo_bank = bank[6:8]

        def chunks(ph):
            return 2 * NG if ph == "F3" else NF

        def chunk_before(ph, g, j, n):
            j -= n
            return (g, j) if j >= 0 else (g + -1, j + chunks(ph))

        def chunk_bank(ph, g, j):
            return fh_bank[(chunks(ph) * g.par + j) % 4][:, 0:FT]

        def pair_of(ap, g):
            return at(ap, g, GB).rearrange("b t d -> t b d")

        def ff_sync(sp, ph):
            late = 2 if ph == "F2" else 1
            taken = fz_made[ph] if ph == "F3" else fxT_made[ph]

            def step(g, has):
                if has(2):
                    n = g + 2
                    if (n + -2).exists:
                        sp.wait_ge(taken.sem(n + -2), taken.count(ph, n + -2))
                    if (n + -2).exists:
                        sp.wait_ge(fxb_made[ph].sem(n + -2), fxb_made[ph].count(ph, n + -2))
                    stored = y3_stored if ph == "F3" else y_stored
                    even, odd = (Batch(n.pair * 2 + n.par, k) for k in range(2))
                    sp.wait_ge(stored.sem(even), stored.count(phase_before(ph), even))
                    sp.wait_ge(stored.sem(odd), stored.count(phase_before(ph), odd))
                    sp.dma_start(fx_s[n.par][:], pair_of(source[ph], n)).then_inc(fx_loaded.sem(n), 16)
                if has(-late):
                    p = g + -late
                    done = fy_made if ph == "F2" else ft_made
                    sp.wait_ge(done.sem(p), done.count(ph, p))
                    sp.dma_start(pair_of(target[ph], p), (fy_s if ph == "F2" else ft_s)[p.par][:]).then_inc(fy_stored, 16)
            drive(sp, GROUPS, step, reach=2)

        def ff_tensor(pe, ph):
            w1, w2 = (w1g, w2g) if ph == "F3" else (ffw[ph]["w1"], ffw[ph]["w2"])
            made = gates_made if ph == "F3" else hidden_made

            def wait_kept(g, j):
                if ph == "F3":
                    done = (silu_kept, gated_kept)[j % 2]
                    pe.wait_ge(done.sem(g), done.count(ph, g, j // 2))
                else:
                    pe.wait_ge(hidden_kept.sem(g), hidden_kept.count(ph, g, j))

            def transpose_x(g):
                if (g + -2).exists:
                    pe.wait_ge(fxT_kept.sem(g + -2), fxT_kept.count(ph, g + -2))
                for k in range(GB):
                    if ph == "F3":
                        pe.wait_ge(fz_made[ph].sem(g), fz_made[ph].count(ph, g))
                        src = fz_s[g.par][:, k, :]
                    else:
                        pe.wait_ge(fx_loaded.sem(g), fx_loaded.count(ph, g))
                        src = fx_s[g.par][:, k, :]
                    mm = nc.tensor.transpose(fx_bank[g.par][:, k * T:(k + 1) * T], src, ident[:])
                mm.then_inc(fxT_made[ph].sem(g), 1)

            def hidden(g):
                pe.wait_ge(fxT_kept.sem(g), fxT_kept.count(ph, g))
                for j in range(chunks(ph)):
                    bg, bj = chunk_before(ph, g, j, 4)
                    if bg.exists:
                        wait_kept(bg, bj)
                    col = ((j // 2 + NG * (1 - j % 2)) if ph == "F3" else j) * 128
                    nc.tensor.matmul(chunk_bank(ph, g, j), w1[:, col:col + 128], fxT_s[g.par][:], start=True, stop=True)\
                        .then_inc(made.sem(g), 1)

            def down(g):
                last = range(1, 2 * NG, 2) if ph == "F3" else range(NF)
                wait_kept(g, last[-1])
                if (g + -2).exists:
                    pe.wait_ge(ft_made.sem(g + -2), ft_made.count(ph, g + -2))
                for k in range(GB):
                    for f in range(len(last)):
                        mm = nc.tensor.matmul(fo_bank[g.par][:, k * D:(k + 1) * D], fh_s[g.par][:, f, k * T:(k + 1) * T],
                                              w2[:, f, :], start=(f == 0), stop=(f == len(last) - 1))
                mm.then_inc(fo_made.sem(g), 1)

            def step(g, has):
                if has(0):
                    hidden(g)
                if has(1):
                    transpose_x(g + 1)
                if has(-1):
                    down(g + -1)
            drive(pe, GROUPS, step)

        def ff_scalar(act, ph):
            made = gates_made if ph == "F3" else hidden_made

            def keep_xT(g):
                act.wait_ge(fxT_made[ph].sem(g), fxT_made[ph].count(ph, g))
                if (g + -2).exists:
                    act.wait_ge(made.sem(g + -2), made.count(ph, g + -2, chunks(ph) - 1))
                nc.scalar.activation(fxT_s[g.par][:], fx_bank[g.par][:, 0:FT], ACT.Copy).then_inc(fxT_kept.sem(g), 1)

            def activate(g):
                for j in range(0, chunks(ph), 2 if ph == "F3" else 1):
                    act.wait_ge(made.sem(g), made.count(ph, g, j))
                    src = chunk_bank(ph, g, j)
                    if ph == "F3":
                        if (g + -2).exists:
                            act.wait_ge(gated_kept.sem(g + -2), gated_kept.count(ph, g + -2, j // 2))
                        nc.scalar.activation(fsilu_s[g.par][:, j // 2, :], src, ACT.Silu, bias=b1g[:, NG + j // 2:NG + j // 2 + 1])\
                            .then_inc(silu_kept.sem(g), 1)
                    else:
                        if (g + -2).exists:
                            act.wait_ge(fo_made.sem(g + -2), fo_made.count(ph, g + -2))
                        nc.scalar.activation(fh_s[g.par][:, j, :], src, ACT.Gelu if ph == "F0" else ACT.Relu,
                                             bias=ffw[ph]["b1"][:, j:j + 1]).then_inc(hidden_kept.sem(g), 1)

            def step(g, has):
                if has(0):
                    activate(g)
                if has(1):
                    keep_xT(g + 1)
            drive(act, GROUPS, step)

        def ff_vector(dve, ph):
            def squares(g):
                dve.wait_ge(fx_loaded.sem(g), fx_loaded.count(ph, g))
                if (g + -2).exists:
                    dve.wait_ge(frstd_made.sem(g + -2), frstd_made.count(ph, g + -2))
                for k in range(GB):
                    nc.vector.tensor_tensor_reduce(fsq_s[k][:], fx_s[g.par][:, k, :], fx_s[g.par][:, k, :], 1.0 / D, RMS_EPS, ALU.mult, ALU.add,
                                                   fvar_s[g.par][:, k:k + 1]).then_inc(fstats_made.sem(g), 1)

            def norm(g):
                dve.wait_ge(frstd_made.sem(g), frstd_made.count(ph, g))
                if (g + -2).exists:
                    dve.wait_ge(fxT_made[ph].sem(g + -2), fxT_made[ph].count(ph, g + -2))
                nc.vector.tensor_tensor(fz_s[g.par][:], fx_s[g.par][:], spread(frstd_s[g.par][:], D), ALU.mult).then_inc(fz_made[ph].sem(g), 1)

            def gate(g):
                for f in range(NG):
                    dve.wait_ge(gates_made.sem(g), gates_made.count(ph, g, 2 * f + 1))
                    dve.wait_ge(silu_kept.sem(g), silu_kept.count(ph, g, f))
                    if (g + -2).exists:
                        dve.wait_ge(fo_made.sem(g + -2), fo_made.count(ph, g + -2))
                    nc.vector.scalar_tensor_tensor(fh_s[g.par][:, f, :], chunk_bank(ph, g, 2 * f + 1), b1g[:, f:f + 1],
                                                   fsilu_s[g.par][:, f, :], ALU.add, ALU.mult).then_inc(gated_kept.sem(g), 1)

            def total(g):
                dve.wait_ge(fo_made.sem(g), fo_made.count(ph, g))
                dve.wait_ge(fxb_made[ph].sem(g), fxb_made[ph].count(ph, g))
                if ph == "F2":
                    if (g + -2).exists:
                        dve.wait_ge(fz_made[ph].sem(g + -2), fz_made[ph].count(ph, g + -2))
                else:
                    if not (ph == "F0" and g.first):
                        dve.wait_ge(fy_stored, (g.pair * 2 + (g.par + fy_before[ph])) * 16)
                nc.vector.tensor_tensor(ft_s[g.par][:], fo_bank[g.par][:, 0:GB * D].rearrange("p (b d) -> p b d", b=GB),
                                        fxb_s[g.par][:], ALU.add).then_inc(ft_made.sem(g), 1)

            def layernorm(g):
                dve.wait_ge(ft_made.sem(g), ft_made.count(ph, g))
                nc.vector.bn_stats(fstats_s[g.par][:, 0, :], ft_s[g.par][:, 0, :]).then_inc(fstats_made.sem(g), 1)
                dve.wait_ge(fstats_made.sem(g), fstats_made.count(ph, g, 0))
                nc.vector.bn_stats(fstats_s[g.par][:, 1, :], ft_s[g.par][:, 1, :]).then_inc(fstats_made.sem(g), 1)
                nc.vector.bn_aggr(fmv_s[g.par][:, 0, :], fstats_s[g.par][:, 0, :]).then_inc(fmv_made.sem(g), 1)
                dve.wait_ge(fmv_made.sem(g), fmv_made.count(ph, g, 0))
                dve.wait_ge(fstats_made.sem(g), fstats_made.count(ph, g, 1))
                if (g + -2).exists:
                    dve.wait_ge(fz_made[ph].sem(g + -2), fz_made[ph].count(ph, g + -2))
                centred(g, 0)
                nc.vector.bn_aggr(fmv_s[g.par][:, 1, :], fstats_s[g.par][:, 1, :]).then_inc(fmv_made.sem(g), 1)
                dve.wait_ge(fmv_made.sem(g), fmv_made.count(ph, g, 1))
                centred(g, 1)
                dve.wait_ge(frstd_made.sem(g), frstd_made.count(ph, g))
                dve.wait_ge(fcentred.sem(g), fcentred.count(ph, g, 1))
                if (g + -2).exists:
                    dve.wait_ge(fzg_made.sem(g + -2), fzg_made.count(ph, g + -2))
                nc.vector.tensor_tensor(fz_s[g.par][:], fc_s[g.par][:], spread(frstd_s[g.par][:], D), ALU.mult).then_inc(fz_made[ph].sem(g), 1)

            def centred(g, k):
                nc.vector.tensor_scalar(fc_s[g.par][:, k, :], ft_s[g.par][:, k, :], fmv_s[g.par][:, k, 0:1], None, ALU.subtract)\
                    .then_inc(fcentred.sem(g), 1)

            def step(g, has):
                if has(1) and ph == "F3":
                    norm(g + 1)
                if has(0) and ph == "F3":
                    gate(g)
                if has(2) and ph == "F3":
                    squares(g + 2)
                if has(-1):
                    total(g + -1)
                    if ph == "F2":
                        layernorm(g + -1)
            drive(dve, GROUPS, step, reach=2)

        def ff_gpsimd(pool, ph):
            b2 = b2g if ph == "F3" else ffw[ph]["b2"]

            def every(row):
                return row[:].unsqueeze(1).to_broadcast([T, GB, D])

            def residual(g):
                pool.wait_ge(fx_loaded.sem(g), fx_loaded.count(ph, g))
                if (g + -2).exists:
                    pool.wait_ge(ft_made.sem(g + -2), ft_made.count(ph, g + -2))
                nc.gpsimd.tensor_tensor(fxb_s[g.par][:], fx_s[g.par][:], every(b2), ALU.add).then_inc(fxb_made[ph].sem(g), 1)

            def rstd(g):
                done = fstats_made if ph == "F3" else fmv_made
                pool.wait_ge(done.sem(g), done.count(ph, g, GB - 1))
                if ph == "F2":
                    nc.gpsimd.tensor_tensor(fvar_s[g.par][:], fmv_s[g.par][:, :, 1], ln_eps[:], ALU.add).then_inc(fvar_made.sem(g), 1)
                    pool.wait_ge(fvar_made.sem(g), fvar_made.count(ph, g))
                if (g + -2).exists:
                    pool.wait_ge(fz_made[ph].sem(g + -2), fz_made[ph].count(ph, g + -2))
                nc.gpsimd.tensor_tensor(frstd_s[g.par][:], fvar_s[g.par][:], minus_half[:], ALU.pow).then_inc(frstd_made.sem(g), 1)

            def affine(g):
                pool.wait_ge(fz_made[ph].sem(g), fz_made[ph].count(ph, g))
                nc.gpsimd.tensor_tensor(fn_s[g.par][:], fz_s[g.par][:], every(ffw[ph]["g"]), ALU.mult).then_inc(fzg_made.sem(g), 1)
                pool.wait_ge(fzg_made.sem(g), fzg_made.count(ph, g))
                pool.wait_ge(fy_stored, (g.pair * 2 + (g.par + fy_before[ph])) * 16)
                nc.gpsimd.tensor_tensor(fy_s[g.par][:], fn_s[g.par][:], every(ffw[ph]["b"]), ALU.add).then_inc(fy_made.sem(g), 1)

            def step(g, has):
                if has(2) and ph == "F3":
                    rstd(g + 2)
                if has(1):
                    residual(g + 1)
                if has(-1) and ph == "F2":
                    rstd(g + -1)
                    affine(g + -1)
            drive(pool, GROUPS, step, reach=2)

        ph3 = "A3"
        q_bank, k_bank, v_bank = bank[0:3]
        turn3 = bank[3:5]
        s_even, s_odd = bank[5], bank[6]
        att3 = bank[7]
        LOC = HC * SEG
        HALF = 2 * HC * KH

        IN = {"q": q_bank, "k": k_bank, "v": v_bank}
        def self_sync(sp):
            def tokens(ap, b):
                return at(ap, b).rearrange("b t d -> (b t) d")

            def step(b, has):
                if has(2):
                    n = b + 2
                    if b.exists:
                        sp.wait_ge(xn_made.sem(b), xn_made.count(ph3, b))
                    sp.wait_ge(fy_stored, (n.pair + (fy_before["F2"] + 1)) * 16)
                    sp.dma_start(x_s[n.par][:], tokens(source[ph3], n)).then_inc(x3_loaded.sem(n), 16)
                if has(1):
                    n = b + 1
                    if (n + -2).exists:
                        sp.wait_ge(att3_made.sem(n + -2), att3_made.count(ph3, n + -2, 1))
                    mem = at(vmem_dram, n).rearrange("b (g k d) -> (b k) g d", k=4, d=KH)
                    for k in range(4):
                        sp.dma_start(vpre_s[n.par][PRE * k:PRE * k + NM, :, k, :],
                                     mem[k:k + 1].to_broadcast([NM, H // 4, KH])).then_inc(vpre_loaded.sem(n), 16)
                    if (n + -2).exists:
                        sp.wait_ge(y3_made.sem(n + -2), y3_made.count(ph3, n + -2))
                    sp.dma_start(xb_s[n.par][:], tokens(source[ph3], n)).then_inc(xr_loaded.sem(n), 16)
                if has(-1):
                    sp.wait_ge(y3_made.sem(b + -1), y3_made.count(ph3, b + -1))
                    sp.dma_start(tokens(target[ph3], b + -1), y_s[(b + -1).par][:]).then_inc(y3_stored.sem(b + -1), 16)
            drive(sp, NB, step, reach=2)

        def self_tensor(pe):
            made = {"q": q3_made, "k": k3_made, "v": v3_made}

            def project(b, what, h):
                col = "qkv".index(what) * HD3 + h * HALF
                before, other = (b if h else b + -1), 1 - h
                if what == "q" and h == 0:
                    pe.wait_ge(xnT_kept.sem(b), xnT_kept.count(ph3, b))
                elif what == "q":
                    pe.wait_ge(q3_roped.sem(b), q3_roped.count(ph3, b, 0))
                elif what == "k":
                    if before.exists:
                        pe.wait_ge(k3_roped.sem(before), k3_roped.count(ph3, before, other))
                    if h == 0 and (b + -2).exists:
                        pe.wait_ge(y3_made.sem(b + -2), y3_made.count(ph3, b + -2))
                elif what == "v" and (b + -1).exists:
                    pe.wait_ge(pT3_kept.sem(b + -1), pT3_kept.count(ph3, b + -1, 3 * h + 2))
                elif what == "v" and before.exists:
                    pe.wait_ge(v3_kept.sem(before), v3_kept.count(ph3, before, other))
                nc.tensor.matmul(IN[what][:], xnT_s[b.par][:], wqkv[:, col:col + HALF], start=True, stop=True)\
                    .then_inc(made[what].sem(b), 1)

            def turn(b, what, h):
                src_done, dst_done = (q3_turned, qT3_made) if what == "q" else (k3_turned, kT3_made)
                pe.wait_ge(src_done.sem(b), src_done.count(ph3, b, h))
                if (b + -1).exists:
                    pe.wait_ge(pT3_kept.sem(b + -1), pT3_kept.count(ph3, b + -1, 3 * h + "qk".index(what)))
                for c in range(HC):
                    mm = nc.tensor.transpose(turn3["qk".index(what)][:, c * T:(c + 1) * T], turned[what][h][:, c * 128:(c + 1) * 128], ident[:])
                mm.then_inc(dst_done.sem(b), 1)

            def scores(b, h):
                pe.wait_ge(qT3_kept.sem(b), qT3_kept.count(ph3, b, h))
                pe.wait_ge(kT3_kept.sem(b), kT3_kept.count(ph3, b, h))
                if h == 0:
                    pe.wait_ge(kpre_made.sem(b), kpre_made.count(ph3, b))
                old = b if h else b + -1
                if old.exists:
                    pe.wait_ge(shifted3.sem(old), shifted3.count(ph3, old, 1 - h))
                qT, kT = turnedT["q"][h], turnedT["k"][h]
                for s_bank in (s_even, s_odd):
                    nc.tensor.matmul(s_bank[:, 0:LOC], identb[:], tri[:], start=True, stop=False, skip_group_check=True)
                for c in range(HC):
                    nc.tensor.matmul(s_even[:, LOC + c * 2 * PRE:LOC + (c + 1) * 2 * PRE], qT[:, c * T:(c + 1) * T],
                                     kpre_s[b.par][:, h * HC + c, :], start=False, stop=False, skip_group_check=True)
                for c in range(HC):
                    for r, s_bank in enumerate((s_even, s_odd)):
                        rows = slice(r * KH, (r + 1) * KH)
                        for g in range(T // SEG):
                            own = slice(c * T + g * SEG, c * T + (g + 1) * SEG)
                            mm = nc.tensor.matmul(s_bank[g * SEG:(g + 1) * SEG, c * SEG:(c + 1) * SEG], qT[rows, own], kT[rows, own],
                                                  start=False, stop=(c == HC - 1), skip_group_check=True)
                mm.then_inc(s3_made.sem(b), 1)

            def transpose_p(b, h, more):
                pe.wait_ge(p3_made.sem(b), p3_made.count(ph3, b, h))
                pe.wait_ge(p3_second.sem(b), p3_second.count(ph3, b, h))
                after, follows = (b + 1 if h else b), more or h == 0
                for r in range(2):
                    if follows:
                        kept = (qT3_kept, kT3_kept)[r]
                        pe.wait_ge(kept.sem(after), kept.count(ph3, after, 1 - h))
                    for c in range(HC):
                        n = r * HC + c
                        mm = nc.tensor.transpose(turn3[r][:, c * T:(c + 1) * T], dense_s[h][:, n * T:(n + 1) * T], ident[:])
                    mm.then_inc(pT3_made.sem(b), 1)
                if follows:
                    pe.wait_ge(v3_kept.sem(after), v3_kept.count(ph3, after, 1 - h))
                for n in range(2):
                    mm = nc.tensor.transpose(v_bank[:, n * T:(n + 1) * T], pp_s[h][:, n * 128:(n + 1) * 128], ident[:])
                mm.then_inc(pT3_made.sem(b), 1)

            def attend(b, h):
                pe.wait_ge(pT3_kept.sem(b), pT3_kept.count(ph3, b, 3 * h + 2))
                pe.wait_ge(v3_kept.sem(b), v3_kept.count(ph3, b, h))
                if h == 0:
                    pe.wait_ge(vpre_loaded.sem(b), vpre_loaded.count(ph3, b))
                before = b if h else b + -1
                if before.exists:
                    pe.wait_ge(att3_kept.sem(before), att3_kept.count(ph3, before, 1 - h))
                for c in range(HC):
                    k = 2 * c % 4
                    nc.tensor.matmul(att3[:, c * T:(c + 1) * T], vpre_s[b.par][:, 2 * h + c // 2, k:k + 2, :],
                                     ppT_s[h][:, (c // 2) * T:(c // 2 + 1) * T], start=True, stop=False, skip_group_check=True)
                    for r in range(2):
                        n = r * HC + c
                        mm = nc.tensor.matmul(att3[r * KH:(r + 1) * KH, c * T:(c + 1) * T], v3_s[h][:, (2 * c + r) * KH:(2 * c + r + 1) * KH],
                                              denseT_s[h][:, n * T:(n + 1) * T], start=False, stop=True, skip_group_check=True)
                mm.then_inc(att3_made.sem(b), 1)

            def project_out(b, more):
                pe.wait_ge(att3_kept.sem(b), att3_kept.count(ph3, b, 1))
                if more:
                    pe.wait_ge(k3_roped.sem(b + 1), k3_roped.count(ph3, b + 1, 1))
                for c in range(H // 2):
                    mm = nc.tensor.matmul(k_bank[:, 0:D], att3_s[c // HC][:, (c % HC) * T:(c % HC + 1) * T], wout3[:, c, :],
                                          start=(c == 0), stop=(c == H // 2 - 1))
                mm.then_inc(proj3_made.sem(b), 1)

            def transpose_x(b):
                pe.wait_ge(xn_made.sem(b), xn_made.count(ph3, b))
                if (b + -1).exists:
                    pe.wait_ge(q3_roped.sem(b + -1), q3_roped.count(ph3, b + -1, 1))
                nc.tensor.transpose(q_bank[:, 0:T], xn_s[b.par][:], ident[:]).then_inc(xnT_made.sem(b), 1)

            def step(b, has):
                if has(0):
                    scores(b, 0)
                if has(-1):
                    transpose_p(b + -1, 1, has(0))
                if has(0):
                    project(b, "q", 1)
                    project(b, "k", 1)
                if has(-1):
                    attend(b + -1, 1)
                if has(0):
                    turn(b, "q", 1)
                if has(-1):
                    project_out(b + -1, has(0))
                if has(0):
                    turn(b, "k", 1)
                    project(b, "v", 1)
                if has(1):
                    transpose_x(b + 1)
                if has(0):
                    scores(b, 1)
                    transpose_p(b, 0, has(1))
                if has(1):
                    project(b + 1, "q", 0)
                    project(b + 1, "k", 0)
                if has(0):
                    attend(b, 0)
                if has(1):
                    turn(b + 1, "q", 0)
                    turn(b + 1, "k", 0)
                    project(b + 1, "v", 0)
            drive(pe, NB, step)

        def self_scalar(act):
            def keep_v(b, h):
                act.wait_ge(v3_made.sem(b), v3_made.count(ph3, b, h))
                if (b + -1).exists:
                    act.wait_ge(att3_made.sem(b + -1), att3_made.count(ph3, b + -1, h))
                nc.scalar.activation(v3_s[h][:], IN["v"][:], ACT.Copy).then_inc(v3_kept.sem(b), 1)

            def keep_turned(b, h):
                for what, done, kept in (("q", qT3_made, qT3_kept), ("k", kT3_made, kT3_kept)):
                    act.wait_ge(done.sem(b), done.count(ph3, b, h))
                    if (b + -1).exists:
                        act.wait_ge(s3_made.sem(b + -1), s3_made.count(ph3, b + -1, h))
                    nc.scalar.activation(turnedT[what][h][:], turn3["qk".index(what)][:], ACT.Copy).then_inc(kept.sem(b), 1)

            def keep_p(b, h):
                if (b + -1).exists:
                    act.wait_ge(att3_made.sem(b + -1), att3_made.count(ph3, b + -1, h))
                for r in range(2):
                    act.wait_ge(pT3_made.sem(b), pT3_made.count(ph3, b, 3 * h + r))
                    nc.scalar.activation(denseT_s[h][:, r * HC * T:(r + 1) * HC * T], turn3[r][:], ACT.Copy)\
                        .then_inc(pT3_kept.sem(b), 1)
                act.wait_ge(pT3_made.sem(b), pT3_made.count(ph3, b, 3 * h + 2))
                nc.scalar.activation(ppT_s[h][:], v_bank[:, 0:2 * T], ACT.Copy).then_inc(pT3_kept.sem(b), 1)

            def keep_att(b, h):
                act.wait_ge(att3_made.sem(b), att3_made.count(ph3, b, h))
                if (b + -1).exists:
                    act.wait_ge(proj3_made.sem(b + -1), proj3_made.count(ph3, b + -1))
                nc.scalar.activation(att3_s[h][:], att3[:], ACT.Copy).then_inc(att3_kept.sem(b), 1)

            def exps(b, h):
                act.wait_ge(shifted3.sem(b), shifted3.count(ph3, b, h))
                nc.scalar.activation(l_s[h][:], l_s[h][:], ACT.Exp, scale=KH ** -0.5)
                nc.scalar.activation(lp_s[h][:], lp_s[h][:], ACT.Exp, scale=KH ** -0.5).then_inc(exp3_made.sem(b), 1)

            def keep_xT(b):
                act.wait_ge(xnT_made.sem(b), xnT_made.count(ph3, b))
                if (b + -2).exists:
                    act.wait_ge(v3_made.sem(b + -2), v3_made.count(ph3, b + -2, 1))
                nc.scalar.activation(xnT_s[b.par][:], q_bank[:, 0:T], ACT.Copy).then_inc(xnT_kept.sem(b), 1)

            def step(b, has):
                if has(-1):
                    keep_p(b + -1, 1)
                if has(0):
                    exps(b, 0)
                if has(-1):
                    keep_att(b + -1, 1)
                if has(0):
                    keep_turned(b, 1)
                    keep_v(b, 1)
                if has(1):
                    keep_xT(b + 1)
                if has(0):
                    keep_p(b, 0)
                    exps(b, 1)
                    keep_att(b, 0)
                if has(1):
                    keep_turned(b + 1, 0)
                    keep_v(b + 1, 0)
            drive(act, NB, step)

        def by_half(ap, w):
            return ap.rearrange("p (n k) -> p n k", k=w)

        def swap_order(ap):
            return ap.rearrange("p (c r) -> p r c", r=2)

        def spread_segment(engine, h, g):
            rows = slice(g * SEG, (g + 1) * SEG)
            return engine.tensor_tensor(by_half(dense_s[h][rows, :], T)[:, :, g * SEG:(g + 1) * SEG], by_half(l_s[h][rows, :], SEG),
                                        spread(r_all[h][rows, :], SEG), ALU.mult)

        def self_vector(dve):
            def rope(b, what, h):
                done, roped = (q3_made, q3_roped) if what == "q" else (k3_made, k3_roped)
                dve.wait_ge(done.sem(b), done.count(ph3, b, h))
                if what == "q" and (b + -1).exists:
                    dve.wait_ge(q3_turned.sem(b + -1), q3_turned.count(ph3, b + -1, h))
                src = IN[what][:]
                nc.vector.tensor_tensor(by_half(ropeC[what][h][:], KH), by_half(src, KH),
                                        cos[:].unsqueeze(1).to_broadcast([T, 2 * HC, KH]), ALU.mult)
                pairs = src.rearrange("p (n f two) -> p n f two", two=2, f=KH // 2)
                swapped = ropeS[what][h][:].rearrange("p (n f two) -> p n f two", two=2, f=KH // 2)
                factor = sin[:].rearrange("p (f two) -> p f two", two=2)
                for k in range(2):
                    ins = nc.vector.tensor_tensor(swapped[:, :, :, k], pairs[:, :, :, 1 - k],
                                                  factor[:, :, k].unsqueeze(1).to_broadcast([T, 2 * HC, KH // 2]), ALU.mult)
                ins.then_inc(roped.sem(b), 1)
                if what == "k":
                    dve.wait_ge(k3_roped.sem(b), k3_roped.count(ph3, b, h))
                    if (b + -1).exists:
                        dve.wait_ge(kT3_made.sem(b + -1), kT3_made.count(ph3, b + -1, h))
                    nc.vector.tensor_tensor(turned[what][h][:], ropeC[what][h][:], ropeS[what][h][:], ALU.add).then_inc(k3_turned.sem(b), 1)

            def shift(b, h):
                dve.wait_ge(s3_made.sem(b), s3_made.count(ph3, b, h))
                for r, s_bank in enumerate((s_even, s_odd)):
                    nc.vector.tensor_reduce(m_loc[h][:, r * HC:(r + 1) * HC], by_half(s_bank[:, 0:LOC], SEG), AX.X, ALU.max)
                prefix = s_even[:, LOC:LOC + 2 * HC * PRE]
                nc.vector.tensor_reduce(m_pre[h][:], by_half(prefix, PRE), AX.X, ALU.max).then_inc(max3_parts.sem(b), 1)
                dve.wait_ge(max3_parts.sem(b), max3_parts.count(ph3, b, h))
                nc.vector.tensor_tensor(m_all[h][:].rearrange("p (r c) -> p r c", r=2), m_loc[h][:].rearrange("p (r c) -> p r c", r=2),
                                        swap_order(m_pre[h][:]), ALU.max).then_inc(max3_made.sem(b), 1)
                dve.wait_ge(max3_made.sem(b), max3_made.count(ph3, b, h))
                if (b + -1).exists:
                    dve.wait_ge(p3_made.sem(b + -1), p3_made.count(ph3, b + -1, h))
                for r, s_bank in enumerate((s_even, s_odd)):
                    nc.vector.tensor_tensor(by_half(l_s[h][:, r * LOC:(r + 1) * LOC], SEG), by_half(s_bank[:, 0:LOC], SEG),
                                            spread(m_all[h][:, r * HC:(r + 1) * HC], SEG), ALU.subtract)
                for r in range(2):
                    pre_r = lambda ap: ap.rearrange("p (c r k) -> p r c k", r=2, k=PRE)[:, r]
                    ins = nc.vector.tensor_tensor(pre_r(lp_s[h][:]), pre_r(prefix), spread(m_all[h][:, r * HC:(r + 1) * HC], PRE), ALU.subtract)
                ins.then_inc(shifted3.sem(b), 1)

            def denominators(b, h):
                dve.wait_ge(exp3_made.sem(b), exp3_made.count(ph3, b, h))
                nc.vector.tensor_reduce(d_loc[h][:], by_half(l_s[h][:], SEG), AX.X, ALU.add)
                nc.vector.tensor_reduce(d_pre[h][:], by_half(lp_s[h][:], PRE), AX.X, ALU.add).then_inc(den3_parts.sem(b), 1)
                dve.wait_ge(den3_parts.sem(b), den3_parts.count(ph3, b, h))
                nc.vector.tensor_tensor(d_all[h][:].rearrange("p (r c) -> p r c", r=2), d_loc[h][:].rearrange("p (r c) -> p r c", r=2),
                                        swap_order(d_pre[h][:]), ALU.add).then_inc(den3_sum.sem(b), 1)
                dve.wait_ge(den3_sum.sem(b), den3_sum.count(ph3, b, h))
                if (b + -1).exists:
                    dve.wait_ge(p3_made.sem(b + -1), p3_made.count(ph3, b + -1, h))
                nc.vector.reciprocal(r_all[h][:], d_all[h][:]).then_inc(den3_inv.sem(b), 1)
                dve.wait_ge(den3_inv.sem(b), den3_inv.count(ph3, b, h))
                if (b + -1).exists:
                    dve.wait_ge(pT3_made.sem(b + -1), pT3_made.count(ph3, b + -1, 3 * h + 1))
                spread_segment(nc.vector, h, 1).then_inc(p3_second.sem(b), 1)

            def squares(b):
                dve.wait_ge(x3_loaded.sem(b), x3_loaded.count(ph3, b))
                if (b + -2).exists:
                    dve.wait_ge(rms_made.sem(b + -2), rms_made.count(ph3, b + -2))
                nc.vector.tensor_tensor_reduce(sq_s[b.par][:], x_s[b.par][:], x_s[b.par][:], 1.0 / D, RMS_EPS, ALU.mult, ALU.add,
                                               var_s[b.par][:]).then_inc(sq_made.sem(b), 1)

            def norm(b):
                dve.wait_ge(rms_made.sem(b), rms_made.count(ph3, b))
                if (b + -2).exists:
                    dve.wait_ge(xnT_made.sem(b + -2), xnT_made.count(ph3, b + -2))
                nc.vector.tensor_scalar(xn_s[b.par][:], x_s[b.par][:], rstd_s[b.par][:, 0:1], None, ALU.mult).then_inc(xn_made.sem(b), 1)

            def residual(b):
                dve.wait_ge(proj3_made.sem(b), proj3_made.count(ph3, b))
                dve.wait_ge(xr_loaded.sem(b), xr_loaded.count(ph3, b))
                if (b + -2).exists:
                    dve.wait_ge(y3_stored.sem(b + -2), y3_stored.count(ph3, b + -2))
                nc.vector.tensor_tensor(y_s[b.par][:], k_bank[:, 0:D], xb_s[b.par][:], ALU.add).then_inc(y3_made.sem(b), 1)

            def step(b, has):
                if has(1):
                    squares(b + 1)
                if has(0):
                    shift(b, 0)
                    rope(b, "q", 1)
                if has(1):
                    norm(b + 1)
                if has(0):
                    rope(b, "k", 1)
                    denominators(b, 0)
                if has(-1):
                    residual(b + -1)
                if has(0):
                    shift(b, 1)
                if has(1):
                    rope(b + 1, "q", 0)
                    rope(b + 1, "k", 0)
                if has(0):
                    denominators(b, 1)
            drive(dve, NB, step)

        def self_gpsimd(pool):
            def add_queries(b, h):
                pool.wait_ge(q3_roped.sem(b), q3_roped.count(ph3, b, h))
                if (b + -1).exists:
                    pool.wait_ge(qT3_made.sem(b + -1), qT3_made.count(ph3, b + -1, h))
                nc.gpsimd.tensor_tensor(turned["q"][h][:], ropeC["q"][h][:], ropeS["q"][h][:], ALU.add).then_inc(q3_turned.sem(b), 1)

            def normalise(b, h):
                pool.wait_ge(den3_inv.sem(b), den3_inv.count(ph3, b, h))
                if (b + -1).exists:
                    pool.wait_ge(pT3_made.sem(b + -1), pT3_made.count(ph3, b + -1, 3 * h + 2))
                spread_segment(nc.gpsimd, h, 0).then_inc(p3_rows.sem(b), 1)
                pool.wait_ge(p3_rows.sem(b), p3_rows.count(ph3, b, h))
                for r in range(2):
                    pre_r = lambda ap: ap.rearrange("p (c r k) -> p r c k", r=2, k=PRE)[:, r]
                    ins = nc.gpsimd.tensor_tensor(pre_r(pp_s[h][:]), pre_r(lp_s[h][:]), spread(r_all[h][:, r * HC:(r + 1) * HC], PRE), ALU.mult)
                ins.then_inc(p3_made.sem(b), 1)

            def rms(b):
                pool.wait_ge(sq_made.sem(b), sq_made.count(ph3, b))
                if (b + -2).exists:
                    pool.wait_ge(xn_made.sem(b + -2), xn_made.count(ph3, b + -2))
                nc.gpsimd.tensor_tensor(rstd_s[b.par][:], var_s[b.par][:], minus_half[:, 0:1], ALU.pow).then_inc(rms_made.sem(b), 1)

            def prefix_keys(b):
                if (b + -2).exists:
                    pool.wait_ge(s3_made.sem(b + -2), s3_made.count(ph3, b + -2, 1))
                mem = kmemT[:, :, bass.ds(b.pair * 2 + b.par, 1)].unsqueeze(2).to_broadcast([128, H // 2, 2, NM])
                own = halfmask[:].unsqueeze(1).unsqueeze(3).to_broadcast([128, H // 2, 2, NM])
                nc.gpsimd.tensor_tensor(kpre_s[b.par][:].rearrange("p c (r k) -> p c r k", r=2)[:, :, :, 0:NM], mem, own, ALU.mult)\
                    .then_inc(kpre_made.sem(b), 1)

            def step(b, has):
                if has(1):
                    rms(b + 1)
                if has(0):
                    add_queries(b, 1)
                    normalise(b, 0)
                if has(1):
                    prefix_keys(b + 1)
                    add_queries(b + 1, 0)
                if has(0):
                    normalise(b, 1)
            drive(pool, NB, step)

        with_self = "A3" in order
        pooled = slots("pooled", [NB, D], n=5)
        pool_var = slots("pool_var", [NB, 1], n=3)
        poolT = sb("poolT", [D, NB])
        memT = sb("memT", [D, NB])
        vmem_sb = sb("vmem", [NB, HD3])
        pool_step = sem("pool_step")
        mem_ctx_loaded = sem("mem_ctx_loaded")

        def memory_vector(dve):
            total, mean, square, normed, scaled = pooled
            dve.wait_ge(mem_ctx_loaded, 16)
            nc.vector.tensor_reduce(total[:], ctx_all[:].rearrange("b (k d) -> b d k", d=D), AX.X, ALU.add).then_inc(pool_step, 1)
            dve.wait_ge(pool_step, 1)
            nc.vector.tensor_scalar(mean[:], total[:], 1.0 / C, None, ALU.mult).then_inc(pool_step, 1)
            dve.wait_ge(pool_step, 2)
            nc.vector.tensor_tensor_reduce(square[:], mean[:], mean[:], 1.0, 0.0, ALU.mult, ALU.add, pool_var[0][:]).then_inc(pool_step, 1)
            dve.wait_ge(pool_step, 5)
            nc.vector.tensor_scalar(normed[:], mean[:], pool_var[2][:, 0:1], None, ALU.mult).then_inc(pool_step, 1)
            dve.wait_ge(pool_step, 6)
            nc.vector.tensor_tensor(scaled[:], normed[:], pool_norm[0:NB, :], ALU.mult).then_inc(pool_step, 1)
            dve.wait_ge(mem_kv, 1)
            nc.vector.tensor_scalar(wqkv[:], wqkv[:], attn_norm[:, 0:1], None, ALU.mult).then_inc(weights_scaled, 1)
            nc.vector.tensor_scalar(w1g[:], w1g[:], ff_norm[:, 0:1], None, ALU.mult).then_inc(weights_scaled, 1)
            dve.wait_ge(weights_scaled, 2)

        def memory_gpsimd(pool):
            pool.wait_ge(pool_step, 3)
            nc.gpsimd.tensor_scalar(pool_var[1][:], pool_var[0][:], 1.0 / D, RMS_EPS, ALU.mult, ALU.add).then_inc(pool_step, 1)
            pool.wait_ge(pool_step, 4)
            nc.gpsimd.tensor_tensor(pool_var[2][:], pool_var[1][:], minus_half[0:NB, 0:1], ALU.pow).then_inc(pool_step, 1)

        def memory_tensor(pe):
            pe.wait_ge(pool_step, 7)
            nc.tensor.transpose(bank[0][:, 0:NB], pooled[4][:], ident[0:NB, 0:NB]).then_inc(mem_poolT, 1)
            pe.wait_ge(mem_poolT_kept, 1)
            nc.tensor.matmul(bank[1][:, 0:NB], wmem[:], poolT[:], start=True, stop=True).then_inc(mem_tok, 1)
            pe.wait_ge(mem_tok_kept, 1)
            for c in range(H // 2):
                nc.tensor.matmul(bank[2][:, c * NB:(c + 1) * NB], wqkv[:, HD3 + c * 128:HD3 + (c + 1) * 128], memT[:], start=True, stop=True)
            for n in range(2):
                mm = nc.tensor.matmul(bank[3 + n][0:NB, :], memT[:], wqkv[:, 2 * HD3 + n * 512:2 * HD3 + (n + 1) * 512], start=True, stop=True)
            mm.then_inc(mem_kv, 1)
            pe.wait_ge(mem_kv_kept, 3)
            pe.wait_ge(weights_scaled, 2)

        def memory_scalar(act):
            act.wait_ge(mem_poolT, 1)
            nc.scalar.activation(poolT[:], bank[0][:, 0:NB], ACT.Copy).then_inc(mem_poolT_kept, 1)
            act.wait_ge(mem_tok, 1)
            nc.scalar.activation(memT[:], bank[1][:, 0:NB], ACT.Copy).then_inc(mem_tok_kept, 1)
            act.wait_ge(mem_kv, 1)
            nc.scalar.activation(kmemT[:].rearrange("p c b -> p (c b)"), bank[2][:, 0:H // 2 * NB], ACT.Copy).then_inc(mem_kv_kept, 1)
            for n in range(2):
                nc.scalar.activation(vmem_sb[:, n * 512:(n + 1) * 512], bank[3 + n][0:NB, :], ACT.Copy).then_inc(mem_kv_kept, 1)

        def memory_sync(sp):
            sp.wait_ge(mem_kv_kept, 3)
            sp.dma_start(vmem_dram, vmem_sb[:]).then_inc(mem_stored, 16)
            sp.wait_ge(mem_stored, 16)

        def phases(eng, by_cross, by_ff, by_self):
            for ph in order:
                if ph in cross:
                    by_cross(eng, ph)
                elif ph[0] == "F":
                    by_ff(eng, ph)
                else:
                    by_self(eng)

        block = ctx.enter_context(nc.Block())

        N_ZERO = 11

        @block.sync
        def _(sp):
            sp.dma_start(ctx_all[:], a["ctx"]).then_inc(mem_ctx_loaded, 16)
            for dst, src in consts:
                sp.dma_start(dst[:], src).then_inc(loaded, 16)
            sp.wait_ge(zeroed, N_ZERO)
            for s in range(2):
                for r in range(2):
                    sp.dma_start(kpre_s[s][r * KH:(r + 1) * KH, :, r * PRE + NM:(r + 1) * PRE], a["persistT"][r]).then_inc(loaded, 16)
                for k in range(4):
                    sp.dma_start(vpre_s[s][PRE * k + NM:PRE * (k + 1), :, k, :], a["persist"][k]).then_inc(loaded, 16)
            memory_sync(sp)
            phases(sp, cross_sync, ff_sync, self_sync)
            for slot in range(2):
                sp.wait_ge(y_stored.sems[slot], y_stored.total_count)
                sp.wait_ge(y3_stored.sems[slot], y3_stored.total_count)
            sp.wait_ge(fy_stored, 16 * GROUPS * len(FFS))

        @block.tensor
        def _(pe):
            pe.wait_ge(loaded, 16 * N_LOADS)
            pe.wait_ge(zeroed, N_ZERO)
            pe.wait_ge(masks_made, 3)
            memory_tensor(pe)
            phases(pe, cross_tensor, ff_tensor, self_tensor)

        @block.scalar
        def _(act):
            act.wait_ge(loaded, 16 * N_LOADS)
            memory_scalar(act)
            phases(act, cross_scalar, ff_scalar, self_scalar)

        @block.vector
        def _(dve):
            for s in range(2):
                nc.vector.memset(v_s[s][:], 0.0).then_inc(setup, 1)
                nc.vector.memset(dense_s[s][:], 0.0).then_inc(zeroed, 1)
                nc.vector.memset(kpre_s[s][:], 0.0).then_inc(zeroed, 1)
                nc.vector.memset(vpre_s[s][:], 0.0).then_inc(zeroed, 1)
            dve.wait_ge(setup, 2)
            for s in range(2):
                nc.vector.memset(v_s[s][:].rearrange("p (h v) -> p h v", v=VP)[:, :, DH:DH + 1], 1.0).then_inc(zeroed, 1)
            nc.vector.memset(onesb[:], 1.0).then_inc(zeroed, 1)
            nc.vector.memset(minus_half[:], -0.5).then_inc(zeroed, 1)
            nc.vector.memset(ln_eps[:], LN_EPS).then_inc(zeroed, 1)
            dve.wait_ge(loaded, 16 * N_LOADS)
            dve.wait_ge(zeroed, N_ZERO)
            nc.vector.tensor_copy(identb[:], ident[:]).then_inc(masks_made, 1)
            nc.vector.tensor_copy(causal[:], causal32).then_inc(masks_made, 1)
            nc.vector.tensor_copy(tri[:], tri32).then_inc(masks_made, 1)
            memory_vector(dve)
            phases(dve, cross_vector, ff_vector, self_vector)

        @block.gpsimd
        def _(pool):
            pool.wait_ge(loaded, 16 * N_LOADS)
            pool.wait_ge(zeroed, N_ZERO)
            memory_gpsimd(pool)
            phases(pool, cross_gpsimd, ff_gpsimd, self_gpsimd)


def lay_out(i):
    f = lambda x: np.ascontiguousarray(np.asarray(x))
    NB = i["x"].shape[0]
    a = {"x": f(i["x"]), "ctx": f(i["ctx_1024"]).reshape(NB, C * D)}
    a["ctxT"] = f(np.transpose(i["ctx_1024"], (0, 2, 1)))
    a["side"] = f(np.transpose(i["fside_Bx16xSxS2_0"], (0, 2, 1, 3))).reshape(NB, T, H * C)
    a["mask"] = f(np.transpose(i["mask_Bx16xSxS2_bk0"], (0, 2, 1, 3))).reshape(NB, T, H * C)
    a["keymask"] = f(i["mask_Bx1x1xS2_if1"]).reshape(NB, C)
    for p in ("L0_xattn_", "L1_xattn_"):
        for k in "qkv":
            a[f"{p}w{k}"] = f(np.transpose(i[f"{p}W{k}"]))
            a[f"{p}b{k}"] = f(i[f"{p}b{k}"])
    p = "L0_xattn_"
    a[p + "ln_g"], a[p + "ln_b"] = f(i[p + "ln_g"]), f(i[p + "ln_b"])
    a[p + "ffw1"] = f(np.transpose(i[p + "W1"]))
    a[p + "ffb1"] = f(np.transpose(np.reshape(i[p + "b1"], (NF, 128))))
    a[p + "ffw2"] = f(np.transpose(np.reshape(np.transpose(i[p + "W2"]), (NF, 128, D)), (1, 0, 2)))
    a[p + "ffb2"] = f(i[p + "b2"])
    p = "L1_xattn_"
    a[p + "wo"], a[p + "bo"] = f(np.transpose(i[p + "Wo"])), f(i[p + "bo"])
    a[p + "ln_g"], a[p + "ln_b"] = f(i[p + "gamma"]), f(i[p + "beta"])
    p = "L2_xattn_"
    for k in "qkv":
        w = np.zeros((D, D), np.float32)
        for h in range(H):
            w[h * DH:(h + 1) * DH, h * DH:(h + 1) * DH] = i[f"{p}w{k}"]
        a[f"{p}w{k}"] = w
    a[p + "wo"], a[p + "bo"] = f(i[p + "w_out"]), f(i[p + "b_out"])
    a[p + "ln_g"], a[p + "ln_b"] = f(i[p + "g1"]), f(i[p + "beta1"])
    a[p + "ffw1"] = f(i[p + "w_ff1"])
    a[p + "ffb1"] = f(np.transpose(np.reshape(i[p + "b_ff1"], (NF, 128))))
    a[p + "ffw2"] = f(np.transpose(np.reshape(i[p + "w_ff2"], (NF, 128, D)), (1, 0, 2)))
    a[p + "ffb2"] = f(i[p + "b_ff2"])
    a[p + "g2"], a[p + "beta2"] = f(i[p + "g2"]), f(i[p + "beta2"])
    p = "L3_xattn_"
    for k in ("attn_norm_w", "to_qkv_w", "to_out_w", "mem_pool_norm_w", "to_mem_tokens_w", "ff_norm_w", "ff_b2"):
        a[p + k] = f(i[p + k])
    w1, b1, w2 = (np.asarray(i[p + k]) for k in ("ff_w1", "ff_b1", "ff_w2"))
    pw1 = np.zeros((D, 2, NG * 128), np.float32)
    pw1[:, 0, :DG], pw1[:, 1, :DG] = w1[:, :DG], w1[:, DG:]
    a[p + "ffw1"] = pw1.reshape(D, 2 * NG * 128)
    pb1 = np.zeros((2, NG * 128), np.float32)
    pb1[0, :DG], pb1[1, :DG] = b1[:DG], b1[DG:]
    a[p + "ffb1"] = f(np.transpose(pb1.reshape(2 * NG, 128)))
    pw2 = np.zeros((NG * 128, D), np.float32)
    pw2[:DG] = w2
    a[p + "ffw2"] = f(np.transpose(pw2.reshape(NG, 128, D), (1, 0, 2)))
    pm = np.asarray(i[p + "persist_mem"])
    a["persistT"] = f(np.transpose(pm.reshape(H // 2, 2, NPM, KH), (1, 3, 0, 2)))
    a["persist"] = f(np.transpose(pm.reshape(H // 4, 4, NPM, KH), (1, 2, 0, 3)))

    a["c_ident"] = np.eye(128, dtype=np.float32)
    later = np.arange(C)[None, :] > np.arange(T)[:, None]
    a["c_causal"] = np.tile(np.where(later, -1.0e9, 0.0), (1, QH)).astype(np.float32)
    later = np.arange(SEG)[None, :] > (np.arange(T) % SEG)[:, None]
    a["c_tri"] = np.tile(np.where(later, -1.0e30, 0.0), (1, HC)).astype(np.float32)
    a["c_headmask"] = (np.arange(D)[:, None] // DH == np.arange(H)[None, :]).astype(np.float32)
    a["c_halfmask"] = (np.arange(128)[:, None] // KH == np.arange(2)[None, :]).astype(np.float32)
    inv = (np.float32(1.0) / np.float32(10000.0) ** (np.arange(0, KH, 2, dtype=np.float32) / np.float32(KH))).astype(np.float32)
    angle = np.repeat(np.arange(T, dtype=np.float32)[:, None] * inv[None, :], 2, axis=-1)
    a["c_cos"] = np.cos(angle).astype(np.float32)
    a["c_sin"] = (np.sin(angle) * np.tile([-1.0, 1.0], KH // 2)[None, :]).astype(np.float32)
    return a


def kernel(**inputs):
    import concourse.bacc as bacc
    from concourse.bass_utils import run_bass_kernel_spmd

    nc = bacc.Bacc("TRN2", target_bir_lowering=False, num_devices=1)
    arrays = {"in_" + k: v for k, v in lay_out(inputs).items()}
    aps = {k[3:]: nc.dram_tensor(k, v.shape, mybir.dt.from_np(v.dtype), kind="ExternalInput").ap() for k, v in arrays.items()}
    out = nc.dram_tensor("out", inputs["x"].shape, F32, kind="ExternalOutput").ap()
    build_layers(nc, aps, out)
    return run_bass_kernel_spmd(nc, [arrays], core_ids=[0]).results[0]["out"]
```

```python
from contextlib import ExitStack
from dataclasses import dataclass

import numpy as np

import concourse.bass as bass
from concourse import mybir

F32 = mybir.dt.float32
BF16 = mybir.dt.bfloat16
I32 = mybir.dt.int32
U8 = mybir.dt.uint8
ACT = mybir.ActivationFunctionType
ALU = mybir.AluOpType
AX = mybir.AxisListType

T = 128
D = 128
C = 77
H = 16
DH = D // H
QH = 4
NQ = H // QH
QC = QH * C
VP = 32
FF = 512
NF = FF // 128
GB = 2
DG = 341
NG = 3
KH = 64
HD3 = H * KH
SEG = 64
NM = 16
NPM = 16
PRE = NM + NPM
HC = 4
LN_EPS = 1e-5
RMS_EPS = 1.1920929e-07
UNROLL = 2
MASKED = -3.0e38


@dataclass(frozen=True)
class Batch:

    pair: object
    par: int

    @property
    def exists(self):
        return not isinstance(self.pair, int) or self.pair >= 0

    @property
    def first(self):
        return isinstance(self.pair, int) and (self.pair, self.par) == (0, 0)

    def __add__(self, k):
        p = self.par + k
        return Batch(self.pair + p // 2 if p // 2 else self.pair, p % 2)


class Event:

    def __init__(self, new_semaphore, name, phases, parts=1, transfers=0):
        self.parts, self.transfers = parts, transfers
        self.sems = [new_semaphore(f"{name}_{s}") for s in range(2)] if transfers else [new_semaphore(name)]
        self.before, self.total = {}, 0
        for phase, batches in phases:
            self.before[phase] = self.total
            self.total += batches

    def sem(self, b):
        return self.sems[b.par if self.transfers else 0]

    def count(self, phase, b, part=0):
        before = self.before[phase]
        if self.transfers:
            return (b.pair + (before // 2 + 1)) * (16 * self.transfers)
        return b.pair * (2 * self.parts) + ((b.par + before) * self.parts + part + 1)

    @property
    def total_count(self):
        return self.total // 2 * 16 * self.transfers


def drive(eng, n, step, reach=1, ahead=None, begun=False):
    lo, hi = 2 * reach, n - 2
    static = lambda t: step(Batch(t // 2, t % 2), lambda k: 0 <= t + k < n)
    for t in range(0 if begun else -reach, lo):
        static(t)
    hi -= (hi - lo) % (2 * UNROLL)
    with eng.Fori(lo // 2, hi // 2 - UNROLL + 1, UNROLL) as i:
        for t in range(2 * UNROLL):
            step(Batch(i, 0) + t, lambda k: True)
    for t in range(hi, n + reach):
        if ahead and t >= n:
            ahead(t - n - reach)
        static(t)


def at(ap, b, per=1):
    return ap[bass.ds((b.pair * 2 + b.par) * per, per)]


def build_layers(nc, a, out):
    NB = a["x"].shape[0]
    PAIRS = NB // 2
    GROUPS = NB // GB
    with ExitStack() as ctx:
        def sb(name, shape, dt=F32):
            return ctx.enter_context(nc.sbuf_tensor("sb_" + name, shape, dt))

        def slots(name, shape, dt=F32, n=2):
            return [sb(f"{name}{s}", shape, dt) for s in range(n)]

        def sem(name):
            return ctx.enter_context(nc.semaphore(name))

        def scratch(name, shape):
            return nc.dram_tensor("scratch_" + name, shape, F32, kind="Internal").ap()

        bank = [ctx.enter_context(nc.psum_tensor(f"bank{i}", [128, 512], F32)) for i in range(8)]

        order = ["A0", "F0", "A1", "A2", "F2", "A3", "F3"]
        source, target = {}, {}
        held = a["x"]
        for ph in order:
            source[ph] = held
            held = out if ph == order[-1] else scratch("after_" + ph, [NB, T, D])
            target[ph] = held
        vmem_dram = scratch("vmem", [NB, HD3])

        ident = sb("ident", [128, 128])
        identb = sb("identb", [128, 128], BF16)
        causal = sb("causal", [T, QC], BF16)
        tri = sb("tri", [T, HC * SEG], BF16)
        headmask = sb("headmask", [D, H])
        halfmask = sb("halfmask", [D, 2])
        cos = sb("cos", [T, KH])
        sin = sb("sin", [T, KH])
        onesb = sb("onesb", [1, T], BF16)
        minus_half = sb("minus_half", [128, GB])
        ln_eps = sb("ln_eps", [128, GB])
        consts = [(ident, a["c_ident"]), (headmask, a["c_headmask"])]

        def weight(name, shape, src):
            w = sb(name, shape)
            consts.append((w, src))
            return w

        def row_everywhere(name):
            n = a[name].shape[0]
            return weight(name, [128, n], a[name].partition_broadcast(128))

        def column(name):
            return weight(name, [128, 1], a[name].rearrange("(p a) -> p a", a=1))

        cross = {}
        for ph, p in (("A0", "L0_xattn_"), ("A1", "L1_xattn_"), ("A2", "L2_xattn_")):
            w = {k: weight(p + k, [D, D], a[p + k]) for k in ("wq", "wk", "wv")}
            if ph != "A2":
                w |= {k: column(p + k) for k in ("bq", "bk")}
                w["bv"] = row_everywhere(p + "bv")
            if ph == "A0":
                w["bo"] = w["bv"]
            else:
                w["wo"] = weight(p + "wo", [D, D], a[p + "wo"])
                w["bo"] = row_everywhere(p + "bo")
            w |= {k: row_everywhere(p + k) for k in ("ln_g", "ln_b")}
            cross[ph] = w
            if ph == "A0":
                first_loads = consts
                consts = [(halfmask, a["c_halfmask"]), (cos, a["c_cos"]), (sin, a["c_sin"])]
        ffw = {}
        for ph, p in (("F0", "L0_xattn_"), ("F2", "L2_xattn_")):
            ffw[ph] = {
                "w1": weight(p + "ffw1", [D, FF], a[p + "ffw1"]),
                "b1": weight(p + "ffb1", [128, NF], a[p + "ffb1"]),
                "w2": weight(p + "ffw2", [128, NF, D], a[p + "ffw2"]),
                "b2": row_everywhere(p + "ffb2"),
            }
        ffw["F2"] |= {"g": row_everywhere("L2_xattn_g2"), "b": row_everywhere("L2_xattn_beta2")}
        p = "L3_xattn_"
        wqkv = weight("wqkv", [D, 3 * HD3], a[p + "to_qkv_w"])
        wout3 = weight("wout3", [128, H // 2, D], a[p + "to_out_w"].rearrange("(c p) d -> p c d", p=128))
        attn_norm = column(p + "attn_norm_w")
        ff_norm = column(p + "ff_norm_w")
        pool_norm = row_everywhere(p + "mem_pool_norm_w")
        wmem = weight("wmem", [D, D], a[p + "to_mem_tokens_w"])
        w1g = weight("w1g", [D, 2 * NG * 128], a[p + "ffw1"])
        b1g = weight("b1g", [128, 2 * NG], a[p + "ffb1"])
        w2g = weight("w2g", [128, NG, D], a[p + "ffw2"])
        b2g = row_everywhere(p + "ff_b2")

        REGION = C * D
        region = sb("region", [128, REGION])

        class Carve:

            def __init__(self):
                self.used = 0

            def __call__(self, rows, cols):
                view = region[0:rows, self.used:self.used + cols]
                self.used += cols
                assert self.used <= REGION
                return view

            def slots(self, rows, cols, n=2):
                return [self(rows, cols) for _ in range(n)]

        carve = Carve()
        x_s = slots("x", [T, D])
        ctx_s = slots("ctx", [D, C])
        side_s = carve.slots(T, H * C)
        mask_s = slots("mask", [T, H * C], U8)
        keymask_s = slots("keymask", [1, C], I32)
        keybias_s = slots("keybias", [1, C], BF16)
        xT_s = slots("xT", [D, T])
        qT_s = slots("qT", [D, T])
        kT_s = slots("kT", [D, C])
        kblk_s = carve.slots(D, H * C)
        v_s = slots("v", [C, H * VP])
        xb_s = slots("xb", [T, D])
        prod_s = carve.slots(T, QC)
        scored_s = carve.slots(T, QC, n=NQ)
        shifted_s = carve.slots(T, QC, n=NQ)
        p_s = carve.slots(T, QC)
        pT_s = slots("pT", [C, QH * T])
        max_s = slots("max", [T, QH], n=NQ)
        att_s = carve.slots(128, NQ * T)
        rden_s = slots("rden", [T, H])
        o_s = slots("o", [T, D])
        oT_s = slots("oT", [D, T])
        t_s = slots("t", [T, D])
        stats_s = slots("stats", [T, 6])
        mv_s = slots("mv", [T, 2])
        var_s = slots("var", [T, 1])
        rstd_s = slots("rstd", [T, 1])
        z_s = slots("z", [T, D])
        zg_s = slots("zg", [T, D])
        y_s = slots("y", [T, D])

        fx_s = slots("fx", [T, GB, D])
        fxT_s = slots("fxT", [D, GB * T])
        fh_s = slots("fh", [128, NF, GB * T])
        fg_s = fh_s
        fsilu_s = slots("fsilu", [128, NG, GB * T])
        fxb_s = slots("fxb", [T, GB, D])
        ft_s = slots("ft", [T, GB, D])
        fc_s = slots("fc", [T, GB, D])
        fz_s = slots("fz", [T, GB, D])
        fn_s = slots("fn", [T, GB, D])
        fy_s = slots("fy", [T, GB, D])
        fsq_s = slots("fsq", [T, D])
        fstats_s = slots("fstats", [T, GB, 6])
        fmv_s = slots("fmv", [T, GB, 2])
        fvar_s = slots("fvar", [T, GB])
        frstd_s = slots("frstd", [T, GB])

        sumT = sb("sumT", [D, NB])
        kmemT = sb("kmemT", [128, H // 2, NB])
        carve = Carve()
        sq_s = slots("sq", [T, D])
        xn_s = slots("xn", [T, D])
        xnT_s = slots("xnT", [D, T])
        ropeC = {k: carve.slots(T, HC * 2 * KH) for k in "qk"}
        ropeS = {k: carve.slots(T, HC * 2 * KH) for k in "qk"}
        turned = {k: carve.slots(T, HC * 2 * KH) for k in "qk"}
        turnedT = {k: carve.slots(128, HC * T) for k in "qk"}
        v3_s = carve.slots(T, HC * 2 * KH)
        kpre_s = slots("kpre", [128, H // 2, 2 * PRE])
        vpre_s = slots("vpre", [128, H // 4, 4, KH])
        l_s = slots("l", [T, 2 * HC * SEG])
        lp_s = slots("lp", [T, 2 * HC * PRE])
        m_loc = slots("m_loc", [T, 2 * HC])
        m_pre = slots("m_pre", [T, 2 * HC])
        m_all = slots("m_all", [T, 2 * HC])
        d_loc = slots("d_loc", [T, 2 * HC])
        d_pre = slots("d_pre", [T, 2 * HC])
        d_all = slots("d_all", [T, 2 * HC])
        r_all = slots("r_all", [T, 2 * HC])
        dense_s = slots("dense", [T, 2 * HC * T])
        pp_s = slots("pp", [T, 2 * HC * PRE])
        denseT_s = slots("denseT", [T, 2 * HC * T])
        causal32, tri32 = denseT_s[0][:, 0:QC], denseT_s[1][:, 0:HC * SEG]
        first_loads.append((causal32, a["c_causal"]))
        consts.append((tri32, a["c_tri"]))
        ppT_s = slots("ppT", [128, 2 * T])
        att3_s = slots("att3", [128, HC * T])

        loaded = sem("loaded")
        masks_made = sem("masks_made")
        setup = sem("setup_chain")
        mem_poolT = sem("mem_poolT")
        mem_poolT_kept = sem("mem_poolT_kept")
        mem_tok = sem("mem_tok")
        mem_tok_kept = sem("mem_tok_kept")
        mem_kv = sem("mem_kv")
        mem_kv_kept = sem("mem_kv_kept")
        mem_stored = sem("mem_stored")
        weights_scaled = sem("weights_scaled")
        zeroed = sem("zeroed")
        first_loaded = sem("first_loaded")
        presets = sem("presets")
        N_LOADS = len(consts) + 12

        def event(name, phases, parts=1, transfers=0):
            return Event(sem, name, [(ph, NB if ph[0] == "A" else GROUPS) for ph in phases], parts, transfers)

        CROSS = ["A0", "A1", "A2"]
        X_loaded = event("X_loaded", CROSS, transfers=1)
        ctx_loaded = event("ctx_loaded", CROSS, transfers=1)
        weights_loaded = event("weights_loaded", ["A1"], transfers=2)
        keymask_loaded = event("keymask_loaded", ["A2"], transfers=1)
        keybias_made = event("keybias_made", ["A2"])
        kv_made = event("kv_made", CROSS)
        ctx_summed = event("ctx_summed", ["A0"])
        k_kept = event("k_kept", CROSS)
        v_kept = event("v_kept", CROSS)
        kblk_made = event("kblk_made", CROSS, parts=NQ)
        xT_made = event("xT_made", CROSS)
        xT_kept = event("xT_kept", CROSS)
        q_made = event("q_made", CROSS)
        q_kept = event("q_kept", CROSS)
        xb_made = event("xb_made", CROSS)
        s_made = event("s_made", CROSS, parts=NQ)
        s_weighted = event("s_weighted", ["A1"], parts=NQ)
        s_masked = event("s_masked", ["A1"], parts=NQ)
        max_made = event("max_made", CROSS, parts=NQ)
        shifted = event("shifted", CROSS, parts=NQ)
        exp_made = event("exp_made", CROSS, parts=NQ)
        pT_made = event("pT_made", CROSS, parts=NQ)
        pT_kept = event("pT_kept", CROSS, parts=NQ)
        att_made = event("att_made", CROSS, parts=NQ)
        att_kept = event("att_kept", CROSS)
        back_made = event("back_made", CROSS)
        den_inverted = event("den_inverted", CROSS)
        o_made = event("o_made", CROSS)
        oT_made = event("oT_made", ["A1", "A2"])
        oT_kept = event("oT_kept", ["A1", "A2"])
        proj_made = event("proj_made", ["A1", "A2"])
        sum_made = event("sum_made", CROSS)
        stats_made = event("stats_made", CROSS)
        mv_made = event("mv_made", CROSS)
        var_made = event("var_made", CROSS)
        rstd_made = event("rstd_made", CROSS)
        z_made = event("z_made", CROSS)
        zg_made = event("zg_made", CROSS)
        y_made = event("y_made", CROSS)
        y_stored = event("y_stored", CROSS, transfers=1)

        FFS = ["F0", "F2", "F3"]
        fx_loaded = event("fx_loaded", FFS, transfers=1)
        fxT_made = {ph: event("fxT_made_" + ph, [ph]) for ph in FFS}
        fxT_kept = event("fxT_kept", FFS)
        fxb_made = {ph: event("fxb_made_" + ph, [ph]) for ph in FFS}
        PLAIN = ["F0", "F2"]
        hidden_made = event("hidden_made", PLAIN, parts=NF)
        hidden_kept = event("hidden_kept", PLAIN, parts=NF)
        gates_made = event("gates_made", ["F3"], parts=2 * NG)
        silu_kept = event("silu_kept", ["F3"], parts=NG)
        gated_kept = event("gated_kept", ["F3"], parts=NG)
        fo_made = event("fo_made", FFS)
        ft_made = event("ft_made", FFS)
        fstats_made = event("fstats_made", ["F2", "F3"], parts=GB)
        fmv_made = event("fmv_made", ["F2"], parts=GB)
        fcentred = event("fcentred", ["F2"], parts=GB)
        fvar_made = event("fvar_made", ["F2"])
        frstd_made = event("frstd_made", ["F2", "F3"])
        fz_made = {ph: event("fz_made_" + ph, [ph]) for ph in FFS[1:]}
        fzg_made = event("fzg_made", ["F2"])
        fy_made = event("fy_made", ["F2"])
        fy_stored = sem("fy_stored")
        fy_before = {ph: k * GROUPS for k, ph in enumerate(FFS)}

        x3_loaded = event("x3_loaded", ["A3"], transfers=1)
        xr_loaded = event("xr_loaded", ["A3"], transfers=1)
        vpre_loaded = event("vpre_loaded", ["A3"], transfers=4)
        sq_made = event("sq_made", ["A3"])
        rms_made = event("rms_made", ["A3"])
        xn_made = event("xn_made", ["A3"])
        xnT_made = event("xnT_made", ["A3"])
        xnT_kept = event("xnT_kept", ["A3"])
        q3_made = event("q3_made", ["A3"], parts=2)
        k3_made = event("k3_made", ["A3"], parts=2)
        v3_made = event("v3_made", ["A3"], parts=2)
        v3_kept = event("v3_kept", ["A3"], parts=2)
        q3_roped = event("q3_roped", ["A3"], parts=2)
        k3_roped = event("k3_roped", ["A3"], parts=2)
        q3_turned = event("q3_turned", ["A3"], parts=2)
        k3_turned = event("k3_turned", ["A3"], parts=2)
        qT3_made = event("qT3_made", ["A3"], parts=2)
        kT3_made = event("kT3_made", ["A3"], parts=2)
        qT3_kept = event("qT3_kept", ["A3"], parts=2)
        kT3_kept = event("kT3_kept", ["A3"], parts=2)
        kpre_made = event("kpre_made", ["A3"])
        s3_made = event("s3_made", ["A3"], parts=2)
        max3_parts = event("max3_parts", ["A3"], parts=2)
        max3_made = event("max3_made", ["A3"], parts=2)
        shifted3 = event("shifted3", ["A3"], parts=2)
        exp3_made = event("exp3_made", ["A3"], parts=2)
        den3_parts = event("den3_parts", ["A3"], parts=2)
        den3_sum = event("den3_sum", ["A3"], parts=2)
        den3_inv = event("den3_inv", ["A3"], parts=2)
        p3_rows = event("p3_rows", ["A3"], parts=2)
        p3_second = event("p3_second", ["A3"], parts=2)
        p3_made = event("p3_made", ["A3"], parts=2)
        pT3_made = event("pT3_made", ["A3"], parts=6)
        pT3_kept = event("pT3_kept", ["A3"], parts=6)
        att3_made = event("att3_made", ["A3"], parts=2)
        att3_kept = event("att3_kept", ["A3"], parts=2)
        proj3_made = event("proj3_made", ["A3"])
        y3_made = event("y3_made", ["A3"])
        y3_stored = event("y3_stored", ["A3"], transfers=1)

        SCALE = {"A0": DH ** -0.5, "A1": DH ** -0.5, "A2": D ** -0.5}
        scores_bank = bank[0:2]
        pT_bank = bank[2:4]
        att_bank = bank[4]
        kv_bank = bank[5]
        x_bank = bank[6]
        out_bank = bank[7]
        K_COL, V_COL, Q_COL = 0, 128, 128

        def quarter(ap, c):
            return ap[:, c * QC:(c + 1) * QC]

        def by_head(ap):
            return ap.rearrange("p (h k) -> p h k", k=C)

        def spread(col, n):
            return col.unsqueeze(2).to_broadcast([col.shape[0], col.shape[1], n])

        def phase_before(ph):
            return order[order.index(ph) - 1] if ph != order[0] else None

        def two_before(b, c):
            return (b if c >= 2 else b + -1), (c - 2) % NQ

        def cross_sync(sp, ph):
            prev = phase_before(ph)

            def load(b):
                if (b + -2).exists or prev in cross:
                    done = ctx_summed if ph == "A0" else kv_made
                    sp.wait_ge(done.sem(b + -2), done.count(ph, b + -2))
                sp.dma_start(ctx_s[b.par][:], at(a["ctxT"], b).rearrange("b d k -> (b d) k")).then_inc(ctx_loaded.sem(b), 16)
                if prev in FFS:
                    sp.wait_ge(fy_stored, (b.pair + (fy_before[prev] + 1)) * 16)
                elif prev:
                    sp.wait_ge(y_stored.sem(b), y_stored.count(prev, b))
                if (b + -2).exists or prev in cross:
                    sp.wait_ge(xT_made.sem(b + -2), xT_made.count(ph, b + -2))
                if (b + -2).exists or prev in cross:
                    sp.wait_ge(xb_made.sem(b + -2), xb_made.count(ph, b + -2))
                sp.dma_start(x_s[b.par][:], at(source[ph], b).rearrange("b t d -> (b t) d")).then_inc(X_loaded.sem(b), 16)
                if ph == "A1":
                    if (b + -2).exists:
                        sp.wait_ge(s_masked.sem(b + -2), s_masked.count(ph, b + -2, NQ - 1))
                    sp.dma_start(side_s[b.par][:], at(a["side"], b).rearrange("b t n -> (b t) n")).then_inc(weights_loaded.sem(b), 16)
                    sp.dma_start(mask_s[b.par][:], at(a["mask"], b).rearrange("b t n -> (b t) n")).then_inc(weights_loaded.sem(b), 16)
                if ph == "A2":
                    if (b + -2).exists:
                        sp.wait_ge(keybias_made.sem(b + -2), keybias_made.count(ph, b + -2))
                    sp.dma_start(keymask_s[b.par][:], at(a["keymask"], b)).then_inc(keymask_loaded.sem(b), 16)

            def step(b, has):
                if has(2):
                    load(b + 2)
                if ph == "A0":
                    load_rest(sp, b)
                if has(-2):
                    sp.wait_ge(y_made.sem(b + -2), y_made.count(ph, b + -2))
                    sp.dma_start(at(target[ph], b + -2).rearrange("b t d -> (b t) d"), y_s[(b + -2).par][:]).then_inc(y_stored.sem(b + -2), 16)
            return NB, step

        def cross_tensor(pe, ph):
            w = cross[ph]

            def project_context(b):
                if (b + -1).exists:
                    pe.wait_ge(k_kept.sem(b + -1), k_kept.count(ph, b + -1))
                    pe.wait_ge(v_kept.sem(b + -1), v_kept.count(ph, b + -1))
                pe.wait_ge(ctx_loaded.sem(b), ctx_loaded.count(ph, b))
                nc.tensor.matmul(kv_bank[:, K_COL:K_COL + C], w["wk"][:], ctx_s[b.par][:], start=True, stop=True)
                nc.tensor.matmul(kv_bank[0:C, V_COL:V_COL + D], ctx_s[b.par][:], w["wv"][:], start=True, stop=True).then_inc(kv_made.sem(b), 1)

            def transpose_x(b):
                pe.wait_ge(X_loaded.sem(b), X_loaded.count(ph, b))
                if (b + -1).exists:
                    pe.wait_ge(q_kept.sem(b + -1), q_kept.count(ph, b + -1))
                nc.tensor.transpose(x_bank[:, 0:T], x_s[b.par][:], ident[:]).then_inc(xT_made.sem(b), 1)

            def project_queries(b):
                pe.wait_ge(xT_kept.sem(b), xT_kept.count(ph, b))
                nc.tensor.matmul(x_bank[:, Q_COL:Q_COL + T], w["wq"][:], xT_s[b.par][:], start=True, stop=True).then_inc(q_made.sem(b), 1)

            def scores(b, c):
                pe.wait_ge(kblk_made.sem(b), kblk_made.count(ph, b, c))
                if c == 0:
                    pe.wait_ge(q_kept.sem(b), q_kept.count(ph, b))
                    if ph == "A2":
                        pe.wait_ge(keybias_made.sem(b), keybias_made.count(ph, b))
                done = s_weighted if ph == "A1" else shifted
                old, old_c = two_before(b, c)
                if old.exists:
                    pe.wait_ge(done.sem(old), done.count(ph, old, old_c))
                dst = scores_bank[c % 2][:, 0:QC]
                mm = nc.tensor.matmul(dst, qT_s[b.par][:], quarter(kblk_s[b.par], c), start=True, stop=(ph == "A1"))
                if ph == "A0":
                    mm = nc.tensor.matmul(dst, identb[:], causal[:], start=False, stop=True)
                if ph == "A2":
                    bias = keybias_s[b.par][0:1, :].unsqueeze(1).to_broadcast([1, QH, C])
                    mm = nc.tensor.matmul(dst, onesb[0:1, :], bias, start=False, stop=True)
                mm.then_inc(s_made.sem(b), 1)

            def transpose_p(b, c):
                pe.wait_ge(exp_made.sem(b), exp_made.count(ph, b, c))
                old, old_c = two_before(b, c)
                if old.exists:
                    pe.wait_ge(pT_kept.sem(old), pT_kept.count(ph, old, old_c))
                for h in range(QH):
                    mm = nc.tensor.transpose(pT_bank[c % 2][0:C, h * T:(h + 1) * T], p_s[c % 2][:, h * C:(h + 1) * C], ident[:])
                mm.then_inc(pT_made.sem(b), 1)

            def attend(b, c):
                pe.wait_ge(pT_kept.sem(b), pT_kept.count(ph, b, c))
                if c == 0:
                    pe.wait_ge(v_kept.sem(b), v_kept.count(ph, b))
                    if (b + -1).exists:
                        pe.wait_ge(att_kept.sem(b + -1), att_kept.count(ph, b + -1))
                for h in range(QH):
                    head = c * QH + h
                    mm = nc.tensor.matmul(att_bank[VP * h:VP * h + VP, c * T:(c + 1) * T],
                                          v_s[b.par][:, head * VP:(head + 1) * VP], pT_s[c % 2][:, h * T:(h + 1) * T],
                                          start=True, stop=True)
                mm.then_inc(att_made.sem(b), 1)

            def back(b):
                pe.wait_ge(att_kept.sem(b), att_kept.count(ph, b))
                done = o_made if ph == "A0" else sum_made
                if (b + -1).exists:
                    pe.wait_ge(done.sem(b + -1), done.count(ph, b + -1))
                for c in range(NQ):
                    mm = nc.tensor.transpose(out_bank[:, c * T:(c + 1) * T], att_s[b.par][:, c * T:(c + 1) * T], ident[:])
                mm.then_inc(back_made.sem(b), 1)

            def transpose_o(b):
                pe.wait_ge(o_made.sem(b), o_made.count(ph, b))
                nc.tensor.transpose(out_bank[:, 0:T], o_s[b.par][:], ident[:]).then_inc(oT_made.sem(b), 1)

            def project_out(b):
                pe.wait_ge(oT_kept.sem(b), oT_kept.count(ph, b))
                nc.tensor.matmul(out_bank[:, 0:D], oT_s[b.par][:], w["wo"][:], start=True, stop=True).then_inc(proj_made.sem(b), 1)

            def step(b, has):
                if has(0):
                    scores(b, 3)
                if has(1):
                    project_queries(b + 1)
                if has(0):
                    transpose_p(b, 0)
                if has(-1):
                    attend(b + -1, 2)
                    attend(b + -1, 3)
                if has(1):
                    scores(b + 1, 0)
                if has(0):
                    transpose_p(b, 1)
                if has(-1):
                    back(b + -1)
                if has(1):
                    scores(b + 1, 1)
                if has(0):
                    transpose_p(b, 2)
                    attend(b, 0)
                    attend(b, 1)
                if has(-1) and ph != "A0":
                    transpose_o(b + -1)
                if has(2):
                    project_context(b + 2)
                if has(1):
                    scores(b + 1, 2)
                if has(2):
                    transpose_x(b + 2)
                if has(0):
                    transpose_p(b, 3)
                if has(-1) and ph != "A0":
                    project_out(b + -1)
            drive(pe, NB, step, reach=2)

        def cross_scalar(act, ph):
            w = cross[ph]

            def exps(b, c):
                act.wait_ge(shifted.sem(b), shifted.count(ph, b, c))
                old, old_c = two_before(b, c)
                if old.exists:
                    act.wait_ge(pT_made.sem(old), pT_made.count(ph, old, old_c))
                nc.scalar.activation(p_s[c % 2][:], shifted_s[c][:], ACT.Exp, scale=SCALE[ph]).then_inc(exp_made.sem(b), 1)

            def keep_pT(b, c):
                act.wait_ge(pT_made.sem(b), pT_made.count(ph, b, c))
                old, old_c = two_before(b, c)
                if old.exists:
                    act.wait_ge(att_made.sem(old), att_made.count(ph, old, old_c))
                nc.scalar.activation(pT_s[c % 2][:], pT_bank[c % 2][0:C, :], ACT.Copy).then_inc(pT_kept.sem(b), 1)

            def keep_k(b):
                act.wait_ge(kv_made.sem(b), kv_made.count(ph, b))
                if (b + -2).exists:
                    act.wait_ge(kblk_made.sem(b + -2), kblk_made.count(ph, b + -2, NQ - 1))
                src = kv_bank[:, K_COL:K_COL + C]
                if ph == "A2":
                    nc.scalar.activation(kT_s[b.par][:], src, ACT.Copy).then_inc(k_kept.sem(b), 1)
                else:
                    nc.scalar.activation(kT_s[b.par][:], src, ACT.Identity, bias=w["bk"][:, 0:1]).then_inc(k_kept.sem(b), 1)

            def keep_xT(b):
                act.wait_ge(xT_made.sem(b), xT_made.count(ph, b))
                if (b + -2).exists:
                    act.wait_ge(q_made.sem(b + -2), q_made.count(ph, b + -2))
                nc.scalar.activation(xT_s[b.par][:], x_bank[:, 0:T], ACT.Copy).then_inc(xT_kept.sem(b), 1)

            def keep_q(b):
                act.wait_ge(q_made.sem(b), q_made.count(ph, b))
                if (b + -2).exists:
                    act.wait_ge(s_made.sem(b + -2), s_made.count(ph, b + -2, NQ - 1))
                if ph == "A2":
                    nc.scalar.activation(qT_s[b.par][:], x_bank[:, Q_COL:Q_COL + T], ACT.Copy).then_inc(q_kept.sem(b), 1)
                else:
                    nc.scalar.activation(qT_s[b.par][:], x_bank[:, Q_COL:Q_COL + T], ACT.Identity, bias=w["bq"][:, 0:1]).then_inc(q_kept.sem(b), 1)

            def keep_att(b):
                act.wait_ge(att_made.sem(b), att_made.count(ph, b, NQ - 1))
                if (b + -2).exists:
                    act.wait_ge(back_made.sem(b + -2), back_made.count(ph, b + -2))
                nc.scalar.activation(att_s[b.par][:], att_bank[:], ACT.Copy).then_inc(att_kept.sem(b), 1)

            def keep_oT(b):
                act.wait_ge(oT_made.sem(b), oT_made.count(ph, b))
                if (b + -2).exists:
                    act.wait_ge(proj_made.sem(b + -2), proj_made.count(ph, b + -2))
                if ph == "A1" and (b + -2).exists:
                    act.wait_ge(y_stored.sem(b + -2), y_stored.count(ph, b + -2))
                nc.scalar.activation(oT_s[b.par][:], out_bank[:, 0:T], ACT.Copy).then_inc(oT_kept.sem(b), 1)

            def step(b, has):
                if has(0):
                    exps(b, 1)
                if has(1):
                    keep_q(b + 1)
                if has(0):
                    keep_pT(b, 0)
                if has(-1):
                    keep_att(b + -1)
                if has(0):
                    exps(b, 2)
                    keep_pT(b, 1)
                    exps(b, 3)
                    keep_pT(b, 2)
                if has(-1) and ph != "A0":
                    keep_oT(b + -1)
                if has(2):
                    keep_k(b + 2)
                if has(1):
                    exps(b + 1, 0)
                if has(2):
                    keep_xT(b + 2)
                if has(0):
                    keep_pT(b, 3)
            drive(act, NB, step, reach=2)

        def cross_vector(dve, ph):
            w = cross[ph]

            def shift(b, c):
                dve.wait_ge(s_made.sem(b), s_made.count(ph, b, c))
                src = by_head(scores_bank[c % 2][:, 0:QC])
                nc.vector.tensor_reduce(max_s[c][:], src, AX.X, ALU.max).then_inc(max_made.sem(b), 1)
                dve.wait_ge(max_made.sem(b), max_made.count(ph, b, c))
                if (b + -1).exists:
                    dve.wait_ge(exp_made.sem(b + -1), exp_made.count(ph, b + -1, c))
                nc.vector.tensor_tensor(by_head(shifted_s[c][:]), src, spread(max_s[c][:], C), ALU.subtract)\
                    .then_inc(shifted.sem(b), 1)

            def weigh(b, c):
                dve.wait_ge(s_made.sem(b), s_made.count(ph, b, c))
                if c == 0:
                    dve.wait_ge(weights_loaded.sem(b), weights_loaded.count(ph, b))
                nc.vector.tensor_tensor(prod_s[c % 2][:], scores_bank[c % 2][:, 0:QC], quarter(side_s[b.par], c), ALU.mult)\
                    .then_inc(s_weighted.sem(b), 1)

            def mask(b, c):
                dve.wait_ge(s_weighted.sem(b), s_weighted.count(ph, b, c))
                if (b + -1).exists:
                    dve.wait_ge(shifted.sem(b + -1), shifted.count(ph, b + -1, c))
                nc.vector.scalar_tensor_tensor(scored_s[c][:], quarter(mask_s[b.par], c), MASKED, prod_s[c % 2][:],
                                               ALU.mult, ALU.add).then_inc(s_masked.sem(b), 1)

            def peak(b, c):
                dve.wait_ge(s_masked.sem(b), s_masked.count(ph, b, c))
                nc.vector.tensor_reduce(max_s[c][:], by_head(scored_s[c][:]), AX.X, ALU.max).then_inc(max_made.sem(b), 1)

            def keep_v(b):
                dve.wait_ge(kv_made.sem(b), kv_made.count(ph, b))
                dve.wait_ge(k_kept.sem(b), k_kept.count(ph, b))
                if (b + -2).exists:
                    dve.wait_ge(att_made.sem(b + -2), att_made.count(ph, b + -2, NQ - 1))
                dst = v_s[b.par][:].rearrange("p (h v) -> p h v", v=VP)[:, :, 0:DH]
                src = kv_bank[0:C, V_COL:V_COL + D].rearrange("p (h v) -> p h v", v=DH)
                if ph != "A1":
                    nc.vector.tensor_copy(dst, src).then_inc(v_kept.sem(b), 1)
                    if ph == "A0":
                        nc.vector.tensor_reduce(sumT[:, bass.ds(b.pair * 2 + b.par, 1)], ctx_s[b.par][:], AX.X, ALU.add).then_inc(ctx_summed.sem(b), 1)
                else:
                    nc.vector.tensor_tensor(dst, src, w["bv"][0:C, :].rearrange("p (h v) -> p h v", v=DH), ALU.add).then_inc(v_kept.sem(b), 1)

            def key_bias(b):
                dve.wait_ge(keymask_loaded.sem(b), keymask_loaded.count(ph, b))
                if (b + -2).exists:
                    dve.wait_ge(s_made.sem(b + -2), s_made.count(ph, b + -2, NQ - 1))
                nc.vector.tensor_scalar(keybias_s[b.par][:], keymask_s[b.par][:], 0, -1.0e20, ALU.is_equal, ALU.mult)\
                    .then_inc(keybias_made.sem(b), 1)

            raw = out_bank[:].rearrange("p (h v) -> p h v", v=VP)

            def invert(b):
                dve.wait_ge(back_made.sem(b), back_made.count(ph, b))
                nc.vector.reciprocal(rden_s[b.par][:].unsqueeze(2), raw[:, :, DH:DH + 1]).then_inc(den_inverted.sem(b), 1)

            def normalise(b):
                dve.wait_ge(den_inverted.sem(b), den_inverted.count(ph, b))
                if ph == "A0":
                    if (b + -2).exists:
                        dve.wait_ge(sum_made.sem(b + -2), sum_made.count(ph, b + -2))
                else:
                    if (b + -2).exists:
                        dve.wait_ge(oT_made.sem(b + -2), oT_made.count(ph, b + -2))
                nc.vector.tensor_tensor(o_s[b.par][:].rearrange("p (h v) -> p h v", v=DH), raw[:, :, 0:DH],
                                        spread(rden_s[b.par][:], DH), ALU.mult).then_inc(o_made.sem(b), 1)

            def sums(b):
                if b.first:
                    dve.wait_ge(xb_made.sem(b), xb_made.count(ph, b))
                if ph == "A0":
                    dve.wait_ge(o_made.sem(b), o_made.count(ph, b))
                    nc.vector.tensor_tensor(t_s[b.par][:], o_s[b.par][:], xb_s[b.par][:], ALU.add).then_inc(sum_made.sem(b), 1)
                else:
                    dve.wait_ge(proj_made.sem(b), proj_made.count(ph, b))
                    nc.vector.tensor_tensor(t_s[b.par][:], out_bank[:, 0:D], xb_s[b.par][:], ALU.add).then_inc(sum_made.sem(b), 1)

            def statistics(b):
                dve.wait_ge(sum_made.sem(b), sum_made.count(ph, b))
                nc.vector.bn_stats(stats_s[b.par][:], t_s[b.par][:]).then_inc(stats_made.sem(b), 1)
                dve.wait_ge(stats_made.sem(b), stats_made.count(ph, b))

            def aggregate(b):
                nc.vector.bn_aggr(mv_s[b.par][:], stats_s[b.par][:]).then_inc(mv_made.sem(b), 1)

            def centre(b):
                dve.wait_ge(rstd_made.sem(b), rstd_made.count(ph, b))
                if (b + -2).exists:
                    dve.wait_ge(zg_made.sem(b + -2), zg_made.count(ph, b + -2))
                nc.vector.tensor_scalar(z_s[b.par][:], t_s[b.par][:], mv_s[b.par][:, 0:1], rstd_s[b.par][:, 0:1],
                                        ALU.subtract, ALU.mult).then_inc(z_made.sem(b), 1)

            def scale(b):
                dve.wait_ge(z_made.sem(b), z_made.count(ph, b))
                nc.vector.tensor_tensor(zg_s[b.par][:], z_s[b.par][:], w["ln_g"][:], ALU.mult).then_inc(zg_made.sem(b), 1)

            def offset(b):
                dve.wait_ge(zg_made.sem(b), zg_made.count(ph, b))
                nc.vector.tensor_tensor(y_s[b.par][:], zg_s[b.par][:], w["ln_b"][:], ALU.add).then_inc(y_made.sem(b), 1)

            def step_weighted(b, has):
                if has(-2):
                    sums(b + -2)
                if has(0):
                    weigh(b, 3)
                if has(-2):
                    statistics(b + -2)
                if has(0):
                    peak(b, 2)
                    mask(b, 3)
                if has(-2):
                    aggregate(b + -2)
                if has(1):
                    weigh(b + 1, 0)
                if has(0):
                    peak(b, 3)
                if has(1):
                    mask(b + 1, 0)
                    keep_v(b + 1)
                if has(-1):
                    invert(b + -1)
                if has(1):
                    weigh(b + 1, 1)
                if has(-1):
                    normalise(b + -1)
                if has(1):
                    peak(b + 1, 0)
                    mask(b + 1, 1)
                if has(-2):
                    centre(b + -2)
                if has(1):
                    weigh(b + 1, 2)
                    peak(b + 1, 1)
                if has(-2):
                    scale(b + -2)
                if has(1):
                    mask(b + 1, 2)
                if has(-2):
                    offset(b + -2)

            def step(b, has):
                if has(-2):
                    sums(b + -2)
                    statistics(b + -2)
                if has(0):
                    shift(b, 3)
                if has(-2):
                    aggregate(b + -2)
                if has(1):
                    shift(b + 1, 0)
                    keep_v(b + 1)
                if has(-1):
                    invert(b + -1)
                    normalise(b + -1)
                if has(1):
                    shift(b + 1, 1)
                if has(-2):
                    centre(b + -2)
                if has(2) and ph == "A2":
                    key_bias(b + 2)
                if has(1):
                    shift(b + 1, 2)
            drive(dve, NB, step_weighted if ph == "A1" else step, reach=2)

        def cross_gpsimd(pool, ph):
            w = cross[ph]

            def block_keys(b, c):
                pool.wait_ge(k_kept.sem(b), k_kept.count(ph, b))
                if (b + -2).exists:
                    pool.wait_ge(s_made.sem(b + -2), s_made.count(ph, b + -2, c))
                nc.gpsimd.tensor_tensor(by_head(quarter(kblk_s[b.par], c)), kT_s[b.par][:].unsqueeze(1).to_broadcast([D, QH, C]),
                                        spread(headmask[:, c * QH:(c + 1) * QH], C), ALU.mult).then_inc(kblk_made.sem(b), 1)

            def shift(b, c):
                pool.wait_ge(max_made.sem(b), max_made.count(ph, b, c))
                if (b + -1).exists:
                    pool.wait_ge(exp_made.sem(b + -1), exp_made.count(ph, b + -1, c))
                nc.gpsimd.tensor_tensor(by_head(shifted_s[c][:]), by_head(scored_s[c][:]), spread(max_s[c][:], C), ALU.subtract)\
                    .then_inc(shifted.sem(b), 1)

            def residual(b):
                pool.wait_ge(X_loaded.sem(b), X_loaded.count(ph, b))
                if (b + -2).exists:
                    pool.wait_ge(sum_made.sem(b + -2), sum_made.count(ph, b + -2))
                nc.gpsimd.tensor_tensor(xb_s[b.par][:], x_s[b.par][:], w["bo"][:], ALU.add).then_inc(xb_made.sem(b), 1)

            def rstd(b):
                pool.wait_ge(mv_made.sem(b), mv_made.count(ph, b))
                nc.gpsimd.tensor_tensor(var_s[b.par][:], mv_s[b.par][:, 1:2], ln_eps[:, 0:1], ALU.add).then_inc(var_made.sem(b), 1)
                pool.wait_ge(var_made.sem(b), var_made.count(ph, b))
                if (b + -2).exists:
                    pool.wait_ge(z_made.sem(b + -2), z_made.count(ph, b + -2))
                nc.gpsimd.tensor_tensor(rstd_s[b.par][:], var_s[b.par][:], minus_half[:, 0:1], ALU.pow).then_inc(rstd_made.sem(b), 1)

            def affine(b):
                pool.wait_ge(z_made.sem(b), z_made.count(ph, b))
                nc.gpsimd.tensor_tensor(zg_s[b.par][:], z_s[b.par][:], w["ln_g"][:], ALU.mult).then_inc(zg_made.sem(b), 1)
                pool.wait_ge(zg_made.sem(b), zg_made.count(ph, b))
                if (b + -2).exists:
                    pool.wait_ge(y_stored.sem(b + -2), y_stored.count(ph, b + -2))
                nc.gpsimd.tensor_tensor(y_s[b.par][:], zg_s[b.par][:], w["ln_b"][:], ALU.add).then_inc(y_made.sem(b), 1)

            def step(b, has):
                weighted = ph == "A1"
                if has(0):
                    residual(b)
                if has(1):
                    block_keys(b + 1, 2)
                if has(0) and weighted:
                    shift(b, 3)
                if has(-2):
                    rstd(b + -2)
                if has(1) and weighted:
                    shift(b + 1, 0)
                if has(1):
                    block_keys(b + 1, 3)
                if has(-2) and not weighted:
                    affine(b + -2)
                if has(1) and weighted:
                    shift(b + 1, 1)
                if has(2):
                    block_keys(b + 2, 0)
                if has(2):
                    block_keys(b + 2, 1)
                if has(1) and weighted:
                    shift(b + 1, 2)
            drive(pool, NB, step, reach=2)

        FT = GB * T
        fx_bank = bank[0:2]
        fh_bank = bank[2:6]
        fo_bank = bank[6:8]

        def chunks(ph):
            return 2 * NG if ph == "F3" else NF

        def chunk_before(ph, g, j, n):
            j -= n
            return (g, j) if j >= 0 else (g + -1, j + chunks(ph))

        def chunk_bank(ph, g, j):
            return fh_bank[(chunks(ph) * g.par + j) % 4][:, 0:FT]

        def pair_of(ap, g):
            return at(ap, g, GB).rearrange("b t d -> t b d")

        def ff_sync(sp, ph):
            late = 2 if ph == "F2" else 1
            taken = fz_made[ph] if ph == "F3" else fxT_made[ph]

            def step(g, has):
                if has(2):
                    n = g + 2
                    if (n + -2).exists:
                        sp.wait_ge(taken.sem(n + -2), taken.count(ph, n + -2))
                    if (n + -2).exists:
                        sp.wait_ge(fxb_made[ph].sem(n + -2), fxb_made[ph].count(ph, n + -2))
                    stored = y3_stored if ph == "F3" else y_stored
                    even, odd = (Batch(n.pair * 2 + n.par, k) for k in range(2))
                    sp.wait_ge(stored.sem(even), stored.count(phase_before(ph), even))
                    sp.wait_ge(stored.sem(odd), stored.count(phase_before(ph), odd))
                    sp.dma_start(fx_s[n.par][:], pair_of(source[ph], n)).then_inc(fx_loaded.sem(n), 16)
                if has(-late):
                    p = g + -late
                    done = fy_made if ph == "F2" else ft_made
                    sp.wait_ge(done.sem(p), done.count(ph, p))
                    sp.dma_start(pair_of(target[ph], p), (fy_s if ph == "F2" else ft_s)[p.par][:]).then_inc(fy_stored, 16)
            return GROUPS, step

        def ff_tensor(pe, ph):
            w1, w2 = (w1g, w2g) if ph == "F3" else (ffw[ph]["w1"], ffw[ph]["w2"])
            made = gates_made if ph == "F3" else hidden_made

            def wait_kept(g, j):
                if ph == "F3":
                    done = (silu_kept, gated_kept)[j % 2]
                    pe.wait_ge(done.sem(g), done.count(ph, g, j // 2))
                else:
                    pe.wait_ge(hidden_kept.sem(g), hidden_kept.count(ph, g, j))

            def transpose_x(g):
                if (g + -2).exists:
                    pe.wait_ge(fxT_kept.sem(g + -2), fxT_kept.count(ph, g + -2))
                for k in range(GB):
                    if ph == "F3":
                        pe.wait_ge(fz_made[ph].sem(g), fz_made[ph].count(ph, g))
                        src = fz_s[g.par][:, k, :]
                    else:
                        pe.wait_ge(fx_loaded.sem(g), fx_loaded.count(ph, g))
                        src = fx_s[g.par][:, k, :]
                    mm = nc.tensor.transpose(fx_bank[g.par][:, k * T:(k + 1) * T], src, ident[:])
                mm.then_inc(fxT_made[ph].sem(g), 1)

            def hidden(g):
                pe.wait_ge(fxT_kept.sem(g), fxT_kept.count(ph, g))
                for j in range(chunks(ph)):
                    bg, bj = chunk_before(ph, g, j, 4)
                    if bg.exists:
                        wait_kept(bg, bj)
                    col = ((j // 2 + NG * (1 - j % 2)) if ph == "F3" else j) * 128
                    nc.tensor.matmul(chunk_bank(ph, g, j), w1[:, col:col + 128], fxT_s[g.par][:], start=True, stop=True)\
                        .then_inc(made.sem(g), 1)

            def down(g):
                last = range(1, 2 * NG, 2) if ph == "F3" else range(NF)
                wait_kept(g, last[-1])
                if (g + -2).exists:
                    pe.wait_ge(ft_made.sem(g + -2), ft_made.count(ph, g + -2))
                for k in range(GB):
                    for f in range(len(last)):
                        mm = nc.tensor.matmul(fo_bank[g.par][:, k * D:(k + 1) * D], fh_s[g.par][:, f, k * T:(k + 1) * T],
                                              w2[:, f, :], start=(f == 0), stop=(f == len(last) - 1))
                mm.then_inc(fo_made.sem(g), 1)

            def step(g, has):
                if has(0):
                    hidden(g)
                if has(1):
                    transpose_x(g + 1)
                if has(-1):
                    down(g + -1)
            drive(pe, GROUPS, step)

        def ff_scalar(act, ph):
            made = gates_made if ph == "F3" else hidden_made

            def keep_xT(g):
                act.wait_ge(fxT_made[ph].sem(g), fxT_made[ph].count(ph, g))
                if (g + -2).exists:
                    act.wait_ge(made.sem(g + -2), made.count(ph, g + -2, chunks(ph) - 1))
                nc.scalar.activation(fxT_s[g.par][:], fx_bank[g.par][:, 0:FT], ACT.Copy).then_inc(fxT_kept.sem(g), 1)

            def activate(g):
                for j in range(0, chunks(ph), 2 if ph == "F3" else 1):
                    act.wait_ge(made.sem(g), made.count(ph, g, j))
                    src = chunk_bank(ph, g, j)
                    if ph == "F3":
                        if (g + -2).exists:
                            act.wait_ge(gated_kept.sem(g + -2), gated_kept.count(ph, g + -2, j // 2))
                        nc.scalar.activation(fsilu_s[g.par][:, j // 2, :], src, ACT.Silu, bias=b1g[:, NG + j // 2:NG + j // 2 + 1])\
                            .then_inc(silu_kept.sem(g), 1)
                    else:
                        if (g + -2).exists:
                            act.wait_ge(fo_made.sem(g + -2), fo_made.count(ph, g + -2))
                        nc.scalar.activation(fh_s[g.par][:, j, :], src, ACT.Gelu if ph == "F0" else ACT.Relu,
                                             bias=ffw[ph]["b1"][:, j:j + 1]).then_inc(hidden_kept.sem(g), 1)

            def step(g, has):
                if has(0):
                    activate(g)
                if has(1):
                    keep_xT(g + 1)
            drive(act, GROUPS, step)

        def ff_vector(dve, ph):
            def squares(g):
                dve.wait_ge(fx_loaded.sem(g), fx_loaded.count(ph, g))
                if (g + -2).exists:
                    dve.wait_ge(frstd_made.sem(g + -2), frstd_made.count(ph, g + -2))
                for k in range(GB):
                    nc.vector.tensor_tensor_reduce(fsq_s[k][:], fx_s[g.par][:, k, :], fx_s[g.par][:, k, :], 1.0 / D, RMS_EPS, ALU.mult, ALU.add,
                                                   fvar_s[g.par][:, k:k + 1]).then_inc(fstats_made.sem(g), 1)

            def norm(g):
                dve.wait_ge(frstd_made.sem(g), frstd_made.count(ph, g))
                if (g + -2).exists:
                    dve.wait_ge(fxT_made[ph].sem(g + -2), fxT_made[ph].count(ph, g + -2))
                nc.vector.tensor_tensor(fz_s[g.par][:], fx_s[g.par][:], spread(frstd_s[g.par][:], D), ALU.mult).then_inc(fz_made[ph].sem(g), 1)

            def gate(g):
                for f in range(NG):
                    dve.wait_ge(gates_made.sem(g), gates_made.count(ph, g, 2 * f + 1))
                    dve.wait_ge(silu_kept.sem(g), silu_kept.count(ph, g, f))
                    if (g + -2).exists:
                        dve.wait_ge(fo_made.sem(g + -2), fo_made.count(ph, g + -2))
                    nc.vector.scalar_tensor_tensor(fh_s[g.par][:, f, :], chunk_bank(ph, g, 2 * f + 1), b1g[:, f:f + 1],
                                                   fsilu_s[g.par][:, f, :], ALU.add, ALU.mult).then_inc(gated_kept.sem(g), 1)

            def total(g):
                dve.wait_ge(fo_made.sem(g), fo_made.count(ph, g))
                dve.wait_ge(fxb_made[ph].sem(g), fxb_made[ph].count(ph, g))
                if ph == "F2":
                    if (g + -2).exists:
                        dve.wait_ge(fz_made[ph].sem(g + -2), fz_made[ph].count(ph, g + -2))
                else:
                    if not (ph == "F0" and g.first):
                        dve.wait_ge(fy_stored, (g.pair * 2 + (g.par + fy_before[ph])) * 16)
                nc.vector.tensor_tensor(ft_s[g.par][:], fo_bank[g.par][:, 0:GB * D].rearrange("p (b d) -> p b d", b=GB),
                                        fxb_s[g.par][:], ALU.add).then_inc(ft_made.sem(g), 1)

            def layernorm(g):
                dve.wait_ge(ft_made.sem(g), ft_made.count(ph, g))
                nc.vector.bn_stats(fstats_s[g.par][:, 0, :], ft_s[g.par][:, 0, :]).then_inc(fstats_made.sem(g), 1)
                dve.wait_ge(fstats_made.sem(g), fstats_made.count(ph, g, 0))
                nc.vector.bn_stats(fstats_s[g.par][:, 1, :], ft_s[g.par][:, 1, :]).then_inc(fstats_made.sem(g), 1)
                nc.vector.bn_aggr(fmv_s[g.par][:, 0, :], fstats_s[g.par][:, 0, :]).then_inc(fmv_made.sem(g), 1)
                dve.wait_ge(fmv_made.sem(g), fmv_made.count(ph, g, 0))
                dve.wait_ge(fstats_made.sem(g), fstats_made.count(ph, g, 1))
                if (g + -2).exists:
                    dve.wait_ge(fz_made[ph].sem(g + -2), fz_made[ph].count(ph, g + -2))
                centred(g, 0)
                nc.vector.bn_aggr(fmv_s[g.par][:, 1, :], fstats_s[g.par][:, 1, :]).then_inc(fmv_made.sem(g), 1)
                dve.wait_ge(fmv_made.sem(g), fmv_made.count(ph, g, 1))
                centred(g, 1)
                dve.wait_ge(frstd_made.sem(g), frstd_made.count(ph, g))
                dve.wait_ge(fcentred.sem(g), fcentred.count(ph, g, 1))
                if (g + -2).exists:
                    dve.wait_ge(fzg_made.sem(g + -2), fzg_made.count(ph, g + -2))
                nc.vector.tensor_tensor(fz_s[g.par][:], fc_s[g.par][:], spread(frstd_s[g.par][:], D), ALU.mult).then_inc(fz_made[ph].sem(g), 1)

            def centred(g, k):
                nc.vector.tensor_scalar(fc_s[g.par][:, k, :], ft_s[g.par][:, k, :], fmv_s[g.par][:, k, 0:1], None, ALU.subtract)\
                    .then_inc(fcentred.sem(g), 1)

            def step(g, has):
                if has(1) and ph == "F3":
                    norm(g + 1)
                if has(0) and ph == "F3":
                    gate(g)
                if has(2) and ph == "F3":
                    squares(g + 2)
                if has(-1):
                    total(g + -1)
                    if ph == "F2":
                        layernorm(g + -1)
            drive(dve, GROUPS, step, reach=2)

        def ff_gpsimd(pool, ph):
            b2 = b2g if ph == "F3" else ffw[ph]["b2"]

            def every(row):
                return row[:].unsqueeze(1).to_broadcast([T, GB, D])

            def residual(g):
                pool.wait_ge(fx_loaded.sem(g), fx_loaded.count(ph, g))
                if (g + -2).exists:
                    pool.wait_ge(ft_made.sem(g + -2), ft_made.count(ph, g + -2))
                nc.gpsimd.tensor_tensor(fxb_s[g.par][:], fx_s[g.par][:], every(b2), ALU.add).then_inc(fxb_made[ph].sem(g), 1)

            def rstd(g):
                done = fstats_made if ph == "F3" else fmv_made
                pool.wait_ge(done.sem(g), done.count(ph, g, GB - 1))
                if ph == "F2":
                    nc.gpsimd.tensor_tensor(fvar_s[g.par][:], fmv_s[g.par][:, :, 1], ln_eps[:], ALU.add).then_inc(fvar_made.sem(g), 1)
                    pool.wait_ge(fvar_made.sem(g), fvar_made.count(ph, g))
                if (g + -2).exists:
                    pool.wait_ge(fz_made[ph].sem(g + -2), fz_made[ph].count(ph, g + -2))
                nc.gpsimd.tensor_tensor(frstd_s[g.par][:], fvar_s[g.par][:], minus_half[:], ALU.pow).then_inc(frstd_made.sem(g), 1)

            def affine(g):
                pool.wait_ge(fz_made[ph].sem(g), fz_made[ph].count(ph, g))
                nc.gpsimd.tensor_tensor(fn_s[g.par][:], fz_s[g.par][:], every(ffw[ph]["g"]), ALU.mult).then_inc(fzg_made.sem(g), 1)
                pool.wait_ge(fzg_made.sem(g), fzg_made.count(ph, g))
                pool.wait_ge(fy_stored, (g.pair * 2 + (g.par + fy_before[ph])) * 16)
                nc.gpsimd.tensor_tensor(fy_s[g.par][:], fn_s[g.par][:], every(ffw[ph]["b"]), ALU.add).then_inc(fy_made.sem(g), 1)

            def step(g, has):
                if has(2) and ph == "F3":
                    rstd(g + 2)
                if has(1):
                    residual(g + 1)
                if has(-1) and ph == "F2":
                    rstd(g + -1)
                    affine(g + -1)
            drive(pool, GROUPS, step, reach=2)

        ph3 = "A3"
        q_bank, k_bank, v_bank = bank[0:3]
        turn3 = bank[3:5]
        s_even, s_odd = bank[5], bank[6]
        att3 = bank[7]
        LOC = HC * SEG
        HALF = 2 * HC * KH
        SPLIT = HALF * 3 // 4

        IN = {"q": q_bank, "k": k_bank, "v": v_bank}
        def self_sync(sp):
            def tokens(ap, b):
                return at(ap, b).rearrange("b t d -> (b t) d")

            def step(b, has):
                if has(2):
                    n = b + 2
                    if b.exists:
                        sp.wait_ge(xn_made.sem(b), xn_made.count(ph3, b))
                    sp.wait_ge(fy_stored, (n.pair + (fy_before["F2"] + 1)) * 16)
                    sp.dma_start(x_s[n.par][:], tokens(source[ph3], n)).then_inc(x3_loaded.sem(n), 16)
                if has(1):
                    n = b + 1
                    if (n + -2).exists:
                        sp.wait_ge(att3_made.sem(n + -2), att3_made.count(ph3, n + -2, 1))
                    mem = at(vmem_dram, n).rearrange("b (g k d) -> (b k) g d", k=4, d=KH)
                    for k in range(4):
                        sp.dma_start(vpre_s[n.par][PRE * k:PRE * k + NM, :, k, :],
                                     mem[k:k + 1].to_broadcast([NM, H // 4, KH])).then_inc(vpre_loaded.sem(n), 16)
                    if (n + -2).exists:
                        sp.wait_ge(y3_made.sem(n + -2), y3_made.count(ph3, n + -2))
                    sp.dma_start(xb_s[n.par][:], tokens(source[ph3], n)).then_inc(xr_loaded.sem(n), 16)
                if has(-1):
                    sp.wait_ge(y3_made.sem(b + -1), y3_made.count(ph3, b + -1))
                    sp.dma_start(tokens(target[ph3], b + -1), y_s[(b + -1).par][:]).then_inc(y3_stored.sem(b + -1), 16)
            return NB, step

        def self_tensor(pe):
            made = {"q": q3_made, "k": k3_made, "v": v3_made}

            def project(b, what, h):
                col = "qkv".index(what) * HD3 + h * HALF
                before, other = (b if h else b + -1), 1 - h
                if what == "q" and h == 0:
                    pe.wait_ge(xnT_kept.sem(b), xnT_kept.count(ph3, b))
                elif what == "q":
                    pe.wait_ge(q3_roped.sem(b), q3_roped.count(ph3, b, 0))
                elif what == "k":
                    if before.exists:
                        pe.wait_ge(k3_roped.sem(before), k3_roped.count(ph3, before, other))
                    if h == 0 and (b + -2).exists:
                        pe.wait_ge(y3_made.sem(b + -2), y3_made.count(ph3, b + -2))
                elif what == "v" and (b + -1).exists:
                    pe.wait_ge(pT3_kept.sem(b + -1), pT3_kept.count(ph3, b + -1, 3 * h + 2))
                elif what == "v" and before.exists:
                    pe.wait_ge(v3_kept.sem(before), v3_kept.count(ph3, before, other))
                if what != "v":
                    nc.tensor.matmul(IN[what][:], xnT_s[b.par][:], wqkv[:, col:col + HALF], start=True, stop=True)\
                        .then_inc(made[what].sem(b), 1)
                else:
                    nc.tensor.matmul(IN[what][:, 0:SPLIT], xnT_s[b.par][:], wqkv[:, col:col + SPLIT], start=True, stop=True)

            def project_more_values(b, h):
                col = 2 * HD3 + h * HALF
                nc.tensor.matmul(IN["v"][:, SPLIT:HALF], xnT_s[b.par][:], wqkv[:, col + SPLIT:col + HALF], start=True, stop=True)\
                    .then_inc(v3_made.sem(b), 1)

            def turn(b, what, h):
                src_done, dst_done = (q3_turned, qT3_made) if what == "q" else (k3_turned, kT3_made)
                pe.wait_ge(src_done.sem(b), src_done.count(ph3, b, h))
                if (b + -1).exists:
                    pe.wait_ge(pT3_kept.sem(b + -1), pT3_kept.count(ph3, b + -1, 3 * h + "qk".index(what)))
                for c in range(HC):
                    mm = nc.tensor.transpose(turn3["qk".index(what)][:, c * T:(c + 1) * T], turned[what][h][:, c * 128:(c + 1) * 128], ident[:])
                mm.then_inc(dst_done.sem(b), 1)

            def scores(b, h):
                old = b if h else b + -1
                if old.exists:
                    pe.wait_ge(shifted3.sem(old), shifted3.count(ph3, old, 1 - h))
                qT, kT = turnedT["q"][h], turnedT["k"][h]
                for s_bank in (s_even, s_odd):
                    nc.tensor.matmul(s_bank[:, 0:LOC], identb[:], tri[:], start=True, stop=False, skip_group_check=True)
                pe.wait_ge(qT3_kept.sem(b), qT3_kept.count(ph3, b, h))
                if h == 0:
                    pe.wait_ge(kpre_made.sem(b), kpre_made.count(ph3, b))
                for c in range(HC):
                    if c == HC - 1:
                        pe.wait_ge(kT3_kept.sem(b), kT3_kept.count(ph3, b, h))
                    nc.tensor.matmul(s_even[:, LOC + c * 2 * PRE:LOC + (c + 1) * 2 * PRE], qT[:, c * T:(c + 1) * T],
                                     kpre_s[b.par][:, h * HC + c, :], start=False, stop=False, skip_group_check=True)
                for c in range(HC):
                    for r, s_bank in enumerate((s_even, s_odd)):
                        rows = slice(r * KH, (r + 1) * KH)
                        for g in range(T // SEG):
                            own = slice(c * T + g * SEG, c * T + (g + 1) * SEG)
                            mm = nc.tensor.matmul(s_bank[g * SEG:(g + 1) * SEG, c * SEG:(c + 1) * SEG], qT[rows, own], kT[rows, own],
                                                  start=False, stop=(c == HC - 1), skip_group_check=True)
                mm.then_inc(s3_made.sem(b), 1)

            def transpose_p(b, h, more):
                pe.wait_ge(p3_made.sem(b), p3_made.count(ph3, b, h))
                pe.wait_ge(p3_second.sem(b), p3_second.count(ph3, b, h))
                after, follows = (b + 1 if h else b), more or h == 0
                for r in range(2):
                    if follows:
                        kept = (qT3_kept, kT3_kept)[r]
                        pe.wait_ge(kept.sem(after), kept.count(ph3, after, 1 - h))
                    for c in range(HC):
                        n = r * HC + c
                        mm = nc.tensor.transpose(turn3[r][:, c * T:(c + 1) * T], dense_s[h][:, n * T:(n + 1) * T], ident[:])
                    mm.then_inc(pT3_made.sem(b), 1)
                if follows:
                    pe.wait_ge(v3_kept.sem(after), v3_kept.count(ph3, after, 1 - h))
                for n in range(2):
                    mm = nc.tensor.transpose(v_bank[:, n * T:(n + 1) * T], pp_s[h][:, n * 128:(n + 1) * 128], ident[:])
                mm.then_inc(pT3_made.sem(b), 1)

            def attend(b, h):
                pe.wait_ge(pT3_kept.sem(b), pT3_kept.count(ph3, b, 3 * h + 2))
                pe.wait_ge(v3_kept.sem(b), v3_kept.count(ph3, b, h))
                if h == 0:
                    pe.wait_ge(vpre_loaded.sem(b), vpre_loaded.count(ph3, b))
                before = b if h else b + -1
                if before.exists:
                    pe.wait_ge(att3_kept.sem(before), att3_kept.count(ph3, before, 1 - h))
                for c in range(HC):
                    k = 2 * c % 4
                    nc.tensor.matmul(att3[:, c * T:(c + 1) * T], vpre_s[b.par][:, 2 * h + c // 2, k:k + 2, :],
                                     ppT_s[h][:, (c // 2) * T:(c // 2 + 1) * T], start=(c == 0), stop=False, skip_group_check=True)
                for c in range(HC):
                    for r in range(2):
                        n = r * HC + c
                        mm = nc.tensor.matmul(att3[r * KH:(r + 1) * KH, c * T:(c + 1) * T], v3_s[h][:, (2 * c + r) * KH:(2 * c + r + 1) * KH],
                                              denseT_s[h][:, n * T:(n + 1) * T], start=False, stop=True, skip_group_check=True)
                mm.then_inc(att3_made.sem(b), 1)

            def project_out(b, more):
                pe.wait_ge(att3_kept.sem(b), att3_kept.count(ph3, b, 1))
                if more:
                    pe.wait_ge(k3_roped.sem(b + 1), k3_roped.count(ph3, b + 1, 1))
                for c in range(H // 2):
                    mm = nc.tensor.matmul(k_bank[:, 0:D], att3_s[c // HC][:, (c % HC) * T:(c % HC + 1) * T], wout3[:, c, :],
                                          start=(c == 0), stop=(c == H // 2 - 1))
                mm.then_inc(proj3_made.sem(b), 1)

            def transpose_x(b):
                pe.wait_ge(xn_made.sem(b), xn_made.count(ph3, b))
                if (b + -1).exists:
                    pe.wait_ge(q3_roped.sem(b + -1), q3_roped.count(ph3, b + -1, 1))
                nc.tensor.transpose(q_bank[:, 0:T], xn_s[b.par][:], ident[:]).then_inc(xnT_made.sem(b), 1)

            def step(b, has):
                if has(0):
                    scores(b, 0)
                if has(-1):
                    transpose_p(b + -1, 1, has(0))
                if has(0):
                    project(b, "q", 1)
                    project(b, "k", 1)
                if has(-1):
                    attend(b + -1, 1)
                if has(0):
                    project(b, "v", 1)
                    turn(b, "q", 1)
                    project_more_values(b, 1)
                if has(-1):
                    project_out(b + -1, has(0))
                if has(0):
                    turn(b, "k", 1)
                if has(1):
                    transpose_x(b + 1)
                if has(0):
                    scores(b, 1)
                    transpose_p(b, 0, has(1))
                if has(1):
                    project(b + 1, "q", 0)
                    project(b + 1, "k", 0)
                if has(0):
                    attend(b, 0)
                if has(1):
                    project(b + 1, "v", 0)
                    turn(b + 1, "q", 0)
                    project_more_values(b + 1, 0)
                    turn(b + 1, "k", 0)
            drive(pe, NB, step)

        def self_scalar(act):
            def keep_v(b, h):
                act.wait_ge(v3_made.sem(b), v3_made.count(ph3, b, h))
                if (b + -1).exists:
                    act.wait_ge(att3_made.sem(b + -1), att3_made.count(ph3, b + -1, h))
                nc.scalar.activation(v3_s[h][:], IN["v"][:], ACT.Copy).then_inc(v3_kept.sem(b), 1)

            def keep_turned(b, h):
                for what, done, kept in (("q", qT3_made, qT3_kept), ("k", kT3_made, kT3_kept)):
                    act.wait_ge(done.sem(b), done.count(ph3, b, h))
                    if (b + -1).exists:
                        act.wait_ge(s3_made.sem(b + -1), s3_made.count(ph3, b + -1, h))
                    nc.scalar.activation(turnedT[what][h][:], turn3["qk".index(what)][:], ACT.Copy).then_inc(kept.sem(b), 1)

            def keep_p(b, h):
                if (b + -1).exists:
                    act.wait_ge(att3_made.sem(b + -1), att3_made.count(ph3, b + -1, h))
                for r in range(2):
                    act.wait_ge(pT3_made.sem(b), pT3_made.count(ph3, b, 3 * h + r))
                    nc.scalar.activation(denseT_s[h][:, r * HC * T:(r + 1) * HC * T], turn3[r][:], ACT.Copy)\
                        .then_inc(pT3_kept.sem(b), 1)
                act.wait_ge(pT3_made.sem(b), pT3_made.count(ph3, b, 3 * h + 2))
                nc.scalar.activation(ppT_s[h][:], v_bank[:, 0:2 * T], ACT.Copy).then_inc(pT3_kept.sem(b), 1)

            def keep_att(b, h):
                act.wait_ge(att3_made.sem(b), att3_made.count(ph3, b, h))
                if (b + -1).exists:
                    act.wait_ge(proj3_made.sem(b + -1), proj3_made.count(ph3, b + -1))
                nc.scalar.activation(att3_s[h][:], att3[:], ACT.Copy).then_inc(att3_kept.sem(b), 1)

            def exps(b, h):
                act.wait_ge(shifted3.sem(b), shifted3.count(ph3, b, h))
                nc.scalar.activation(l_s[h][:], l_s[h][:], ACT.Exp, scale=KH ** -0.5)
                nc.scalar.activation(lp_s[h][:], lp_s[h][:], ACT.Exp, scale=KH ** -0.5).then_inc(exp3_made.sem(b), 1)

            def keep_xT(b):
                act.wait_ge(xnT_made.sem(b), xnT_made.count(ph3, b))
                if (b + -2).exists:
                    act.wait_ge(v3_made.sem(b + -2), v3_made.count(ph3, b + -2, 1))
                nc.scalar.activation(xnT_s[b.par][:], q_bank[:, 0:T], ACT.Copy).then_inc(xnT_kept.sem(b), 1)

            def step(b, has):
                if has(-1):
                    keep_p(b + -1, 1)
                if has(0):
                    exps(b, 0)
                if has(-1):
                    keep_att(b + -1, 1)
                if has(0):
                    keep_turned(b, 1)
                    keep_v(b, 1)
                if has(1):
                    keep_xT(b + 1)
                if has(0):
                    keep_p(b, 0)
                    exps(b, 1)
                    keep_att(b, 0)
                if has(1):
                    keep_turned(b + 1, 0)
                    keep_v(b + 1, 0)
            drive(act, NB, step)

        def by_half(ap, w):
            return ap.rearrange("p (n k) -> p n k", k=w)

        def swap_order(ap):
            return ap.rearrange("p (c r) -> p r c", r=2)

        def spread_segment(engine, h, g):
            rows = slice(g * SEG, (g + 1) * SEG)
            return engine.tensor_tensor(by_half(dense_s[h][rows, :], T)[:, :, g * SEG:(g + 1) * SEG], by_half(l_s[h][rows, :], SEG),
                                        spread(r_all[h][rows, :], SEG), ALU.mult)

        def spread_prefix(engine, h, r):
            pre_r = lambda ap: ap.rearrange("p (c r k) -> p r c k", r=2, k=PRE)[:, r]
            return engine.tensor_tensor(pre_r(pp_s[h][:]), pre_r(lp_s[h][:]), spread(r_all[h][:, r * HC:(r + 1) * HC], PRE), ALU.mult)

        def self_vector(dve):
            def rope(b, what, h):
                done, roped = (q3_made, q3_roped) if what == "q" else (k3_made, k3_roped)
                dve.wait_ge(done.sem(b), done.count(ph3, b, h))
                if what == "q" and (b + -1).exists:
                    dve.wait_ge(q3_turned.sem(b + -1), q3_turned.count(ph3, b + -1, h))
                src = IN[what][:]
                nc.vector.tensor_tensor(by_half(ropeC[what][h][:], KH), by_half(src, KH),
                                        cos[:].unsqueeze(1).to_broadcast([T, 2 * HC, KH]), ALU.mult)
                pairs = src.rearrange("p (n f two) -> p n f two", two=2, f=KH // 2)
                swapped = ropeS[what][h][:].rearrange("p (n f two) -> p n f two", two=2, f=KH // 2)
                factor = sin[:].rearrange("p (f two) -> p f two", two=2)
                for k in range(2):
                    ins = nc.vector.tensor_tensor(swapped[:, :, :, k], pairs[:, :, :, 1 - k],
                                                  factor[:, :, k].unsqueeze(1).to_broadcast([T, 2 * HC, KH // 2]), ALU.mult)
                ins.then_inc(roped.sem(b), 1)
                if what == "k":
                    dve.wait_ge(k3_roped.sem(b), k3_roped.count(ph3, b, h))
                    if (b + -1).exists:
                        dve.wait_ge(kT3_made.sem(b + -1), kT3_made.count(ph3, b + -1, h))
                    nc.vector.tensor_tensor(turned[what][h][:], ropeC[what][h][:], ropeS[what][h][:], ALU.add).then_inc(k3_turned.sem(b), 1)

            def shift(b, h):
                dve.wait_ge(s3_made.sem(b), s3_made.count(ph3, b, h))
                for r, s_bank in enumerate((s_even, s_odd)):
                    nc.vector.tensor_reduce(m_loc[h][:, r * HC:(r + 1) * HC], by_half(s_bank[:, 0:LOC], SEG), AX.X, ALU.max)
                prefix = s_even[:, LOC:LOC + 2 * HC * PRE]
                nc.vector.tensor_reduce(m_pre[h][:], by_half(prefix, PRE), AX.X, ALU.max).then_inc(max3_parts.sem(b), 1)
                dve.wait_ge(max3_parts.sem(b), max3_parts.count(ph3, b, h))
                nc.vector.tensor_tensor(m_all[h][:].rearrange("p (r c) -> p r c", r=2), m_loc[h][:].rearrange("p (r c) -> p r c", r=2),
                                        swap_order(m_pre[h][:]), ALU.max).then_inc(max3_made.sem(b), 1)
                dve.wait_ge(max3_made.sem(b), max3_made.count(ph3, b, h))
                if (b + -1).exists:
                    dve.wait_ge(p3_made.sem(b + -1), p3_made.count(ph3, b + -1, h))
                for r, s_bank in enumerate((s_even, s_odd)):
                    nc.vector.tensor_tensor(by_half(l_s[h][:, r * LOC:(r + 1) * LOC], SEG), by_half(s_bank[:, 0:LOC], SEG),
                                            spread(m_all[h][:, r * HC:(r + 1) * HC], SEG), ALU.subtract)
                for r in range(2):
                    pre_r = lambda ap: ap.rearrange("p (c r k) -> p r c k", r=2, k=PRE)[:, r]
                    ins = nc.vector.tensor_tensor(pre_r(lp_s[h][:]), pre_r(prefix), spread(m_all[h][:, r * HC:(r + 1) * HC], PRE), ALU.subtract)
                ins.then_inc(shifted3.sem(b), 1)

            def denominators(b, h):
                dve.wait_ge(exp3_made.sem(b), exp3_made.count(ph3, b, h))
                nc.vector.tensor_reduce(d_loc[h][:], by_half(l_s[h][:], SEG), AX.X, ALU.add)
                nc.vector.tensor_reduce(d_pre[h][:], by_half(lp_s[h][:], PRE), AX.X, ALU.add).then_inc(den3_parts.sem(b), 1)
                dve.wait_ge(den3_parts.sem(b), den3_parts.count(ph3, b, h))
                nc.vector.tensor_tensor(d_all[h][:].rearrange("p (r c) -> p r c", r=2), d_loc[h][:].rearrange("p (r c) -> p r c", r=2),
                                        swap_order(d_pre[h][:]), ALU.add).then_inc(den3_sum.sem(b), 1)
                dve.wait_ge(den3_sum.sem(b), den3_sum.count(ph3, b, h))
                if (b + -1).exists:
                    dve.wait_ge(p3_made.sem(b + -1), p3_made.count(ph3, b + -1, h))
                nc.vector.reciprocal(r_all[h][:], d_all[h][:]).then_inc(den3_inv.sem(b), 1)
                dve.wait_ge(den3_inv.sem(b), den3_inv.count(ph3, b, h))
                if (b + -1).exists:
                    dve.wait_ge(pT3_made.sem(b + -1), pT3_made.count(ph3, b + -1, 3 * h + 2))
                spread_segment(nc.vector, h, 1)
                spread_prefix(nc.vector, h, 1).then_inc(p3_second.sem(b), 1)

            def squares(b):
                dve.wait_ge(x3_loaded.sem(b), x3_loaded.count(ph3, b))
                if (b + -2).exists:
                    dve.wait_ge(rms_made.sem(b + -2), rms_made.count(ph3, b + -2))
                nc.vector.tensor_tensor_reduce(sq_s[b.par][:], x_s[b.par][:], x_s[b.par][:], 1.0 / D, RMS_EPS, ALU.mult, ALU.add,
                                               var_s[b.par][:]).then_inc(sq_made.sem(b), 1)

            def norm(b):
                dve.wait_ge(rms_made.sem(b), rms_made.count(ph3, b))
                if (b + -2).exists:
                    dve.wait_ge(xnT_made.sem(b + -2), xnT_made.count(ph3, b + -2))
                nc.vector.tensor_scalar(xn_s[b.par][:], x_s[b.par][:], rstd_s[b.par][:, 0:1], None, ALU.mult).then_inc(xn_made.sem(b), 1)

            def residual(b):
                dve.wait_ge(proj3_made.sem(b), proj3_made.count(ph3, b))
                dve.wait_ge(xr_loaded.sem(b), xr_loaded.count(ph3, b))
                if (b + -2).exists:
                    dve.wait_ge(y3_stored.sem(b + -2), y3_stored.count(ph3, b + -2))
                nc.vector.tensor_tensor(y_s[b.par][:], k_bank[:, 0:D], xb_s[b.par][:], ALU.add).then_inc(y3_made.sem(b), 1)

            def step(b, has):
                if has(1):
                    squares(b + 1)
                if has(0):
                    shift(b, 0)
                    rope(b, "q", 1)
                if has(1):
                    norm(b + 1)
                if has(0):
                    rope(b, "k", 1)
                    denominators(b, 0)
                if has(-1):
                    residual(b + -1)
                if has(0):
                    shift(b, 1)
                if has(1):
                    rope(b + 1, "q", 0)
                    rope(b + 1, "k", 0)
                if has(0):
                    denominators(b, 1)
            drive(dve, NB, step)

        def self_gpsimd(pool):
            def add_queries(b, h):
                pool.wait_ge(q3_roped.sem(b), q3_roped.count(ph3, b, h))
                if (b + -1).exists:
                    pool.wait_ge(qT3_made.sem(b + -1), qT3_made.count(ph3, b + -1, h))
                nc.gpsimd.tensor_tensor(turned["q"][h][:], ropeC["q"][h][:], ropeS["q"][h][:], ALU.add).then_inc(q3_turned.sem(b), 1)

            def normalise(b, h):
                pool.wait_ge(den3_inv.sem(b), den3_inv.count(ph3, b, h))
                if (b + -1).exists:
                    pool.wait_ge(pT3_made.sem(b + -1), pT3_made.count(ph3, b + -1, 3 * h + 2))
                spread_segment(nc.gpsimd, h, 0).then_inc(p3_rows.sem(b), 1)
                pool.wait_ge(p3_rows.sem(b), p3_rows.count(ph3, b, h))
                spread_prefix(nc.gpsimd, h, 0).then_inc(p3_made.sem(b), 1)

            def rms(b):
                pool.wait_ge(sq_made.sem(b), sq_made.count(ph3, b))
                if (b + -2).exists:
                    pool.wait_ge(xn_made.sem(b + -2), xn_made.count(ph3, b + -2))
                nc.gpsimd.tensor_tensor(rstd_s[b.par][:], var_s[b.par][:], minus_half[:, 0:1], ALU.pow).then_inc(rms_made.sem(b), 1)

            def prefix_keys(b):
                if (b + -2).exists:
                    pool.wait_ge(s3_made.sem(b + -2), s3_made.count(ph3, b + -2, 1))
                mem = kmemT[:, :, bass.ds(b.pair * 2 + b.par, 1)].unsqueeze(2).to_broadcast([128, H // 2, 2, NM])
                own = halfmask[:].unsqueeze(1).unsqueeze(3).to_broadcast([128, H // 2, 2, NM])
                nc.gpsimd.tensor_tensor(kpre_s[b.par][:].rearrange("p c (r k) -> p c r k", r=2)[:, :, :, 0:NM], mem, own, ALU.mult)\
                    .then_inc(kpre_made.sem(b), 1)

            def step(b, has):
                if has(1):
                    rms(b + 1)
                if has(0):
                    add_queries(b, 1)
                    normalise(b, 0)
                if has(1):
                    prefix_keys(b + 1)
                    add_queries(b + 1, 0)
                if has(0):
                    normalise(b, 1)
            drive(pool, NB, step)

        mean, square, normed, scaled = slots("pooled", [NB, D], n=4)
        pool_var = slots("pool_var", [NB, 1], n=3)
        poolT = sb("poolT", [D, NB])
        memT = sb("memT", [D, NB])
        vmem_sb = sb("vmem", [NB, HD3])
        pool_step = sem("pool_step")
        sums_turned = sem("sums_turned")
        turn_bank = bank[3]

        rest = [(dst[:], src) for dst, src in consts]
        for slot in range(2):
            for r in range(2):
                rest.append((kpre_s[slot][r * KH:(r + 1) * KH, :, r * PRE + NM:(r + 1) * PRE], a["persistT"][r]))
            for k in range(4):
                rest.append((vpre_s[slot][PRE * k + NM:PRE * (k + 1), :, k, :], a["persist"][k]))
        PORTIONS = 5
        portion = -(-len(rest) // PORTIONS)

        def load_rest(sp, b):
            n = 2 * b.pair + b.par + 1 if isinstance(b.pair, int) else PORTIONS
            if n == 0:
                sp.wait_ge(presets, 6)
            if 0 <= n < PORTIONS:
                for dst, src in rest[n * portion:(n + 1) * portion]:
                    sp.dma_start(dst, src).then_inc(loaded, 16)

        def turn_sums(pe):
            pe.wait_ge(ctx_summed.sems[0], NB)
            nc.tensor.transpose(turn_bank[0:NB, 0:D], sumT[:], ident[:]).then_inc(sums_turned, 1)

        def pool_vector(dve):
            dve.wait_ge(sums_turned, 1)
            nc.vector.tensor_scalar(mean[:], turn_bank[0:NB, 0:D], 1.0 / C, None, ALU.mult).then_inc(pool_step, 1)
            dve.wait_ge(pool_step, 1)
            nc.vector.tensor_tensor_reduce(square[:], mean[:], mean[:], 1.0, 0.0, ALU.mult, ALU.add, pool_var[0][:]).then_inc(pool_step, 1)
            dve.wait_ge(pool_step, 4)
            nc.vector.tensor_scalar(normed[:], mean[:], pool_var[2][:, 0:1], None, ALU.mult).then_inc(pool_step, 1)
            dve.wait_ge(pool_step, 5)
            nc.vector.tensor_tensor(scaled[:], normed[:], pool_norm[0:NB, :], ALU.mult).then_inc(pool_step, 1)

        def pool_gpsimd(pool):
            pool.wait_ge(pool_step, 2)
            nc.gpsimd.tensor_scalar(pool_var[1][:], pool_var[0][:], 1.0 / D, RMS_EPS, ALU.mult, ALU.add).then_inc(pool_step, 1)
            pool.wait_ge(pool_step, 3)
            nc.gpsimd.tensor_tensor(pool_var[2][:], pool_var[1][:], minus_half[0:NB, 0:1], ALU.pow).then_inc(pool_step, 1)

        def memory_tensor(pe):
            pe.wait_ge(pool_step, 6)
            nc.tensor.transpose(bank[0][:, 0:NB], scaled[:], ident[0:NB, 0:NB]).then_inc(mem_poolT, 1)
            pe.wait_ge(mem_poolT_kept, 1)
            nc.tensor.matmul(bank[1][:, 0:NB], wmem[:], poolT[:], start=True, stop=True).then_inc(mem_tok, 1)
            pe.wait_ge(mem_tok_kept, 1)
            for c in range(H // 2):
                nc.tensor.matmul(bank[2][:, c * NB:(c + 1) * NB], wqkv[:, HD3 + c * 128:HD3 + (c + 1) * 128], memT[:], start=True, stop=True)
            for n in range(2):
                mm = nc.tensor.matmul(bank[3 + n][0:NB, :], memT[:], wqkv[:, 2 * HD3 + n * 512:2 * HD3 + (n + 1) * 512], start=True, stop=True)
            mm.then_inc(mem_kv, 1)
            pe.wait_ge(mem_kv_kept, 3)

        def memory_scalar(act):
            act.wait_ge(mem_poolT, 1)
            nc.scalar.activation(poolT[:], bank[0][:, 0:NB], ACT.Copy).then_inc(mem_poolT_kept, 1)
            act.wait_ge(mem_tok, 1)
            nc.scalar.activation(memT[:], bank[1][:, 0:NB], ACT.Copy).then_inc(mem_tok_kept, 1)
            act.wait_ge(mem_kv, 1)
            nc.scalar.activation(kmemT[:].rearrange("p c b -> p (c b)"), bank[2][:, 0:H // 2 * NB], ACT.Copy).then_inc(mem_kv_kept, 1)
            for n in range(2):
                nc.scalar.activation(vmem_sb[:, n * 512:(n + 1) * 512], bank[3 + n][0:NB, :], ACT.Copy).then_inc(mem_kv_kept, 1)

        def memory_sync(sp):
            sp.wait_ge(mem_kv_kept, 3)
            sp.dma_start(vmem_dram, vmem_sb[:]).then_inc(mem_stored, 16)
            sp.wait_ge(mem_stored, 16)

        def scale_weights(dve):
            dve.wait_ge(mem_kv, 1)
            nc.vector.tensor_scalar(wqkv[:], wqkv[:], attn_norm[:, 0:1], None, ALU.mult).then_inc(weights_scaled, 1)
            nc.vector.tensor_scalar(w1g[:], w1g[:], ff_norm[:, 0:1], None, ALU.mult).then_inc(weights_scaled, 1)

        def phases(eng, by_cross, by_ff, by_self, before):
            for ph in order:
                if ph in before:
                    before[ph](eng)
                if ph in cross:
                    by_cross(eng, ph)
                elif ph[0] == "F":
                    by_ff(eng, ph)
                else:
                    by_self(eng)

        def rest_loaded(eng):
            eng.wait_ge(loaded, 16 * N_LOADS)

        block = ctx.enter_context(nc.Block())

        N_ZERO = 5
        N_FIRST = 16 * len(first_loads)

        @block.sync
        def _(sp):
            for dst, src in first_loads:
                sp.dma_start(dst[:], src).then_inc(first_loaded, 16)

            def steps(ph):
                return cross_sync(sp, ph) if ph in cross else ff_sync(sp, ph) if ph in FFS else self_sync(sp)

            for k, ph in enumerate(order):
                n, step = steps(ph)
                ahead = None
                if k + 1 < len(order):
                    n_next, step_next = steps(order[k + 1])
                    ahead = lambda t: step_next(Batch(t // 2, t % 2), lambda d: 0 <= t + d < n_next)
                drive(sp, n, step, reach=2, ahead=ahead, begun=k > 0)
                if ph == "A2":
                    memory_sync(sp)
            for slot in range(2):
                sp.wait_ge(y_stored.sems[slot], y_stored.total_count)
                sp.wait_ge(y3_stored.sems[slot], y3_stored.total_count)
            sp.wait_ge(fy_stored, 16 * GROUPS * len(FFS))

        @block.tensor
        def _(pe):
            pe.wait_ge(first_loaded, N_FIRST)
            pe.wait_ge(zeroed, N_ZERO)
            pe.wait_ge(masks_made, 2)

            def before_self(pe):
                pe.wait_ge(presets, 6)
                pe.wait_ge(masks_made, 3)
                pe.wait_ge(weights_scaled, 2)

            phases(pe, cross_tensor, ff_tensor, self_tensor,
                   {"F0": rest_loaded, "A1": turn_sums, "A2": memory_tensor, "A3": before_self})

        @block.scalar
        def _(act):
            act.wait_ge(first_loaded, N_FIRST)
            phases(act, cross_scalar, ff_scalar, self_scalar, {"F0": rest_loaded, "A2": memory_scalar})

        @block.vector
        def _(dve):
            for s in range(2):
                nc.vector.memset(v_s[s][:], 0.0).then_inc(setup, 1)
            dve.wait_ge(setup, 2)
            for s in range(2):
                nc.vector.memset(v_s[s][:].rearrange("p (h v) -> p h v", v=VP)[:, :, DH:DH + 1], 1.0).then_inc(zeroed, 1)
            nc.vector.memset(onesb[:], 1.0).then_inc(zeroed, 1)
            nc.vector.memset(minus_half[:], -0.5).then_inc(zeroed, 1)
            nc.vector.memset(ln_eps[:], LN_EPS).then_inc(zeroed, 1)
            for s in range(2):
                nc.vector.memset(dense_s[s][:], 0.0).then_inc(presets, 1)
                nc.vector.memset(kpre_s[s][:], 0.0).then_inc(presets, 1)
                nc.vector.memset(vpre_s[s][:], 0.0).then_inc(presets, 1)
            dve.wait_ge(first_loaded, N_FIRST)
            dve.wait_ge(zeroed, N_ZERO)
            nc.vector.tensor_copy(identb[:], ident[:]).then_inc(masks_made, 1)
            nc.vector.tensor_copy(causal[:], causal32).then_inc(masks_made, 1)

            def before_ff(dve):
                dve.wait_ge(loaded, 16 * N_LOADS)
                dve.wait_ge(presets, 6)
                nc.vector.tensor_copy(tri[:], tri32).then_inc(masks_made, 1)

            phases(dve, cross_vector, ff_vector, self_vector, {"F0": before_ff, "A1": pool_vector, "F2": scale_weights})

        @block.gpsimd
        def _(pool):
            pool.wait_ge(first_loaded, N_FIRST)
            pool.wait_ge(zeroed, N_ZERO)
            phases(pool, cross_gpsimd, ff_gpsimd, self_gpsimd, {"F0": rest_loaded, "A1": pool_gpsimd})


def lay_out(i):
    f = lambda x: np.ascontiguousarray(np.asarray(x))
    NB = i["x"].shape[0]
    a = {"x": f(i["x"])}
    a["ctxT"] = f(np.transpose(i["ctx_1024"], (0, 2, 1)))
    a["side"] = f(np.transpose(i["fside_Bx16xSxS2_0"], (0, 2, 1, 3))).reshape(NB, T, H * C)
    a["mask"] = f(np.transpose(i["mask_Bx16xSxS2_bk0"], (0, 2, 1, 3))).reshape(NB, T, H * C)
    a["keymask"] = f(i["mask_Bx1x1xS2_if1"]).reshape(NB, C)
    for p in ("L0_xattn_", "L1_xattn_"):
        for k in "qkv":
            a[f"{p}w{k}"] = f(np.transpose(i[f"{p}W{k}"]))
            a[f"{p}b{k}"] = f(i[f"{p}b{k}"])
    p = "L0_xattn_"
    a[p + "ln_g"], a[p + "ln_b"] = f(i[p + "ln_g"]), f(i[p + "ln_b"])
    a[p + "ffw1"] = f(np.transpose(i[p + "W1"]))
    a[p + "ffb1"] = f(np.transpose(np.reshape(i[p + "b1"], (NF, 128))))
    a[p + "ffw2"] = f(np.transpose(np.reshape(np.transpose(i[p + "W2"]), (NF, 128, D)), (1, 0, 2)))
    a[p + "ffb2"] = f(i[p + "b2"])
    p = "L1_xattn_"
    a[p + "wo"], a[p + "bo"] = f(np.transpose(i[p + "Wo"])), f(i[p + "bo"])
    a[p + "ln_g"], a[p + "ln_b"] = f(i[p + "gamma"]), f(i[p + "beta"])
    p = "L2_xattn_"
    for k in "qkv":
        w = np.zeros((D, D), np.float32)
        for h in range(H):
            w[h * DH:(h + 1) * DH, h * DH:(h + 1) * DH] = i[f"{p}w{k}"]
        a[f"{p}w{k}"] = w
    a[p + "wo"], a[p + "bo"] = f(i[p + "w_out"]), f(i[p + "b_out"])
    a[p + "ln_g"], a[p + "ln_b"] = f(i[p + "g1"]), f(i[p + "beta1"])
    a[p + "ffw1"] = f(i[p + "w_ff1"])
    a[p + "ffb1"] = f(np.transpose(np.reshape(i[p + "b_ff1"], (NF, 128))))
    a[p + "ffw2"] = f(np.transpose(np.reshape(i[p + "w_ff2"], (NF, 128, D)), (1, 0, 2)))
    a[p + "ffb2"] = f(i[p + "b_ff2"])
    a[p + "g2"], a[p + "beta2"] = f(i[p + "g2"]), f(i[p + "beta2"])
    p = "L3_xattn_"
    for k in ("attn_norm_w", "to_qkv_w", "to_out_w", "mem_pool_norm_w", "to_mem_tokens_w", "ff_norm_w", "ff_b2"):
        a[p + k] = f(i[p + k])
    w1, b1, w2 = (np.asarray(i[p + k]) for k in ("ff_w1", "ff_b1", "ff_w2"))
    pw1 = np.zeros((D, 2, NG * 128), np.float32)
    pw1[:, 0, :DG], pw1[:, 1, :DG] = w1[:, :DG], w1[:, DG:]
    a[p + "ffw1"] = pw1.reshape(D, 2 * NG * 128)
    pb1 = np.zeros((2, NG * 128), np.float32)
    pb1[0, :DG], pb1[1, :DG] = b1[:DG], b1[DG:]
    a[p + "ffb1"] = f(np.transpose(pb1.reshape(2 * NG, 128)))
    pw2 = np.zeros((NG * 128, D), np.float32)
    pw2[:DG] = w2
    a[p + "ffw2"] = f(np.transpose(pw2.reshape(NG, 128, D), (1, 0, 2)))
    pm = np.asarray(i[p + "persist_mem"])
    a["persistT"] = f(np.transpose(pm.reshape(H // 2, 2, NPM, KH), (1, 3, 0, 2)))
    a["persist"] = f(np.transpose(pm.reshape(H // 4, 4, NPM, KH), (1, 2, 0, 3)))

    a["c_ident"] = np.eye(128, dtype=np.float32)
    later = np.arange(C)[None, :] > np.arange(T)[:, None]
    a["c_causal"] = np.tile(np.where(later, -1.0e9, 0.0), (1, QH)).astype(np.float32)
    later = np.arange(SEG)[None, :] > (np.arange(T) % SEG)[:, None]
    a["c_tri"] = np.tile(np.where(later, -1.0e30, 0.0), (1, HC)).astype(np.float32)
    a["c_headmask"] = (np.arange(D)[:, None] // DH == np.arange(H)[None, :]).astype(np.float32)
    a["c_halfmask"] = (np.arange(128)[:, None] // KH == np.arange(2)[None, :]).astype(np.float32)
    inv = (np.float32(1.0) / np.float32(10000.0) ** (np.arange(0, KH, 2, dtype=np.float32) / np.float32(KH))).astype(np.float32)
    angle = np.repeat(np.arange(T, dtype=np.float32)[:, None] * inv[None, :], 2, axis=-1)
    a["c_cos"] = np.cos(angle).astype(np.float32)
    a["c_sin"] = (np.sin(angle) * np.tile([-1.0, 1.0], KH // 2)[None, :]).astype(np.float32)
    return a


def kernel(**inputs):
    import concourse.bacc as bacc
    from concourse.bass_utils import run_bass_kernel_spmd

    nc = bacc.Bacc("TRN2", target_bir_lowering=False, num_devices=1)
    arrays = {"in_" + k: v for k, v in lay_out(inputs).items()}
    aps = {k[3:]: nc.dram_tensor(k, v.shape, mybir.dt.from_np(v.dtype), kind="ExternalInput").ap() for k, v in arrays.items()}
    out = nc.dram_tensor("out", inputs["x"].shape, F32, kind="ExternalOutput").ap()
    build_layers(nc, aps, out)
    return run_bass_kernel_spmd(nc, [arrays], core_ids=[0]).results[0]["out"]
```
